# Optimizing a Trainium2 kernel written in Bass

```python
import numpy as np
import jax
import jax.numpy as jnp

def _softmax(x, axis=-1):
    return jax.nn.softmax(x, axis=axis)

def _gelu(x):
    return jax.nn.gelu(x, approximate=True)

def _silu(x):
    return jax.nn.silu(x)

def _sigmoid(x):
    return jax.nn.sigmoid(x)

def _layernorm(x, axis=-1, eps=1e-05):
    m = jnp.mean(x, axis=axis, keepdims=True)
    v = jnp.var(x, axis=axis, keepdims=True)
    return (x - m) / jnp.sqrt(v + eps)

def _scatter_add(tgt, idx, src, axis=0):
    return tgt.at[idx].add(src)

def _segment_sum(src, seg, n):
    return jax.ops.segment_sum(src, seg, n)
kernel_name = 'mk_metaformer_d2_conv_nchw768_r4_e2e7c2'

def setup_inputs(seed: int=0):
    np.random.seed(seed)
    _w = jnp.asarray

    def _rec_inputs():
        import jax
        import jax.numpy as jnp
        _gk = jax.random.key(seed)
        x = -4.65e-05 + 0.9999 * jax.random.normal(jax.random.fold_in(_gk, 1), (16, 192, 16, 16), jnp.float32)
        return x
    x = _rec_inputs()

    def _L0_conv_setup():
        import jax, jax.numpy as jnp
        import numpy as np
        B, C_IN, C_OUT, H, W = (16, 192, 192, 16, 16)
        G = 16
        key = jax.random.key(seed)
        k1, k2 = jax.random.split(key)
        x = jax.random.normal(k1, (B, C_IN, H, W), dtype=jnp.float32)
        bound = float(np.sqrt(6.0 / (C_IN + C_OUT)))
        Wg = jax.random.uniform(k2, (G, C_OUT, C_IN), dtype=jnp.float32, minval=-bound, maxval=bound)
        bg = jnp.zeros((G, C_OUT), dtype=jnp.float32)
        return {'x': x, 'Wg': Wg, 'bg': bg}
    _L0_conv_all = _L0_conv_setup()
    _L0_conv_in = {k: v for k, v in _L0_conv_all.items() if k in ('Wg', 'bg')}
    del _L0_conv_all

    def _L0_ffn_setup():
        import jax, jax.numpy as jnp
        import numpy as np
        NUM_EXPERTS = 8
        TOP_K = 2
        INIT_STD = 0.02
        key = jax.random.key(seed)
        k = jax.random.split(key, 6)
        B, S, D, F, E = (2, 512, 192, 768, NUM_EXPERTS)
        hidden_states = jax.random.normal(k[0], (B, S, D), dtype=jnp.float32)
        gate_w = jax.random.normal(k[1], (D, E), dtype=jnp.float32) * (1.0 / np.sqrt(D))
        w_up = jax.random.normal(k[2], (E, D, F), dtype=jnp.float32) * INIT_STD
        b_up = jnp.zeros((E, F), dtype=jnp.float32)
        w_down = jax.random.normal(k[3], (E, F, D), dtype=jnp.float32) * INIT_STD
        b_down = jnp.zeros((E, D), dtype=jnp.float32)
        return {'hidden_states': hidden_states, 'gate_w': gate_w, 'w_up': w_up, 'b_up': b_up, 'w_down': w_down, 'b_down': b_down}
    _L0_ffn_all = _L0_ffn_setup()
    _L0_ffn_in = {k: v for k, v in _L0_ffn_all.items() if k in ('gate_w', 'w_up', 'b_up', 'w_down', 'b_down')}
    del _L0_ffn_all

    def _L1_conv_setup():
        import jax, jax.numpy as jnp
        import numpy as np
        CHUNK = 16

        def l2norm(x, eps=1e-06):
            return x * jax.lax.rsqrt(jnp.sum(x * x, axis=-1, keepdims=True) + eps)

        def delta_rule_chunked(q, k, v, beta):
            B, H, L, D = q.shape
            n = L // CHUNK

            def to_chunks(t):
                return jnp.moveaxis(t.reshape(B, H, n, CHUNK, *(t.shape[4:] if t.ndim > 4 else ())) if False else t.reshape(B, H, n, CHUNK, -1) if t.ndim == 4 else t.reshape(B, H, n, CHUNK), 2, 0)
            qc = jnp.moveaxis(q.reshape(B, H, n, CHUNK, D), 2, 0)
            kc = jnp.moveaxis(k.reshape(B, H, n, CHUNK, D), 2, 0)
            vc = jnp.moveaxis(v.reshape(B, H, n, CHUNK, D), 2, 0)
            bc = jnp.moveaxis(beta.reshape(B, H, n, CHUNK), 2, 0)
            strict = jnp.tril(jnp.ones((CHUNK, CHUNK), bool), -1)
            incl = jnp.tril(jnp.ones((CHUNK, CHUNK), bool))
            eye = jnp.eye(CHUNK, dtype=q.dtype)

            def step(S, inp):
                qi, ki, vi, bi = inp
                kk = jnp.einsum('bhid,bhjd->bhij', ki, ki)
                T = eye + jnp.where(strict, bi[..., :, None] * kk, 0.0)
                rhs = bi[..., None] * (vi - jnp.einsum('bhcd,bhde->bhce', ki, S))
                U = jax.scipy.linalg.solve_triangular(T, rhs, lower=True)
                qk = jnp.einsum('bhid,bhjd->bhij', qi, ki)
                O = jnp.einsum('bhcd,bhde->bhce', qi, S) + jnp.einsum('bhij,bhje->bhie', jnp.where(incl, qk, 0.0), U)
                S_new = S + jnp.einsum('bhcd,bhce->bhde', ki, U)
                return (S_new, O)
            S0 = jnp.zeros((B, H, D, D), q.dtype)
            _, O = jax.lax.scan(step, S0, (qc, kc, vc, bc))
            return jnp.moveaxis(O, 0, 2).reshape(B, H, L, D)
        key = jax.random.key(seed)
        ks = jax.random.split(key, 7)
        B, C, Hh, Ww = (8, 192, 16, 16)
        n_heads = 12
        s = 1.0 / np.sqrt(C)
        x = jax.random.normal(ks[0], (B, C, Hh, Ww), jnp.float32)
        Wq = jax.random.normal(ks[1], (C, C), jnp.float32) * s
        Wk = jax.random.normal(ks[2], (C, C), jnp.float32) * s
        Wv = jax.random.normal(ks[3], (C, C), jnp.float32) * s
        Wb = jax.random.normal(ks[4], (C, n_heads), jnp.float32) * s
        Wo = jax.random.normal(ks[5], (C, C), jnp.float32) * s
        return {'x': x, 'Wq': Wq, 'Wk': Wk, 'Wv': Wv, 'Wb': Wb, 'Wo': Wo}
    _L1_conv_all = _L1_conv_setup()
    _L1_conv_in = {k: v for k, v in _L1_conv_all.items() if k in ('Wq', 'Wk', 'Wv', 'Wb', 'Wo')}
    del _L1_conv_all

    def _L1_ffn_setup():
        import jax, jax.numpy as jnp
        import numpy as np
        TOP_K = 2
        key = jax.random.key(seed)
        ks = jax.random.split(key, 5)
        B, T, C, H, E = (4, 256, 192, 768, 8)
        x = jax.random.normal(ks[0], (B, T, C), dtype=jnp.float32)
        Wg = jax.random.normal(ks[1], (C, E), dtype=jnp.float32) * 0.02
        W1 = jax.random.normal(ks[2], (E, C, H), dtype=jnp.float32) * (1.0 / np.sqrt(C))
        b1 = jnp.zeros((E, H), dtype=jnp.float32)
        W2 = jax.random.normal(ks[3], (E, H, C), dtype=jnp.float32) * (1.0 / np.sqrt(H))
        b2 = jnp.zeros((E, C), dtype=jnp.float32)
        return {'x': x, 'Wg': Wg, 'W1': W1, 'b1': b1, 'W2': W2, 'b2': b2}
    _L1_ffn_all = _L1_ffn_setup()
    _L1_ffn_in = {k: v for k, v in _L1_ffn_all.items() if k in ('Wg', 'W1', 'b1', 'W2', 'b2')}
    del _L1_ffn_all
    return {'x': x, 'L0_conv_Wg': _L0_conv_in['Wg'], 'L0_conv_bg': _L0_conv_in['bg'], 'L0_ffn_gate_w': _L0_ffn_in['gate_w'], 'L0_ffn_w_up': _L0_ffn_in['w_up'], 'L0_ffn_b_up': _L0_ffn_in['b_up'], 'L0_ffn_w_down': _L0_ffn_in['w_down'], 'L0_ffn_b_down': _L0_ffn_in['b_down'], 'L1_conv_Wq': _L1_conv_in['Wq'], 'L1_conv_Wk': _L1_conv_in['Wk'], 'L1_conv_Wv': _L1_conv_in['Wv'], 'L1_conv_Wb': _L1_conv_in['Wb'], 'L1_conv_Wo': _L1_conv_in['Wo'], 'L1_ffn_Wg': _L1_ffn_in['Wg'], 'L1_ffn_W1': _L1_ffn_in['W1'], 'L1_ffn_b1': _L1_ffn_in['b1'], 'L1_ffn_W2': _L1_ffn_in['W2'], 'L1_ffn_b2': _L1_ffn_in['b2']}

def reference(x, L0_conv_Wg, L0_conv_bg, L0_ffn_gate_w, L0_ffn_w_up, L0_ffn_b_up, L0_ffn_w_down, L0_ffn_b_down, L1_conv_Wq, L1_conv_Wk, L1_conv_Wv, L1_conv_Wb, L1_conv_Wo, L1_ffn_Wg, L1_ffn_W1, L1_ffn_b1, L1_ffn_W2, L1_ffn_b2):
    import jax
    import jax.numpy as jnp

    def _L0_conv_ref(x, Wg, bg):
        import jax, jax.numpy as jnp
        import numpy as np
        B, C_IN, C_OUT, H, W = (16, 192, 192, 16, 16)
        G = 16
        Bb, C, Hh, Ww = x.shape
        H4, W4 = (Hh // 4, Ww // 4)
        xg = x.reshape(Bb, C, H4, 4, W4, 4).transpose(0, 2, 4, 3, 5, 1)
        xg = xg.reshape(Bb, H4, W4, 16, C)
        y = jnp.einsum('bhwgc,goc->bhwgo', xg, Wg) + bg
        O = y.shape[-1]
        y = y.reshape(Bb, H4, W4, 4, 4, O).transpose(0, 5, 1, 3, 2, 4)
        out = y.reshape(Bb, O, Hh, Ww)
        return out

    def _L0_ffn_ref(hidden_states, gate_w, w_up, b_up, w_down, b_down):
        import jax, jax.numpy as jnp
        import numpy as np
        NUM_EXPERTS = 8
        TOP_K = 2
        INIT_STD = 0.02
        B, S, D = hidden_states.shape
        E = gate_w.shape[1]
        x = hidden_states.reshape(-1, D)
        T = x.shape[0]
        logits = x @ gate_w
        probs = jax.nn.softmax(logits, axis=-1)
        top_w, top_i = jax.lax.top_k(probs, TOP_K)
        combine = jnp.zeros((T, E), dtype=x.dtype).at[jnp.arange(T)[:, None], top_i].add(top_w)
        h = jax.nn.gelu(jnp.einsum('td,edf->tef', x, w_up) + b_up, approximate=False)
        y = jnp.einsum('tef,efd->ted', h, w_down) + b_down[None, :, :]
        out = jnp.einsum('ted,te->td', y, combine)
        return out.reshape(B, S, D)

    def _L1_conv_ref(x, Wq, Wk, Wv, Wb, Wo):
        import jax, jax.numpy as jnp
        import numpy as np
        CHUNK = 16

        def l2norm(x, eps=1e-06):
            return x * jax.lax.rsqrt(jnp.sum(x * x, axis=-1, keepdims=True) + eps)

        def delta_rule_chunked(q, k, v, beta):
            B, H, L, D = q.shape
            n = L // CHUNK

            def to_chunks(t):
                return jnp.moveaxis(t.reshape(B, H, n, CHUNK, *(t.shape[4:] if t.ndim > 4 else ())) if False else t.reshape(B, H, n, CHUNK, -1) if t.ndim == 4 else t.reshape(B, H, n, CHUNK), 2, 0)
            qc = jnp.moveaxis(q.reshape(B, H, n, CHUNK, D), 2, 0)
            kc = jnp.moveaxis(k.reshape(B, H, n, CHUNK, D), 2, 0)
            vc = jnp.moveaxis(v.reshape(B, H, n, CHUNK, D), 2, 0)
            bc = jnp.moveaxis(beta.reshape(B, H, n, CHUNK), 2, 0)
            strict = jnp.tril(jnp.ones((CHUNK, CHUNK), bool), -1)
            incl = jnp.tril(jnp.ones((CHUNK, CHUNK), bool))
            eye = jnp.eye(CHUNK, dtype=q.dtype)

            def step(S, inp):
                qi, ki, vi, bi = inp
                kk = jnp.einsum('bhid,bhjd->bhij', ki, ki)
                T = eye + jnp.where(strict, bi[..., :, None] * kk, 0.0)
                rhs = bi[..., None] * (vi - jnp.einsum('bhcd,bhde->bhce', ki, S))
                U = jax.scipy.linalg.solve_triangular(T, rhs, lower=True)
                qk = jnp.einsum('bhid,bhjd->bhij', qi, ki)
                O = jnp.einsum('bhcd,bhde->bhce', qi, S) + jnp.einsum('bhij,bhje->bhie', jnp.where(incl, qk, 0.0), U)
                S_new = S + jnp.einsum('bhcd,bhce->bhde', ki, U)
                return (S_new, O)
            S0 = jnp.zeros((B, H, D, D), q.dtype)
            _, O = jax.lax.scan(step, S0, (qc, kc, vc, bc))
            return jnp.moveaxis(O, 0, 2).reshape(B, H, L, D)
        B, C, Hh, Ww = x.shape
        L = Hh * Ww
        n_heads = Wb.shape[1]
        D = C // n_heads
        t = x.reshape(B, C, L).transpose(0, 2, 1)

        def heads(z):
            return z.reshape(B, L, n_heads, D).transpose(0, 2, 1, 3)
        q = l2norm(heads(jax.nn.silu(t @ Wq)))
        k = l2norm(heads(jax.nn.silu(t @ Wk)))
        v = heads(jax.nn.silu(t @ Wv))
        beta = jax.nn.sigmoid(t @ Wb).transpose(0, 2, 1)
        o = delta_rule_chunked(q, k, v, beta)
        o = o.transpose(0, 2, 1, 3).reshape(B, L, C)
        y = o @ Wo
        out = t + y
        return out.transpose(0, 2, 1).reshape(B, C, Hh, Ww)

    def _L1_ffn_ref(x, Wg, W1, b1, W2, b2):
        import jax, jax.numpy as jnp
        import numpy as np
        TOP_K = 2
        E = Wg.shape[-1]
        logits = jnp.einsum('btc,ce->bte', x, Wg)
        probs = jax.nn.softmax(logits, axis=-1)
        top_vals, top_idx = jax.lax.top_k(probs, TOP_K)
        gates = (jax.nn.one_hot(top_idx, E, dtype=probs.dtype) * top_vals[..., None]).sum(-2)
        h = jax.nn.relu(jnp.einsum('btc,ech->bteh', x, W1) + b1)
        y = jnp.einsum('bteh,ehc->btec', h, W2) + b2
        out = jnp.einsum('bte,btec->btc', gates, y)
        return out

    def _gn(v, G=32, eps=1e-05):
        B_, C_, H_, W_ = v.shape
        g = v.reshape(B_, G, C_ // G, H_, W_)
        m = jnp.mean(g, axis=(2, 3, 4), keepdims=True)
        s = jnp.var(g, axis=(2, 3, 4), keepdims=True)
        return ((g - m) / jnp.sqrt(s + eps)).reshape(v.shape)

    def _ln_c(v, eps=1e-06):
        m = jnp.mean(v, axis=1, keepdims=True)
        s = jnp.var(v, axis=1, keepdims=True)
        return (v - m) / jnp.sqrt(s + eps)

    def _ln_t(v, eps=1e-05):
        m = jnp.mean(v, axis=-1, keepdims=True)
        s = jnp.var(v, axis=-1, keepdims=True)
        return (v - m) / jnp.sqrt(s + eps)

    def _to_tokens(v):
        B_, C_, H_, W_ = v.shape
        return v.reshape(B_, C_, H_ * W_).transpose(0, 2, 1)

    def _from_tokens(t, like):
        B_, C_, H_, W_ = like.shape
        return t.transpose(0, 2, 1).reshape(B_, C_, H_, W_)
    x = x + _L0_conv_ref(_ln_c(x), L0_conv_Wg, L0_conv_bg)
    t = _to_tokens(x)
    t = t + _L0_ffn_ref(_ln_t(t), L0_ffn_gate_w, L0_ffn_w_up, L0_ffn_b_up, L0_ffn_w_down, L0_ffn_b_down)
    x = _from_tokens(t, x)
    x = x + _L1_conv_ref(_ln_c(x), L1_conv_Wq, L1_conv_Wk, L1_conv_Wv, L1_conv_Wb, L1_conv_Wo)
    t = _to_tokens(x)
    t = t + _L1_ffn_ref(_ln_t(t), L1_ffn_Wg, L1_ffn_W1, L1_ffn_b1, L1_ffn_W2, L1_ffn_b2)
    x = _from_tokens(t, x)
    return x

_drawn_inputs = setup_inputs


def setup_inputs(seed=0):
    import zlib

    import numpy as np

    out = dict(_drawn_inputs(seed))
    spreads = {'L0_conv_bg': (0.0, 0.1),
     'L0_ffn_b_up': (0.0, 0.706),
     'L0_ffn_b_down': (0.0, 0.1),
     'L1_ffn_b1': (0.0, 0.8),
     'L1_ffn_b2': (0.0, 0.8)}
    factors = {}
    for name, (base, spread) in spreads.items():
        noise = np.random.default_rng([zlib.crc32(name.encode()), seed]).standard_normal(out[name].shape)
        drawn = base * np.exp(spread * noise) if base else spread * noise
        out[name] = jnp.asarray(drawn.astype(out[name].dtype))
    for name, factor in factors.items():
        out[name] = (out[name] * factor).astype(out[name].dtype)
    return out
```

```python
from contextlib import ExitStack

import concourse.bass as bass
from concourse import mybir

F32 = mybir.dt.float32
I32 = mybir.dt.int32
U32 = mybir.dt.uint32
ALU = mybir.AluOpType
ACT = mybir.ActivationFunctionType
AX_X = mybir.AxisListType.X

P = 128


def spread(ap, axis, n):
    wide = ap.unsqueeze(axis)
    shape = list(wide.shape)
    shape[axis] = n
    return wide.broadcast_to(shape)


def repeat(eng, trips, body):
    body(0)
    if trips > 1:
        with eng.Fori(1, trips) as i:
            body(i)


def one(t, i):
    return t[:, bass.ds(i, 1), :].rearrange("p o c -> p (o c)")


def later(i):
    return not isinstance(i, int)


class Order:

    def __init__(self, eng, sem):
        self.eng, self.sem, self.base, self.k, self.it, self.per = eng, sem, 0, 0, 0, 0

    def mark(self, ins):
        ins.then_inc(self.sem, 1)
        self.k += 1
        return ins

    def wait(self):
        self.eng.wait_ge(self.sem, self.it * self.per + (self.base + self.k))

    def trip(self, i, per):
        self.it, self.per, self.k = i, per, 0

    def end_trip(self):
        assert self.k == self.per, f"the body leaves {self.k} marks"

    def leave(self, trips):
        self.base, self.k, self.it, self.per = self.base + self.per * trips, 0, 0, 0


def metaformer(nc, x, conv_w, conv_b, moe_args, delta_args, out):
    B, C, H, W = x.shape
    L = H * W
    T = B * L
    NT = T // P
    CK = C // 2
    NG = conv_w.shape[0]
    GS = 4
    E = moe_args[0][0].shape[1]
    FF = moe_args[0][1].shape[2]
    FK = FF // P
    FH = FF // 2
    SLOT_TILES = 2 * NT + E
    REGION = T + P
    AHEAD = 2
    LISTED = SLOT_TILES + AHEAD

    with ExitStack() as top:
        def sb(name, shape, dt=F32, ctx=top):
            return ctx.enter_context(nc.sbuf_tensor(name, shape, dt))

        def ps(name, shape, dt=F32, ctx=top):
            return ctx.enter_context(nc.psum_tensor(name, shape, dt))

        def sem(name):
            return top.enter_context(nc.semaphore(name))

        def dram(name, shape, dt=F32):
            return nc.dram_tensor(name, shape, dt, kind="Internal").ap()

        expert_rows = dram("expert_rows", [E * REGION, C])
        slot_out = dram("slot_out", [SLOT_TILES * P, C])

        res = sb("res", [P, NT, C])
        ident = sb("ident", [P, P])
        ones = sb("ones", [P, P])
        before = sb("before", [P, P])
        mean_w = sb("mean_w", [CK, CK])
        zeros = sb("zeros", [P, C])
        expert_no = sb("expert_no", [P, E])
        tile_no = sb("tile_no", [P, LISTED])
        lane_no = sb("lane_no", [P, 1])
        eps = {e: sb(f"eps{n}", [P, 1]) for n, e in enumerate((1e-5, 1e-6))}
        mu_var = sb("mu_var", [P, NT, 2])
        rstd = sb("rstd", [P, NT])
        bn = sb("bn", [P, GS, 6])
        aggr = sb("aggr", [P, GS, 2])
        fence = sb("fence", [P, 1])

        const_pool = sem("const_pool")
        with ExitStack() as c, nc.Block() as block:
            iota_i = sb("iota_i", [P, P], I32, c)

            @block.gpsimd
            def _(pool):
                order = Order(pool, const_pool)
                order.mark(pool.memset(ident[:], 0.0))
                order.mark(pool.memset(before[:], 1.0))
                order.mark(pool.memset(ones[:], 1.0))
                order.mark(pool.memset(zeros[:], 0.0))
                order.mark(pool.memset(mean_w[:], 1.0 / C))
                for e, t in eps.items():
                    order.mark(pool.memset(t[:], e))
                order.wait()
                order.mark(pool.affine_select(out=ident[:], in_=ident[:], compare_op=ALU.not_equal, fill=1.0,
                                              base=0, pattern=[[-1, P]], channel_multiplier=1))
                order.mark(pool.affine_select(out=before[:], in_=before[:], compare_op=ALU.is_gt, fill=0.0,
                                              base=0, pattern=[[1, P]], channel_multiplier=-1))
                for dst, n, step, mult in ((expert_no, E, 1, 0), (tile_no, LISTED, 1, 0), (lane_no, 1, 0, 1)):
                    order.mark(pool.iota(iota_i[:, 0:n], pattern=[[step, n]], base=0, channel_multiplier=mult))
                    order.wait()
                    order.mark(pool.tensor_copy(dst[:], iota_i[:, 0:n]))
                    order.wait()

        def token_stats(tag, e):
            stats_dve, std_ready = sem(f"stats_dve{tag}"), sem(f"std_ready{tag}")
            with nc.Block() as block:
                @block.vector
                def _(v):
                    order = Order(v, stats_dve)

                    def body(i):
                        order.trip(i, 2 * GS + 1)
                        if later(i):
                            order.wait()
                        for u in range(GS):
                            order.mark(v.bn_stats(bn[:, u, :], one(res, i * GS + u)))
                        order.wait()
                        v.tensor_copy(fence[:], lane_no[:])
                        for u in range(GS):
                            order.mark(v.bn_aggr(aggr[:, u, :], bn[:, u, :]))
                        order.wait()
                        order.mark(v.tensor_copy(mu_var[:, bass.ds(i * GS, GS), :], aggr[:]))
                        order.end_trip()
                    repeat(v, NT // GS, body)
                    order.leave(NT // GS)
                    v.wait_ge(std_ready, 1)
                    v.reciprocal(rstd[:], rstd[:])

                @block.scalar
                def _(act):
                    act.wait_ge(stats_dve, (2 * GS + 1) * (NT // GS))
                    act.activation(rstd[:], mu_var[:, :, 1], ACT.Sqrt, bias=eps[e][:, 0:1]).then_inc(std_ready, 1)

        def moe(n, act_fn, w1, w2, b2, w_sem, w_full, ctx):
            gate_w = moe_args[n][0]
            token_stats(f"_m{n}", 1e-5)
            nm = lambda s: f"{s}{n}"
            gate = sb(nm("gate"), [CK, 2, E], ctx=ctx)
            logits = sb(nm("logits"), [P, NT, E], ctx=ctx)
            best = sb(nm("best"), [P, NT, 1], ctx=ctx)
            pick = sb(nm("pick"), [P, NT, 2, E], ctx=ctx)
            rank = sb(nm("rank"), [P, NT, 2], ctx=ctx)
            prob = sb(nm("prob"), [P, NT, 2], ctx=ctx)
            slot = sb(nm("slot"), [P, NT, 2], U32, ctx=ctx)
            listed = sb(nm("listed"), [P, 2, LISTED], U32, ctx=ctx)

            Q = 4
            with ExitStack() as rc:
                xn = sb(nm("xn"), [P, 2, Q, C], ctx=rc)
                xnT = sb(nm("xnT"), [CK, 2, Q, P], ctx=rc)
                lg = sb(nm("lg"), [P, Q, E], ctx=rc)
                top8 = sb(nm("top8"), [P, Q, 8], ctx=rc)
                idx = sb(nm("idx"), [P, Q, 8], U32, ctx=rc)
                idf = sb(nm("idf"), [P, Q, 2], ctx=rc)
                taken = sb(nm("taken"), [P, Q, E], ctx=rc)
                carry = sb(nm("carry"), [P, Q + 1, E], ctx=rc)
                place = sb(nm("place"), [P, Q, E], ctx=rc)
                mine = sb(nm("mine"), [P, Q, 2, E], ctx=rc)
                rowf = sb(nm("rowf"), [P, Q, 2], ctx=rc)
                row = sb(nm("row"), [P, 2, Q, 2], U32, ctx=rc)
                total = sb(nm("total"), [P, E], ctx=rc)
                padf = sb(nm("padf"), [P, E], ctx=rc)
                pad = sb(nm("pad"), [P, E], U32, ctx=rc)
                tilesi = sb(nm("tilesi"), [P, E], I32, ctx=rc)
                tiles = sb(nm("tiles"), [P, E], ctx=rc)
                upto = sb(nm("upto"), [P, E], ctx=rc)
                base = sb(nm("base"), [P, E], ctx=rc)
                wide = sb(nm("wide"), [P, NT * 2, E], ctx=rc)
                past = sb(nm("past"), [P, LISTED, E], ctx=rc)
                skipped = sb(nm("skipped"), [P, LISTED, E], ctx=rc)
                lf = sb(nm("lf"), [P, 4, LISTED], ctx=rc)
                ex = sb(nm("ex"), [P, NT, E], ctx=rc)
                den = sb(nm("den"), [P, NT], ctx=rc)
                psT = ps(nm("psT"), [CK, 2, Q, P], ctx=rc)
                psL = ps(nm("psL"), [P, 512], ctx=rc)
                psR = ps(nm("psR"), [P, 512], ctx=rc)
                (gate_in, dve, xn_ready, xnT_psum, xnT_ready, logits_psum, taken_ready, rank_psum, row_ready,
                 carry_ready, total_psum, pad_ready, padded, exp_in, exp_done) = [sem(nm(s)) for s in (
                    "gate_in", "dve", "xn_ready", "xnT_psum", "xnT_ready", "logits_psum", "taken_ready", "rank_psum",
                    "row_ready", "carry_ready", "total_psum", "pad_ready", "padded", "exp_in", "exp_done")]
                scattered = [sem(nm(f"scattered{u}_")) for u in range(2)]
                TRIPS = NT // (2 * Q)
                with nc.Block() as block:
                    @block.sync
                    def _(sp):
                        sp.dma_start(gate[:], gate_w.rearrange("(k c) e -> c k e", k=2)).then_inc(gate_in, 16)

                    @block.tensor
                    def _(pe):
                        pe.wait_ge(gate_in, 16)

                        def body(i):
                            for u in range(2):
                                g = i * 2 + u
                                pe.wait_ge(xn_ready, g * Q + Q)
                                for q in range(Q):
                                    for k in range(2):
                                        last = pe.transpose(psT[:, k, q, :], xn[:, u, q, k * CK:(k + 1) * CK], ident[:])
                                last.then_inc(xnT_psum, 1)
                                pe.wait_ge(xnT_ready, g + 1)
                                for q in range(Q):
                                    for k in range(2):
                                        last = pe.matmul(psL[:, q * E:(q + 1) * E], xnT[:, k, q, :], gate[:, k, :],
                                                         start=k == 0, stop=k == 1)
                                last.then_inc(logits_psum, 1)
                                pe.wait_ge(carry_ready, g + 1)
                                pe.matmul(psR[:, 0:Q * E], before[:], taken[:].rearrange("p q e -> p (q e)"),
                                          start=True, stop=False)
                                pe.matmul(psR[:, 0:Q * E], ones[:], carry[:, 0:Q, :].rearrange("p q e -> p (q e)"),
                                          start=False, stop=True).then_inc(rank_psum, 1)
                        repeat(pe, TRIPS, body)
                        pe.wait_ge(row_ready, 2 * TRIPS)
                        pe.matmul(psR[:, 0:E], ones[:], carry[:, Q, :], start=True, stop=True).then_inc(total_psum, 1)

                    @block.scalar
                    def _(act):
                        def body(i):
                            for u in range(2):
                                act.wait_ge(xnT_psum, i * 2 + (u + 1))
                                act.activation(xnT[:], psT[:], ACT.Copy).then_inc(xnT_ready, 1)
                        repeat(act, TRIPS, body)
                        act.wait_ge(exp_in, 1)
                        act.activation(ex[:], ex[:], ACT.Exp).then_inc(exp_done, 1)

                    @block.gpsimd
                    def _(pool):
                        def body(i):
                            for u in range(2):
                                pool.wait_ge(row_ready, i * 2 + (u + 1))
                                pool.nop(nofuse=True)
                                for q in range(Q):
                                    for k in range(2):
                                        pool.indirect_dma_start(
                                            expert_rows, bass.IndirectOffsetOnAxis(row[:, u, q, k:k + 1], 0),
                                            xn[:, u, q, :], None).then_inc(scattered[u], 16)
                        repeat(pool, TRIPS, body)
                        pool.wait_ge(pad_ready, 1)
                        for e in range(E):
                            pool.indirect_dma_start(expert_rows, bass.IndirectOffsetOnAxis(pad[:, e:e + 1], 0),
                                                    zeros[:], None).then_inc(padded, 16)
                        for u in range(2):
                            pool.wait_ge(scattered[u], TRIPS * Q * 2 * 16)
                        pool.wait_ge(padded, E * 16)

                    @block.vector
                    def _(v):
                        order = Order(v, dve)
                        order.mark(v.memset(carry[:], 0.0))
                        order.leave(0)
                        order.base = 1

                        def body(i):
                            order.trip(i, 2 * (2 * Q + 11))
                            for u in range(2):
                                g = i * 2 + u
                                if later(i):
                                    v.wait_ge(scattered[u], i * (Q * 2 * 16))
                                for q in range(Q):
                                    at = bass.ds(g * Q + q, 1)
                                    v.tensor_scalar(xn[:, u, q, :], one(res, g * Q + q), mu_var[:, at, 0], rstd[:, at],
                                                    ALU.subtract, ALU.mult).then_inc(xn_ready, 1)
                                group = bass.ds(g * Q, Q)
                                v.wait_ge(logits_psum, g + 1)
                                order.mark(v.tensor_copy(lg[:], psL[:, 0:Q * E].rearrange("p (q e) -> p q e", q=Q)))
                                order.wait()
                                order.mark(v.tensor_copy(logits[:, group, :], lg[:]))
                                for q in range(Q):
                                    order.mark(v.max(top8[:, q, :], lg[:, q, :]))
                                order.wait()
                                order.mark(v.tensor_copy(best[:, group, :], top8[:, :, 0:1]))
                                for q in range(Q):
                                    order.mark(v.max_index(idx[:, q, :], top8[:, q, :], lg[:, q, :]))
                                order.wait()
                                order.mark(v.tensor_copy(idf[:], idx[:, :, 0:2]))
                                order.wait()
                                chosen = pick[:, group, :, :]
                                order.mark(v.tensor_tensor(
                                    chosen.rearrange("p q k e -> p (q k) e"), spread(expert_no[:], 1, 2 * Q),
                                    spread(idf[:].rearrange("p q k -> p (q k)"), 2, E), ALU.is_equal))
                                order.wait()
                                if later(i) or u:
                                    v.wait_ge(rank_psum, g)
                                order.mark(v.tensor_tensor(taken[:], pick[:, group, 0, :], pick[:, group, 1, :], ALU.add))
                                order.mark(v.tensor_copy(carry[:, 0, :], carry[:, Q, :]))
                                order.wait()
                                for q in range(Q):
                                    ins = v.tensor_tensor(carry[:, q + 1, :], carry[:, q, :], taken[:, q, :], ALU.add)
                                    ins.then_inc(carried, 1)
                                    v.wait_ge(carried, g * Q + (q + 1))
                                v.nop().then_inc(carry_ready, 1)
                                v.wait_ge(rank_psum, g + 1)
                                order.mark(v.tensor_copy(place[:], psR[:, 0:Q * E].rearrange("p (q e) -> p q e", q=Q)))
                                order.wait()
                                order.mark(v.tensor_tensor(mine[:], spread(place[:], 2, 2), chosen, ALU.mult))
                                order.wait()
                                order.mark(v.tensor_reduce(rank[:, group, :], mine[:], AX_X, ALU.add))
                                order.wait()
                                order.mark(v.scalar_tensor_tensor(rowf[:], idf[:], float(REGION), rank[:, group, :],
                                                                  ALU.mult, ALU.add))
                                order.wait()
                                v.tensor_copy(row[:, u, :, :], rowf[:]).then_inc(row_ready, 1)
                            order.end_trip()
                        carried = sem(nm("carried"))
                        repeat(v, TRIPS, body)
                        order.leave(TRIPS)

                        def step(ins):
                            order.mark(ins)
                            order.wait()
                        v.tensor_tensor(ex[:], logits[:], best[:].broadcast_to([P, NT, E]),
                                        ALU.subtract).then_inc(exp_in, 1)
                        v.wait_ge(total_psum, 1)
                        step(v.tensor_copy(total[:], psR[:, 0:E]))
                        step(v.scalar_tensor_tensor(padf[:], expert_no[:], float(REGION), total[:], ALU.mult, ALU.add))
                        step(v.tensor_scalar(padf[:], padf[:], lane_no[:, 0:1], None, ALU.add))
                        v.tensor_copy(pad[:], padf[:]).then_inc(pad_ready, 1)
                        step(v.tensor_scalar(tiles[:], total[:], float(P - 1), None, ALU.add))
                        step(v.tensor_copy(tilesi[:], tiles[:]))
                        step(v.tensor_scalar(tilesi[:], tilesi[:], P.bit_length() - 1, None, ALU.arith_shift_right))
                        step(v.tensor_copy(tiles[:], tilesi[:]))
                        step(v.tensor_tensor_scan(upto[:], ones[:, 0:E], tiles[:], 0.0, ALU.mult, ALU.add))
                        step(v.tensor_tensor(base[:], upto[:], tiles[:], ALU.subtract))
                        step(v.tensor_scalar(base[:], base[:], float(P), None, ALU.mult))
                        step(v.tensor_tensor(wide[:], pick[:].rearrange("p t k e -> p (t k) e"), spread(base[:], 1, 2 * NT), ALU.mult))
                        step(v.tensor_reduce(prob[:].rearrange("p t k -> p (t k)"), wide[:], AX_X, ALU.add))
                        step(v.tensor_tensor(rank[:], rank[:], prob[:], ALU.add))
                        step(v.tensor_copy(slot[:], rank[:]))
                        step(v.tensor_tensor(past[:], spread(tile_no[:], 2, E), spread(upto[:], 1, LISTED), ALU.is_ge))
                        step(v.tensor_reduce(lf[:, 0, :], past[:], AX_X, ALU.add))
                        step(v.tensor_tensor(skipped[:], past[:], spread(tiles[:], 1, LISTED), ALU.mult))
                        step(v.tensor_reduce(lf[:, 1, :], skipped[:], AX_X, ALU.add))
                        step(v.tensor_tensor(lf[:, 1, :], tile_no[:], lf[:, 1, :], ALU.subtract))
                        step(v.tensor_scalar(lf[:, 2, :], lf[:, 0, :], float(REGION // P), None, ALU.mult))
                        step(v.tensor_tensor(lf[:, 1, :], lf[:, 1, :], lf[:, 2, :], ALU.add))
                        step(v.tensor_scalar(lf[:, 3, :], lf[:, 0, :], float(E), None, ALU.is_lt))
                        step(v.tensor_tensor(lf[:, 0, :], lf[:, 0, :], lf[:, 3, :], ALU.mult))
                        step(v.tensor_tensor(lf[:, 1, :], lf[:, 1, :], lf[:, 3, :], ALU.mult))
                        step(v.tensor_copy(listed[:], lf[:, 0:2, :]))
                        v.wait_ge(exp_done, 1)
                        step(v.tensor_reduce(den[:], ex[:], AX_X, ALU.add))
                        step(v.reciprocal(den[:], den[:]))
                        step(v.tensor_tensor(wide[:].rearrange("p (t k) e -> p t k e", k=2), pick[:], spread(ex[:], 2, 2), ALU.mult))
                        step(v.tensor_reduce(prob[:].rearrange("p t k -> p (t k)"), wide[:], AX_X, ALU.add))
                        step(v.tensor_tensor(prob[:], prob[:], spread(den[:], 2, 2), ALU.mult))

            with ExitStack() as tc:
                xt = sb(nm("xt"), [P, 2, C], ctx=tc)
                xT = sb(nm("xT"), [CK + 1, 2, 2, P], ctx=tc)
                h = sb(nm("h"), [P, 2, FF], ctx=tc)
                hT = sb(nm("hT"), [P, 2, FK, P], ctx=tc)
                y = sb(nm("y"), [P, 2, C], ctx=tc)
                psX = ps(nm("psX"), [CK, 2, P], ctx=tc)
                psU = ps(nm("psU"), [P, 2, 512], ctx=tc)
                psH = ps(nm("psH"), [P, 2, 512], ctx=tc)
                psY = ps(nm("psY"), [P, 512], ctx=tc)
                (xT_psum, xT_ready, up_psum, h_ready, hT_psum, hT_ready, y_psum, y_ready, ones_set) = [
                    sem(nm(s)) for s in ("xT_psum", "xT_ready", "up_psum", "h_ready", "hT_psum", "hT_ready", "y_psum",
                                         "y_ready", "ones_set")]
                x_in = [sem(nm(f"x_in{u}_")) for u in range(2)]
                y_out = [sem(nm(f"y_out{u}_")) for u in range(2)]
                TRIPS = SLOT_TILES // 2
                rows_of_tiles = expert_rows.rearrange("(t p) c -> t p c", p=P)
                out_tiles = slot_out.rearrange("(t p) c -> t p c", p=P)
                with nc.Block() as block:
                    @block.sync
                    def _(sp):
                        def load(tile, u):
                            r = sp.value_load(listed[0:1, 1, bass.ds(tile, 1)], min_val=0, max_val=E * REGION // P - 1)
                            sp.dma_start(xt[:, u, :], rows_of_tiles[bass.ds(r, 1), :, :].rearrange("t p c -> (t p) c")).then_inc(x_in[u], 16)
                        for u in range(2):
                            load(u, u)

                        def body(i):
                            for u in range(2):
                                sp.wait_ge(xT_psum, i * 2 + (u + 1))
                                load(i * 2 + (u + 2), u)
                        repeat(sp, TRIPS, body)
                        for u in range(2):
                            sp.wait_ge(x_in[u], 16 * (TRIPS + 1))

                    @block.tensor
                    def _(pe):
                        pe.wait_ge(w_sem, w_full)
                        pe.wait_ge(ones_set, 1)

                        def turn_x(tile, u, trip):
                            pe.wait_ge(x_in[u], trip * 16 + 16)
                            for k in range(2):
                                last = pe.transpose(psX[:, k, :], xt[:, u, k * CK:(k + 1) * CK], ident[:])
                            last.then_inc(xT_psum, 1)

                        def up(tile, u, first=False):
                            e = pe.value_load(listed[0:1, 0, bass.ds(tile, 1)], min_val=0, max_val=E - 1)
                            pe.wait_ge(xT_ready, tile + 1)
                            if not first:
                                pe.wait_ge(h_ready, tile)
                            for f in range(2):
                                for k in range(2):
                                    n_k = CK + 1 - k
                                    last = pe.matmul(psU[:, f, 0:FH], xT[0:n_k, u, k, :],
                                                     w1[0:n_k, k, bass.ds(e, 1), f * FH:(f + 1) * FH],
                                                     start=k == 0, stop=k == 1)
                            last.then_inc(up_psum, 1)

                        turn_x(0, 0, 0)
                        up(0, 0, first=True)

                        def body(i):
                            for u in range(2):
                                tile = i * 2 + u
                                turn_x(tile + 1, 1 - u, i + u)
                                pe.wait_ge(h_ready, tile + 1)
                                if later(i) or u:
                                    pe.wait_ge(hT_ready, tile)
                                for k in range(FK):
                                    last = pe.transpose(psH[:, k // 3, (k % 3) * P:(k % 3 + 1) * P],
                                                        h[:, u, k * P:(k + 1) * P], ident[:])
                                last.then_inc(hT_psum, 1)
                                up(tile + 1, 1 - u)
                                e = pe.value_load(listed[0:1, 0, bass.ds(tile, 1)], min_val=0, max_val=E - 1)
                                pe.wait_ge(hT_ready, tile + 1)
                                if later(i) or u:
                                    pe.wait_ge(y_ready, tile)
                                for k in range(FK):
                                    last = pe.matmul(psY[:, 0:C], hT[:, u, k, :], w2[:, k, bass.ds(e, 1), :],
                                                     start=k == 0, stop=k == FK - 1)
                                last.then_inc(y_psum, 1)
                        repeat(pe, TRIPS, body)

                    @block.scalar
                    def _(act):
                        def turn(tile, u):
                            act.wait_ge(xT_psum, tile + 1)
                            act.activation(xT[0:CK, u, :, :], psX[:], ACT.Copy).then_inc(xT_ready, 1)

                        def hidden(tile, u):
                            act.wait_ge(up_psum, tile + 1)
                            act.activation(h[:, u, :].rearrange("p (f m) -> p f m", f=2), psU[:, :, 0:FH], act_fn).then_inc(h_ready, 1)
                        turn(0, 0)
                        hidden(0, 0)

                        def body(i):
                            for u in range(2):
                                turn(i * 2 + (u + 1), 1 - u)
                                hidden(i * 2 + (u + 1), 1 - u)
                        repeat(act, TRIPS, body)

                    @block.vector
                    def _(v):
                        v.memset(xT[CK:CK + 1, :, 0, :], 1.0).then_inc(ones_set, 1)
                        v.wait_ge(w_sem, w_full)

                        def body(i):
                            for u in range(2):
                                tile = i * 2 + u
                                v.wait_ge(hT_psum, tile + 1)
                                v.tensor_copy(hT[:, u, :, :].rearrange("p (a b) t -> p a (b t)", a=2),
                                              psH[:, :, 0:FH]).then_inc(hT_ready, 1)
                                e = v.value_load(listed[0:1, 0, bass.ds(tile, 1)], min_val=0, max_val=E - 1)
                                v.wait_ge(y_psum, tile + 1)
                                if later(i):
                                    v.wait_ge(y_out[u], i * 16)
                                v.tensor_tensor(y[:, u, :], psY[:, 0:C], b2[:, bass.ds(e, 1), :].rearrange("p o c -> p (o c)"), ALU.add).then_inc(y_ready, 1)
                        repeat(v, TRIPS, body)

                    @block.gpsimd
                    def _(pool):
                        def body(i):
                            for u in range(2):
                                pool.wait_ge(y_ready, i * 2 + (u + 1))
                                pool.dma_start(out_tiles[bass.ds(i * 2 + u, 1), :, :].rearrange("t p c -> (t p) c"), y[:, u, :]).then_inc(y_out[u], 16)
                        repeat(pool, TRIPS, body)
                        for u in range(2):
                            pool.wait_ge(y_out[u], 16 * TRIPS)

            with ExitStack() as gc:
                got = sb(nm("got"), [P, 4, 2, C], ctx=gc)
                gathered = [sem(nm(f"gathered{u}_")) for u in range(4)]
                half_added, added = sem(nm("half_added")), sem(nm("added"))
                TRIPS = NT // 4
                with nc.Block() as block:
                    @block.gpsimd
                    def _(pool):
                        def body(i):
                            for u in range(4):
                                if later(i):
                                    pool.wait_ge(added, i * 4 + (u - 3))
                                for k in range(2):
                                    pool.tensor_copy(at_idx[:, u, k:k + 1], slot[:, bass.ds(i * 4 + u, 1), k]).then_inc(idx_set, 1)
                                pool.wait_ge(idx_set, i * 8 + (2 * u + 2))
                                pool.nop(nofuse=True)
                                for k in range(2):
                                    pool.indirect_dma_start(got[:, u, k, :], None, slot_out,
                                                            bass.IndirectOffsetOnAxis(at_idx[:, u, k:k + 1], 0)).then_inc(gathered[u], 16)
                        at_idx = sb(nm("at_idx"), [P, 4, 2], U32, ctx=gc)
                        idx_set = sem(nm("idx_set"))
                        repeat(pool, TRIPS, body)

                    @block.vector
                    def _(v):
                        def body(i):
                            for u in range(4):
                                at = bass.ds(i * 4 + u, 1)
                                v.wait_ge(gathered[u], i * 32 + 32)
                                v.scalar_tensor_tensor(one(res, i * 4 + u), got[:, u, 0, :], prob[:, at, 0], one(res, i * 4 + u),
                                                       ALU.mult, ALU.add).then_inc(half_added, 1)
                                v.wait_ge(half_added, i * 4 + (u + 1))
                                v.scalar_tensor_tensor(one(res, i * 4 + u), got[:, u, 1, :], prob[:, at, 1], one(res, i * 4 + u),
                                                       ALU.mult, ALU.add).then_inc(added, 1)
                        repeat(v, TRIPS, body)

        def delta(ctx):
            wq, wk, wv, wb, wo = delta_args
            NH = wb.shape[1]
            D = C // NH
            K = 16
            HB = P // (L // K)
            HALVES = B // HB
            HT = NT // HALVES
            HC = NH // 2
            X = K + K
            NCH = L // K
            token_stats("_d", 1e-6)
            w_all = sb("w_all", [CK, 2, 3 * C + NH], ctx=ctx)
            w_o = sb("w_o", [CK, 2, C], ctx=ctx)
            blocks = sb("blocks", [CK, HC, D], ctx=ctx)
            area1 = sb("area1", [P, 2 * K * P * 2 // 2], ctx=ctx)
            tT = area1[0:CK, :].rearrange("c (k t) -> c k t", k=2)
            oT = tT
            y_rows = area1[:, 0:K * C].rearrange("p (t c) -> p t c", t=K)
            area2 = sb("area2", [P, K * 3 * C], ctx=ctx)
            qkv = area2[:].rearrange("p (t c) -> p t c", t=K)
            o_sys = area2[:, 0:K * C].rearrange("p (t c) -> p t c", t=K)
            uo_sys = area2[:, K * C:3 * K * C].rearrange("p (x c) -> p x c", x=X)
            z = sb("z", [P, K, 2, C], ctx=ctx)
            wqT = sb("wqT", [CK, 2, P, X], ctx=ctx)
            AREA3 = max(4 * 8 * CK + 8 * C, 4 * HB * X + 8 * C + 4 * C + 16 * CK)
            area3 = sb("area3", [P, AREA3], ctx=ctx)
            k_blk = area3[0:CK, 0:4 * 8 * CK].rearrange("c (u k p m) -> c u k p m", u=2, k=2, p=8)
            kq_out = area3[:, 4 * 8 * CK:4 * 8 * CK + 8 * C].rearrange("p (u g c) -> p u g c", u=2, g=4)
            at = 0

            def cut(n):
                nonlocal at
                at += n
                return area3[:, at - n:at]
            wq_n = cut(2 * 2 * HB * X)[0:CK, :].rearrange("c (u k b x) -> c u k b x", u=2, k=2, b=HB)
            yk = cut(2 * 2 * 2 * C).rearrange("p (u b c) -> p u b c", u=2, b=2)
            uo = cut(2 * 2 * C).rearrange("p (u m) -> p u m", u=2)
            s_blk = cut(4 * 4 * CK)[0:CK, :].rearrange("c (j g m) -> c j g m", j=4, g=4)
            assert at <= AREA3
            kp = sb("kp", [P, X, NH, K], ctx=ctx)
            tmp = sb("tmp", [P, HC * X * K], ctx=ctx)
            tn = tmp[:, 0:2 * 4 * C].rearrange("p (u q c) -> p u q c", u=2, q=4)
            red = sb("red", [P, 2, C], ctx=ctx)
            ss = sb("ss", [P, K, 2 * NH], ctx=ctx)
            beta = sb("beta", [P, K, NH], ctx=ctx)
            bank = ps("bank", [P, 8, 512], ctx=ctx)
            kq_rows = dram("kq_rows", [HALVES, P // 4, P, C])
            yk_rows = dram("yk_rows", [HALVES * P, X, 2 * C])
            uo_rows = dram("uo_rows", [HALVES * P, X, C])

            names = ("d_weights", "d_blocks", "d_pool", "half_open", "t_ready", "t_turned", "t_copied", "proj_psum",
                     "proj_act", "beta_copied", "squares", "norms", "gates", "d_dve", "kq_turned", "kq_copied", "kblk_dve",
                     "kblk_pool", "kk_psum", "kk_copied", "kp_in", "k_out", "z_ready", "w_turned", "w_copied",
                     "y_copied", "y_out", "s_zero", "s_ready", "wq_ready", "ws_psum", "uo_ready", "s_psum", "uo_in",
                     "o_ready", "o_turned_d", "o_copied_d", "y_psum_d", "y_added", "z_rows", "t_added", "wq_free")
            S = {s: sem(s) for s in names}
            yk_in = [sem(f"yk_in{u}") for u in range(2)]
            uo_out = [sem(f"uo_out{u}") for u in range(2)]
            kk_out = [sem(f"kk_out{u}_") for u in range(2)]
            heads_of = lambda ap: ap.rearrange("p (h d) -> p h d", d=D)
            heads = lambda ap: ap.rearrange("p t (h d) -> p t h d", d=D)

            with nc.Block() as block:
                @block.gpsimd
                def _(pool):
                    order = Order(pool, S["d_pool"])
                    order.mark(pool.memset(blocks[:], 1.0))
                    order.wait()
                    order.mark(pool.affine_select(out=blocks[:], in_=blocks[:], compare_op=ALU.is_ge, fill=0.0, base=0,
                                                  pattern=[[-D, HC], [0, D]], channel_multiplier=1))
                    order.wait()
                    pool.affine_select(out=blocks[:], in_=blocks[:], compare_op=ALU.is_ge, fill=0.0, base=D - 1,
                                       pattern=[[D, HC], [0, D]], channel_multiplier=-1).then_inc(S["d_blocks"], 1)
                    pool.wait_ge(S["d_blocks"], 1)
                    with pool.Fori(0, HALVES) as hb:
                        for c in range(16):
                            u = c % 2
                            pool.wait_ge(S["kq_copied"], hb * K + K)
                            if c >= 2:
                                pool.wait_ge(S["kk_psum"], hb * 16 + (c - 1))
                            pool.tensor_tensor(k_blk[:, u, 0, :, :].rearrange("c p (h t) -> c p h t", h=HC),
                                               spread(wqT[:, 0, 8 * c:8 * c + 8, 0:K], 2, HC), spread(blocks[:], 1, 8),
                                               ALU.mult).then_inc(S["kblk_pool"], 1)

                @block.sync
                def _(sp):
                    for n, w in enumerate((wq, wk, wv, wb)):
                        sp.dma_start(w_all[:, :, n * C:n * C + w.shape[1]], w.rearrange("(k c) o -> c k o", k=2)).then_inc(S["d_weights"], 16)
                    sp.dma_start(w_o[:], wo.rearrange("(k c) o -> c k o", k=2)).then_inc(S["d_weights"], 16)
                    for hb in range(HALVES):
                        for c in range(2):
                            sp.dma_start(yk_rows[hb * P:(hb + 1) * P, K:X, c * C:(c + 1) * C], spread(zeros[:], 1, K)).then_inc(S["z_rows"], 16)
                    sp.wait_ge(S["z_rows"], 64)
                    with sp.Fori(0, HALVES) as hb:
                        rows = yk_rows[bass.ds(hb * P, P), :, :]
                        sp.wait_ge(S["norms"], hb * 2 + 2)
                        sp.nop(nofuse=True)
                        sp.dma_start(rows[:, 0:K, C:2 * C], qkv[:, :, C:2 * C]).then_inc(S["k_out"], 16)
                        for c in range(8):
                            u = c % 2
                            sp.wait_ge(S["kk_copied"], hb * 8 + (c + 1))
                            sp.nop(nofuse=True)
                            sp.dma_start(kq_rows[bass.ds(hb, 1), 4 * c:4 * c + 4, :, :].rearrange("o g p c -> (o p) g c"),
                                         kq_out[:, u, :, :]).then_inc(kk_out[u], 16)
                        for u in range(2):
                            sp.wait_ge(kk_out[u], hb * 64 + 64)
                            sp.nop(nofuse=True)
                        sp.dma_start(kp[:].rearrange("p x h t -> p (x h t)"),
                                     kq_rows[bass.ds(hb, 1), :, :, :].rearrange("o g (j x) c -> (o g j) (x c)", j=4)).then_inc(S["kp_in"], 16)
                        sp.wait_ge(S["y_copied"], hb + 1)
                        sp.nop(nofuse=True)
                        sp.dma_start(rows[:, 0:K, 0:C], y_rows[:]).then_inc(S["y_out"], 16)
                        sp.wait_ge(S["y_out"], hb * 16 + 16)
                        sp.wait_ge(S["k_out"], hb * 16 + 16)
                        sp.nop(nofuse=True)

                        chunk_in = yk_rows[bass.ds(hb * P, P), :, :].rearrange("(b j n) x c -> j n x b c", b=2, j=4)
                        chunk_out = uo_rows[bass.ds(hb * P, P), :, :].rearrange("(b j n) x c -> j n x b c", b=2, j=4)

                        def load(n, u):
                            for j in range(4):
                                sp.dma_start(yk[32 * j:32 * j + 32, u, :, :],
                                             chunk_in[j, bass.ds(n, 1), :, :, :].rearrange("o x b c -> (o x) b c")).then_inc(yk_in[u], 16)
                        for u in range(2):
                            load(u, u)

                        def chunks(i, more):
                            for u in range(2):
                                sp.wait_ge(S["uo_ready"], hb * (2 * NCH) + (i * 4 + (2 * u + 2)))
                                sp.nop(nofuse=True)
                                for j in range(4):
                                    sp.dma_start(chunk_out[j, bass.ds(i * 2 + u, 1), :, :, :].rearrange("o x b c -> (o x) b c"),
                                                 uo[32 * j:32 * j + 32, u, :].rearrange("x (b c) -> x b c", b=2)).then_inc(uo_out[u], 16)
                                if more:
                                    sp.wait_ge(S["s_psum"], hb * (2 * NCH) + (i * 4 + (2 * u + 2)))
                                    sp.nop(nofuse=True)
                                    load(i * 2 + (u + 2), u)
                        with sp.Fori(0, NCH // 2 - 1) as i:
                            chunks(i, True)
                        chunks(NCH // 2 - 1, False)
                        for u in range(2):
                            sp.wait_ge(uo_out[u], hb * (64 * NCH // 2) + 64 * NCH // 2)
                            sp.wait_ge(yk_in[u], hb * (32 * NCH) + 32 * NCH)
                            sp.nop(nofuse=True)
                        sp.dma_start(uo_sys[:].rearrange("p x c -> p (x c)"),
                                     uo_rows[bass.ds(hb * P, P), :, :].rearrange("p x c -> p (x c)")).then_inc(S["uo_in"], 16)

                @block.tensor
                def _(pe):
                    pe.wait_ge(S["d_weights"], 16 * 5)
                    with pe.Fori(0, HALVES) as hb:
                        for g in range(4):
                            u = g % 2
                            pe.wait_ge(S["t_ready"], hb * 16 + (4 * g + 4))
                            if g >= 2:
                                pe.wait_ge(S["t_copied"], hb * 4 + (g - 1))
                            for q in range(4):
                                for k in range(2):
                                    last = pe.transpose(bank[0:CK, 2 * u + k, q * P:(q + 1) * P], tn[:, u, q, k * CK:(k + 1) * CK], ident[:])
                            last.then_inc(S["t_turned"], 1)
                        pe.wait_ge(S["t_copied"], hb * 4 + 4)
                        for t in range(K):
                            b0 = 4 + 2 * (t % 2)
                            if t >= 2:
                                pe.wait_ge(S["proj_act"], hb * (2 * K) + 2 * (t - 1))
                                pe.wait_ge(S["beta_copied"], hb * K + (t - 1))
                            for c, (lo, hi) in enumerate(((0, 2 * C), (2 * C, 3 * C + NH))):
                                for k in range(2):
                                    last = pe.matmul(bank[:, b0 + c, 0:hi - lo], tT[:, k, t::K], w_all[:, k, lo:hi], start=k == 0, stop=k == 1)
                            last.then_inc(S["proj_psum"], 1)
                        pe.wait_ge(S["norms"], hb * 2 + 2)
                        for t in range(K):
                            if t < 2:
                                pe.wait_ge(S["beta_copied"], hb * K + K)
                            else:
                                pe.wait_ge(S["kq_copied"], hb * K + (t - 1))
                            for x in range(2):
                                for k in range(2):
                                    lo = (1 - x) * C + k * CK
                                    last = pe.transpose(bank[0:CK, 6 + t % 2, (2 * x + k) * P:(2 * x + k + 1) * P], qkv[:, t, lo:lo + CK], ident[:])
                            last.then_inc(S["kq_turned"], 1)
                        for c in range(16):
                            u = c % 2
                            pe.wait_ge(S["kblk_dve"], hb * 16 + (c + 1))
                            pe.wait_ge(S["kblk_pool"], hb * 16 + (c + 1))
                            v4 = (c // 2) % 2
                            if c >= 4:
                                pe.wait_ge(S["kk_copied"], hb * 8 + (c // 2 - 1))
                            for g in range(2):
                                for j in range(4):
                                    for k in range(2):
                                        q = 4 * g + j
                                        last = pe.matmul(bank[32 * j:32 * j + 32, 2 * v4 + u, g * C + k * CK:g * C + (k + 1) * CK],
                                                         wqT[:, k, 8 * c + q, :], k_blk[:, u, k, q, :], start=True, stop=True,
                                                         tile_position=(0, 32 * j))
                            last.then_inc(S["kk_psum"], 1)
                        pe.wait_ge(S["z_ready"], hb + 1)
                        for t in range(K):
                            if t >= 2:
                                pe.wait_ge(S["w_copied"], hb * K + (t - 1))
                            for k in range(2):
                                last = pe.transpose(bank[0:CK, 6 + t % 2, k * P:(k + 1) * P], z[:, t, 1, k * CK:(k + 1) * CK], ident[:])
                            last.then_inc(S["w_turned"], 1)
                        pe.wait_ge(S["s_zero"], hb + 1)
                        pe.nop(nofuse=True)
                        with pe.Fori(0, NCH // 2) as i:
                            for u in range(2):
                                pe.wait_ge(S["wq_ready"], hb * NCH + (i * 2 + (u + 1)))
                                for s in range(2):
                                    pe.wait_ge(S["s_ready"], hb * (2 * NCH + 2) + (i * 4 + (2 * u + s + 1)))
                                    for j in (2 * s, 2 * s + 1):
                                        for b in range(2):
                                            for k in range(2):
                                                m = (2 * b + k) * CK
                                                last = pe.matmul(bank[32 * j:32 * j + 32, 4 + s, m:m + CK], wq_n[:, u, k, 4 * b + j, :],
                                                                 s_blk[:, j, 2 * b + k, :], start=True, stop=True, tile_position=(0, 32 * j))
                                    last.then_inc(S["ws_psum"], 1)
                                pe.wait_ge(yk_in[u], hb * (32 * NCH) + (i * 64 + 64))
                                for s in range(2):
                                    pe.wait_ge(S["uo_ready"], hb * (2 * NCH) + (i * 4 + (2 * u + s + 1)))
                                    for j in (2 * s, 2 * s + 1):
                                        for b in range(2):
                                            for k in range(2):
                                                m = (2 * b + k) * CK
                                                last = pe.matmul(bank[0:CK, j, m:m + CK], yk[32 * j:32 * j + K, u, b, C + k * CK:C + (k + 1) * CK],
                                                                 uo[32 * j:32 * j + K, u, m:m + CK], start=False, stop=True,
                                                                 skip_group_check=True)
                                    last.then_inc(S["s_psum"], 1)
                        pe.wait_ge(S["o_ready"], hb + 1)
                        for t in range(K):
                            if t >= 2:
                                pe.wait_ge(S["o_copied_d"], hb * K + (t - 1))
                            for k in range(2):
                                last = pe.transpose(bank[0:CK, 6 + t % 2, k * P:(k + 1) * P], o_sys[:, t, k * CK:(k + 1) * CK], ident[:])
                            last.then_inc(S["o_turned_d"], 1)
                        pe.wait_ge(S["o_copied_d"], hb * K + K)
                        for j in range(HT):
                            if j >= 2:
                                pe.wait_ge(S["y_added"], hb * HT + (j - 1))
                            for k in range(2):
                                last = pe.matmul(bank[:, 4 + j % 2, 0:C], oT[:, k, j * P:(j + 1) * P], w_o[:, k, :], start=k == 0, stop=k == 1)
                            last.then_inc(S["y_psum_d"], 1)

                @block.scalar
                def _(act):
                    with act.Fori(0, HALVES) as hb:
                        for g in range(4):
                            act.wait_ge(S["t_turned"], hb * 4 + (g + 1))
                            act.activation(tT[:, :, g * 4 * P:(g + 1) * 4 * P], bank[0:CK, 2 * (g % 2):2 * (g % 2) + 2, :], ACT.Copy).then_inc(S["t_copied"], 1)
                        for t in range(K):
                            act.wait_ge(S["proj_psum"], hb * K + (t + 1))
                            b0 = 4 + 2 * (t % 2)
                            act.activation(qkv[:, t, 0:2 * C], bank[:, b0, 0:2 * C], ACT.Silu).then_inc(S["proj_act"], 1)
                            act.activation(qkv[:, t, 2 * C:3 * C], bank[:, b0 + 1, 0:C], ACT.Silu).then_inc(S["proj_act"], 1)
                            act.activation(beta[:, t, :], bank[:, b0 + 1, C:C + NH], ACT.Copy).then_inc(S["beta_copied"], 1)
                        act.wait_ge(S["beta_copied"], hb * K + K)
                        act.activation(beta[:], beta[:], ACT.Sigmoid).then_inc(S["gates"], 1)
                        act.wait_ge(S["squares"], hb + 1)
                        act.activation(ss[:], ss[:], ACT.Sqrt, bias=eps[1e-6][:, 0:1]).then_inc(S["norms"], 1)
                        for t in range(K):
                            act.wait_ge(S["kq_turned"], hb * K + (t + 1))
                            act.activation(wqT[:].rearrange("c k p (x t) -> c x k p t", x=2)[:, :, :, :, t],
                                           bank[0:CK, 6 + t % 2, :].rearrange("c (x k p) -> c x k p", x=2, k=2), ACT.Copy).then_inc(S["kq_copied"], 1)
                        for c in range(8):
                            u = c % 2
                            act.wait_ge(S["kk_psum"], hb * 16 + (2 * c + 2))
                            if c >= 2:
                                act.wait_ge(kk_out[u], hb * 64 + 16 * (c // 2))
                            act.activation(kq_out[:, u, :, :].rearrange("p (a g) c -> p a (g c)", a=2),
                                           bank[:, 2 * u:2 * u + 2, 0:2 * C], ACT.Copy).then_inc(S["kk_copied"], 1)
                        for t in range(K):
                            act.wait_ge(S["w_turned"], hb * K + (t + 1))
                            act.activation(wqT[:, :, :, t], bank[0:CK, 6 + t % 2, 0:2 * P].rearrange("c (k p) -> c k p", k=2), ACT.Copy).then_inc(S["w_copied"], 1)
                        act.activation(y_rows[:], z[:, :, 0, :], ACT.Copy).then_inc(S["y_copied"], 1)
                        act.wait_ge(S["w_copied"], hb * K + K)
                        with act.Fori(0, NCH // 2) as i:
                            for u in range(2):
                                act.wait_ge(S["half_open"], hb + 1)
                                act.wait_ge(S["wq_free"], hb * (NCH + 2) + (i * 2 + (u + 1)))
                                act.activation(wq_n[:, u, :, :, :], wqT[:].rearrange("c k (b n) x -> c k b n x", n=NCH)[:, :, :, bass.ds(i * 2 + u, 1), :].rearrange("c k b o x -> c k b (o x)"),
                                               ACT.Copy).then_inc(S["wq_ready"], 1)
                        for t in range(K):
                            act.wait_ge(S["o_turned_d"], hb * K + (t + 1))
                            act.activation(oT[:, :, t::K], bank[0:CK, 6 + t % 2, 0:2 * P].rearrange("c (k p) -> c k p", k=2), ACT.Copy).then_inc(S["o_copied_d"], 1)

                @block.vector
                def _(v):
                    order = Order(v, S["d_dve"])
                    v.nop().then_inc(S["half_open"], 1)
                    with v.Fori(0, HALVES) as hb:
                        order.trip(hb, 16 + 1 + 2 + 1 + 15 * 5 + 2 + 16 * 5)

                        def step(ins):
                            order.mark(ins)
                            order.wait()
                        v.wait_ge(S["half_open"], hb + 1)
                        for g in range(4):
                            u = g % 2
                            if g >= 2:
                                v.wait_ge(S["t_turned"], hb * 4 + (g - 1))
                                v.wait_ge(S["t_added"], hb * 4 + (g - 1))
                            for q in range(4):
                                tile = hb * HT + (4 * g + q)
                                v.tensor_scalar(tn[:, u, q, :], one(res, tile), mu_var[:, bass.ds(tile, 1), 0], rstd[:, bass.ds(tile, 1)],
                                                ALU.subtract, ALU.mult).then_inc(S["t_ready"], 1)
                            v.wait_ge(S["t_ready"], hb * 16 + (4 * g + 4))
                            four = res[:, bass.ds(hb * HT + 4 * g, 4), :]
                            v.tensor_tensor(four, four, tn[:, u, :, :], ALU.add).then_inc(S["t_added"], 1)
                        v.wait_ge(S["t_added"], hb * 4 + 4)
                        v.wait_ge(S["t_turned"], hb * 4 + 4)
                        for g in range(8):
                            sq = tmp[:, 0:4 * C].rearrange("p (t c) -> p t c", t=2)
                            v.wait_ge(S["proj_act"], hb * (2 * K) + 4 * (g + 1))
                            step(v.tensor_tensor(sq, qkv[:, 2 * g:2 * g + 2, 0:2 * C], qkv[:, 2 * g:2 * g + 2, 0:2 * C], ALU.mult))
                            step(v.tensor_reduce(ss[:, 2 * g:2 * g + 2, :], sq.rearrange("p t (h d) -> p t h d", d=D), AX_X, ALU.add))
                        v.nop().then_inc(S["squares"], 1)
                        v.wait_ge(S["norms"], hb * 2 + 1)
                        step(v.reciprocal(ss[:], ss[:]))
                        v.tensor_tensor(heads(qkv[:, :, 0:2 * C]), heads(qkv[:, :, 0:2 * C]), spread(ss[:], 3, D), ALU.mult).then_inc(S["norms"], 1)
                        v.wait_ge(S["gates"], hb + 1)
                        v.wait_ge(S["norms"], hb * 2 + 2)
                        order.mark(v.tensor_tensor(heads(z[:, :, 0, :]), heads(qkv[:, :, 2 * C:3 * C]), spread(beta[:], 3, D), ALU.mult))
                        order.mark(v.tensor_tensor(heads(z[:, :, 1, :]), heads(qkv[:, :, C:2 * C]), spread(beta[:], 3, D), ALU.mult))
                        for c in range(16):
                            u = c % 2
                            v.wait_ge(S["kq_copied"], hb * K + K)
                            v.wait_ge(S["d_blocks"], 1)
                            if c >= 2:
                                v.wait_ge(S["kk_psum"], hb * 16 + (c - 1))
                            v.tensor_tensor(k_blk[:, u, 1, :, :].rearrange("c p (h t) -> c p h t", h=HC),
                                            spread(wqT[:, 1, 8 * c:8 * c + 8, 0:K], 2, HC), spread(blocks[:], 1, 8),
                                            ALU.mult).then_inc(S["kblk_dve"], 1)
                        v.wait_ge(S["kp_in"], hb * 16 + 16)
                        step(v.tensor_tensor(kp[:, 0:K, :, :], kp[:, 0:K, :, :], spread(beta[:], 3, K), ALU.mult))
                        for i in range(1, K):
                            for f in range(2):
                                pr = tmp[:, 0:C * i].rearrange("p (h x j) -> p h x j", h=NH, x=D)
                                step(v.tensor_tensor(pr, spread(kp[:, i, :, 0:i], 2, D), z[:, 0:i, f, :].rearrange("p j (h x) -> p h x j", x=D), ALU.mult))
                                step(v.tensor_reduce(red[:, f, :].rearrange("p (h x) -> p h x", x=D), pr, AX_X, ALU.add))
                            step(v.tensor_tensor(z[:, i, :, :], z[:, i, :, :], red[:], ALU.subtract))
                        v.nop().then_inc(S["z_ready"], 1)
                        v.wait_ge(S["kk_copied"], hb * 8 + 8)
                        for u in range(2):
                            v.wait_ge(kk_out[u], hb * 64 + 64)
                        order.mark(v.memset(bank[0:CK, 0:4, 0:4 * CK], 0.0))
                        order.mark(v.memset(s_blk[:], 0.0))
                        order.wait()
                        v.nop().then_inc(S["s_zero"], 1)
                        for s in range(2):
                            v.nop().then_inc(S["s_ready"], 1)
                            v.nop().then_inc(S["wq_free"], 1)

                        def chunks(i):
                            for u in range(2):
                                if later(i):
                                    v.wait_ge(uo_out[u], hb * (32 * NCH) + i * 64)
                                v.wait_ge(yk_in[u], hb * (32 * NCH) + (i * 64 + 64))
                                for s in range(2):
                                    at = slice(64 * s, 64 * s + 64)
                                    v.wait_ge(S["ws_psum"], hb * (2 * NCH) + (i * 4 + (2 * u + s + 1)))
                                    v.tensor_tensor(uo[at, u, :].rearrange("x (b c) -> x b c", b=2), yk[at, u, :, 0:C],
                                                    bank[at, 4 + s, 0:2 * C].rearrange("x (b c) -> x b c", b=2), ALU.subtract).then_inc(S["uo_ready"], 1)
                                v.nop().then_inc(S["wq_free"], 1)
                                for s in range(2):
                                    v.wait_ge(S["s_psum"], hb * (2 * NCH) + (i * 4 + (2 * u + s + 1)))
                                    v.tensor_tensor(s_blk[:, 2 * s:2 * s + 2, :, :], bank[0:CK, 2 * s:2 * s + 2, 0:4 * CK].rearrange("c j (g m) -> c j g m", g=4),
                                                    spread(spread(blocks[:].rearrange("c h d -> c (h d)"), 1, 4), 1, 2), ALU.mult).then_inc(S["s_ready"], 1)
                        repeat(v, NCH // 2, chunks)
                        v.wait_ge(S["uo_in"], hb * 16 + 16)
                        for i in range(K):
                            for f in range(2):
                                hs = slice(f * HC, (f + 1) * HC)
                                cs = slice(f * CK, (f + 1) * CK)
                                pr = tmp[:, 0:HC * D * (i + 1)].rearrange("p (h e j) -> p h e j", h=HC, e=D)
                                step(v.tensor_tensor(pr, spread(kp[:, K + i, hs, 0:i + 1], 2, D),
                                                     uo_sys[:, 0:i + 1, cs].rearrange("p j (h e) -> p h e j", h=HC), ALU.mult))
                                step(v.tensor_reduce(heads_of(red[:, 0, :])[:, hs, :], pr, AX_X, ALU.add))
                            step(v.tensor_tensor(o_sys[:, i, :].rearrange("p (h e) -> p h e", e=D), heads_of(red[:, 0, :]),
                                                 uo_sys[:, K + i, :].rearrange("p (h e) -> p h e", e=D), ALU.subtract))
                        v.nop().then_inc(S["o_ready"], 1)
                        for j in range(HT):
                            v.wait_ge(S["y_psum_d"], hb * HT + (j + 1))
                            tile = hb * HT + j
                            v.tensor_tensor(one(res, tile), one(res, tile), bank[:, 4 + j % 2, 0:C], ALU.add).then_inc(S["y_added"], 1)
                        v.wait_ge(S["y_added"], hb * HT + HT)
                        v.nop().then_inc(S["half_open"], 1)
                        order.end_trip()

        def load_experts(eng, n, w1, w2, b2, done):
            _, up, b_up, down, b_down = moe_args[n]
            for k in range(2):
                eng.dma_start(w1[0:CK, k, :, :], up[:, k * CK:(k + 1) * CK, :].rearrange("e c f -> c e f")).then_inc(done, 16)
            eng.dma_start(w1[CK:CK + 1, 0, :, :], b_up.rearrange("(o e) f -> o e f", o=1)).then_inc(done, 16)
            for k in range(FK):
                eng.dma_start(w2[:, k, :, :], down[:, k * P:(k + 1) * P, :].rearrange("e p d -> p e d")).then_inc(done, 16)
            eng.dma_start(b2[:].rearrange("p e c -> p (e c)"), b_down.rearrange("e d -> (e d)").partition_broadcast(P)).then_inc(done, 16)

        LOADS = 16 * (2 + 1 + FK + 1)

        with ExitStack() as m0:
            w1 = sb("w1_0", [CK + 1, 2, E, FF], ctx=m0)
            w2 = sb("w2_0", [P, FK, E, C], ctx=m0)
            b2 = sb("b2_0", [P, E, C], ctx=m0)
            w_in = sem("w_in0")
            with ExitStack() as a:
                xc = sb("xc", [CK, 2, T], ctx=a)
                xn = sb("xn", [CK, 2, T], ctx=a)
                BLK = 512
                NB = T // BLK
                GRP = 4
                sq = sb("sq", [CK, 2, 2, BLK], ctx=a)
                sd = sb("sd", [CK, 2, BLK], ctx=a)
                w_raw = sb("w_raw", [CK, 2, 2, C], ctx=a)
                w_T = sb("w_T", [CK, 2, 2, C], ctx=a)
                bias = sb("bias", [CK, 2, NG], ctx=a)
                (x_in, bias_in, mean_psum, centred, sq_ready, var_psum, sd_ready, rs_ready, normed, wT_psum, wT_ready,
                 conv_psum, conv_done) = [sem(s) for s in (
                    "x_in", "bias_in", "mean_psum", "centred", "sq_ready", "var_psum", "sd_ready", "rs_ready", "normed",
                    "wT_psum", "wT_ready", "conv_psum", "conv_done")]
                w_raw_in = [sem(f"w_raw_in{u}") for u in range(2)]
                with ExitStack() as s1:
                    ps_mean = ps("ps_mean", [CK, GRP, BLK], ctx=s1)
                    ps_var = ps("ps_var", [CK, GRP, BLK], ctx=s1)
                    with nc.Block() as block:
                        @block.sync
                        def _(sp):
                            for b in range(0, B, 4):
                                for k in range(2):
                                    sp.dma_start(xc[:, k, b * L:(b + 4) * L].rearrange("c (b l) -> c b l", b=4),
                                                 x[b:b + 4, k * CK:(k + 1) * CK, :, :].rearrange("b c h w -> c b (h w)")).then_inc(x_in, 16)
                            with nc.allow_non_contiguous_dma("a small bias"):
                                for k in range(2):
                                    sp.dma_start(bias[:, k, :], conv_b[:, k * CK:(k + 1) * CK].rearrange("g c -> c g")).then_inc(bias_in, 16)

                        @block.scalar
                        def _(act):
                            load_experts(act, 0, w1, w2, b2, w_in)

                            def body(i):
                                for q in range(GRP):
                                    act.wait_ge(centred, i * GRP + (q + 1))
                                    if later(i) or q >= 2:
                                        act.wait_ge(var_psum, i * GRP + (q - 1))
                                    act.activation(sq[:, q % 2, :, :], xn[:, :, bass.ds((i * GRP + q) * BLK, BLK)], ACT.Square).then_inc(sq_ready, 1)
                                    act.wait_ge(var_psum, i * GRP + (q + 1))
                                    if later(i) or q >= 2:
                                        act.wait_ge(normed, i * GRP + (q - 1))
                                    act.activation(sd[:, q % 2, :], ps_var[:, q, :], ACT.Sqrt, bias=eps[1e-6][0:CK, 0:1]).then_inc(sd_ready, 1)
                            repeat(act, NB // GRP, body)

                        @block.tensor
                        def _(pe):
                            pe.wait_ge(x_in, 16 * B // 2)

                            def body(i):
                                for q in range(GRP):
                                    if later(i):
                                        pe.wait_ge(centred, i * GRP + (q - 3))
                                    for k in range(2):
                                        last = pe.matmul(ps_mean[:, q, :], mean_w[:], xc[:, k, bass.ds((i * GRP + q) * BLK, BLK)],
                                                         start=k == 0, stop=k == 1)
                                    last.then_inc(mean_psum, 1)
                                for q in range(GRP):
                                    pe.wait_ge(sq_ready, i * GRP + (q + 1))
                                    for k in range(2):
                                        last = pe.matmul(ps_var[:, q, :], mean_w[:], sq[:, q % 2, k, :], start=k == 0, stop=k == 1)
                                    last.then_inc(var_psum, 1)
                            repeat(pe, NB // GRP, body)

                        @block.vector
                        def _(v):
                            def body(i):
                                for q in range(GRP):
                                    at = bass.ds((i * GRP + q) * BLK, BLK)
                                    v.wait_ge(mean_psum, i * GRP + (q + 1))
                                    v.tensor_tensor(xn[:, :, at], xc[:, :, at], spread(ps_mean[:, q, :], 1, 2), ALU.subtract).then_inc(centred, 1)
                                for q in range(GRP):
                                    at = bass.ds((i * GRP + q) * BLK, BLK)
                                    v.wait_ge(sd_ready, i * GRP + (q + 1))
                                    v.reciprocal(sd[:, q % 2, :], sd[:, q % 2, :]).then_inc(rs_ready, 1)
                                    v.wait_ge(rs_ready, i * GRP + (q + 1))
                                    v.tensor_tensor(xn[:, :, at], xn[:, :, at], spread(sd[:, q % 2, :], 1, 2), ALU.mult).then_inc(normed, 1)
                            v.wait_ge(x_in, 16 * B // 2)
                            repeat(v, NB // GRP, body)

                with ExitStack() as s2:
                    ps_w = ps("ps_w", [CK, 2, 512], ctx=s2)
                    ps_c = ps("ps_c", [CK, 2, 512], ctx=s2)
                    def places(t, k, gh, gw):
                        v = t[:, k, :].rearrange("c (r i w j) -> c r i w j", i=GS, w=W // GS, j=GS)
                        return v[:, :, bass.ds(gh, 1), :, gw].rearrange("c r o w -> c (r o) w")
                    with nc.Block() as block:
                        @block.sync
                        def _(sp):
                            def body(i):
                                for j in range(GS):
                                    u = j % 2
                                    if later(i) or j >= 2:
                                        sp.wait_ge(wT_psum, i * GS + (j - 1))
                                    sp.dma_start(w_raw[:, u, :, :], conv_w[bass.ds(i * GS + j, 1), :, :].rearrange("o (k p) c -> p (o k) c", k=2)).then_inc(w_raw_in[u], 16)
                            repeat(sp, GS, body)

                        @block.tensor
                        def _(pe):
                            def turn(i, j):
                                u = j % 2
                                pe.wait_ge(w_raw_in[u], i * 32 + (16 * (j // 2) + 16))
                                if later(i) or j >= 2:
                                    pe.wait_ge(wT_ready, i * GS + (j - 1))
                                for k in range(2):
                                    for o in range(2):
                                        last = pe.transpose(ps_w[:, u, k * C + o * CK:k * C + (o + 1) * CK],
                                                            w_raw[:, u, o, k * CK:(k + 1) * CK], ident[0:CK, 0:CK])
                                last.then_inc(wT_psum, 1)

                            def body(i):
                                for j in range(GS):
                                    u = j % 2
                                    turn(i, j)
                                    pe.wait_ge(wT_ready, i * GS + (j + 1))
                                    if later(i) or j >= 2:
                                        pe.wait_ge(conv_done, i * (2 * GS) + 2 * (j - 1))
                                    for o in range(2):
                                        for k in range(2):
                                            last = pe.matmul(ps_c[:, u, o * B * 16:(o + 1) * B * 16], w_T[:, u, k, o * CK:(o + 1) * CK],
                                                             places(xn, k, i, j), start=k == 0, stop=k == 1)
                                    last.then_inc(conv_psum, 1)
                            repeat(pe, GS, body)

                        @block.scalar
                        def _(act):
                            def body(i):
                                for j in range(GS):
                                    act.wait_ge(wT_psum, i * GS + (j + 1))
                                    if later(i) or j >= 2:
                                        act.wait_ge(conv_psum, i * GS + (j - 1))
                                    act.activation(w_T[:, j % 2, :, :], ps_w[:, j % 2, 0:2 * C].rearrange("c (k o) -> c k o", k=2), ACT.Copy).then_inc(wT_ready, 1)
                            repeat(act, GS, body)

                        @block.vector
                        def _(v):
                            v.wait_ge(bias_in, 32)

                            def body(i):
                                for j in range(GS):
                                    v.wait_ge(conv_psum, i * GS + (j + 1))
                                    for o in range(2):
                                        v.scalar_tensor_tensor(
                                            places(xc, o, i, j), ps_c[:, j % 2, o * B * 16:(o + 1) * B * 16].rearrange("c (r w) -> c r w", w=W // GS),
                                            bias[:, o, bass.ds(i * GS + j, 1)], places(xc, o, i, j), ALU.add, ALU.add).then_inc(conv_done, 1)
                            repeat(v, GS, body)

                with ExitStack() as s3:
                    ps_t = ps("ps_t", [P, 4, 512], ctx=s3)
                    turned, copied = sem("turned"), sem("copied")
                    with nc.Block() as block:
                        @block.tensor
                        def _(pe):
                            for t in range(NT):
                                if t >= 4:
                                    pe.wait_ge(copied, t - 3)
                                for k in range(2):
                                    last = pe.transpose(ps_t[:, t % 4, k * CK:(k + 1) * CK], xc[:, k, t * P:(t + 1) * P], ident[0:CK, 0:CK])
                                last.then_inc(turned, 1)

                        @block.vector
                        def _(v):
                            for t in range(NT):
                                v.wait_ge(turned, t + 1)
                                v.tensor_copy(res[:, t, :], ps_t[:, t % 4, 0:C]).then_inc(copied, 1)

            moe(0, ACT.Gelu, w1, w2, b2, w_in, LOADS, m0)

        with ExitStack() as d:
            delta(d)
        with ExitStack() as m1:
            w1 = sb("w1_1", [CK + 1, 2, E, FF], ctx=m1)
            w2 = sb("w2_1", [P, FK, E, C], ctx=m1)
            b2 = sb("b2_1", [P, E, C], ctx=m1)
            w_in = sem("w_in1")
            with nc.Block() as block:
                @block.scalar
                def _(act):
                    load_experts(act, 1, w1, w2, b2, w_in)
            moe(1, ACT.Relu, w1, w2, b2, w_in, LOADS, m1)

        with ExitStack() as o:
            oc = sb("oc", [CK, 2, 2, L], ctx=o)
            ps_o = ps("ps_o", [CK, 2, 2, L], ctx=o)
            o_turned, o_copied = sem("o_turned"), sem("o_copied")
            o_out = [sem(f"o_out{u}") for u in range(2)]
            with nc.Block() as block:
                @block.tensor
                def _(pe):
                    for b in range(B):
                        if b >= 2:
                            pe.wait_ge(o_copied, b - 1)
                        for k in range(2):
                            for s in range(2):
                                last = pe.transpose(ps_o[:, b % 2, k, s * P:(s + 1) * P], res[:, 2 * b + s, k * CK:(k + 1) * CK], ident[:])
                        last.then_inc(o_turned, 1)

                @block.vector
                def _(v):
                    for b in range(B):
                        v.wait_ge(o_turned, b + 1)
                        if b >= 2:
                            v.wait_ge(o_out[b % 2], 32 * (b // 2))
                        v.tensor_copy(oc[:, b % 2, :, :], ps_o[:, b % 2, :, :]).then_inc(o_copied, 1)

                @block.sync
                def _(sp):
                    for b in range(B):
                        sp.wait_ge(o_copied, b + 1)
                        for k in range(2):
                            sp.dma_start(out[b, k * CK:(k + 1) * CK, :, :].rearrange("c h w -> c (h w)"), oc[:, b % 2, k, :]).then_inc(o_out[b % 2], 16)
                    for u in range(2):
                        sp.wait_ge(o_out[u], 32 * (B // 2))


_INS = ['x', 'L0_conv_Wg', 'L0_conv_bg', 'L0_ffn_gate_w', 'L0_ffn_w_up', 'L0_ffn_b_up', 'L0_ffn_w_down', 'L0_ffn_b_down',
        'L1_conv_Wq', 'L1_conv_Wk', 'L1_conv_Wv', 'L1_conv_Wb', 'L1_conv_Wo', 'L1_ffn_Wg', 'L1_ffn_W1', 'L1_ffn_b1',
        'L1_ffn_W2', 'L1_ffn_b2']
_OUTS = [((16, 192, 16, 16), 'float32')]


def kernel(**inputs):
    import numpy as _np
    import concourse.bacc as _bacc
    from concourse import mybir as _mybir
    from concourse.bass_utils import run_bass_kernel_spmd as _run

    nc = _bacc.Bacc("TRN2", target_bir_lowering=False, num_devices=1)
    arrays, aps = {}, {}
    for name in _INS:
        a = _np.ascontiguousarray(inputs[name])
        arrays[f"in_{name}_dram"] = a
        aps[name] = nc.dram_tensor(f"in_{name}_dram", a.shape, _mybir.dt.from_np(a.dtype), kind="ExternalInput").ap()
    (shape, dtype), = _OUTS
    out = nc.dram_tensor("out_0_dram", shape, _mybir.dt.from_np(_np.dtype(dtype)), kind="ExternalOutput").ap()
    metaformer(nc, aps['x'], aps['L0_conv_Wg'], aps['L0_conv_bg'],
               [[aps[n] for n in _INS[3:8]], [aps[n] for n in _INS[13:18]]],
               [aps[n] for n in _INS[8:13]], out)
    r = _run(nc, [arrays], core_ids=[0])
    return r.results[0]["out_0_dram"]
```

```python
from contextlib import ExitStack

import concourse.bass as bass
from concourse import mybir

F32 = mybir.dt.float32
F32R = mybir.dt.float32r
I32 = mybir.dt.int32
U32 = mybir.dt.uint32
ALU = mybir.AluOpType
ACT = mybir.ActivationFunctionType
AX_X = mybir.AxisListType.X

P = 128


def spread(ap, axis, n):
    wide = ap.unsqueeze(axis)
    shape = list(wide.shape)
    shape[axis] = n
    return wide.broadcast_to(shape)


def repeat(eng, trips, body):
    body(0)
    if trips > 1:
        with eng.Fori(1, trips) as i:
            body(i)


def repeat_to_last(eng, trips, body):
    body(0, True, trips == 1)
    if trips > 2:
        with eng.Fori(1, trips - 1) as i:
            body(i, False, False)
    if trips > 1:
        body(trips - 1, False, True)


def one(t, i):
    return t[:, bass.ds(i, 1), :].rearrange("p o c -> p (o c)")


def later(i):
    return not isinstance(i, int)


class Order:

    def __init__(self, eng, sem):
        self.eng, self.sem, self.base, self.k, self.it, self.per = eng, sem, 0, 0, 0, 0

    def mark(self, ins):
        ins.then_inc(self.sem, 1)
        self.k += 1
        return ins

    def wait(self):
        self.eng.wait_ge(self.sem, self.it * self.per + (self.base + self.k))

    def trip(self, i, per):
        self.it, self.per, self.k = i, per, 0

    def end_trip(self):
        assert self.k == self.per, f"the body leaves {self.k} marks"

    def leave(self, trips):
        self.base, self.k, self.it, self.per = self.base + self.per * trips, 0, 0, 0


def metaformer(nc, x, conv_w, conv_b, moe_args, delta_args, out):
    B, C, H, W = x.shape
    L = H * W
    T = B * L
    NT = T // P
    CK = C // 2
    NG = conv_w.shape[0]
    GS = 4
    E = moe_args[0][0].shape[1]
    FF = moe_args[0][1].shape[2]
    FK = FF // P
    FH = FF // 2
    SLOT_TILES = 2 * NT + E
    REGION = T + P
    AHEAD = 2
    LISTED = SLOT_TILES + AHEAD

    with ExitStack() as top:
        def sb(name, shape, dt=F32, ctx=top):
            return ctx.enter_context(nc.sbuf_tensor(name, shape, dt))

        def ps(name, shape, dt=F32, ctx=top):
            return ctx.enter_context(nc.psum_tensor(name, shape, dt))

        def sem(name):
            return top.enter_context(nc.semaphore(name))

        def dram(name, shape, dt=F32):
            return nc.dram_tensor(name, shape, dt, kind="Internal").ap()

        expert_rows = dram("expert_rows", [E * REGION, C])
        slot_out = dram("slot_out", [SLOT_TILES * P, C])

        res = sb("res", [P, NT, C])
        ident = sb("ident", [P, P])
        ones = sb("ones", [P, P])
        before = sb("before", [P, P])
        mean_w = sb("mean_w", [CK, CK])
        zeros = sb("zeros", [P, C])
        expert_no = sb("expert_no", [P, E])
        tile_no = sb("tile_no", [P, LISTED])
        lane_no = sb("lane_no", [P, 1])
        eps = {e: sb(f"eps{n}", [P, 1]) for n, e in enumerate((1e-5, 1e-6))}
        mu_var = sb("mu_var", [P, NT, 2])
        rstd = sb("rstd", [P, NT])
        bn = sb("bn", [P, GS, 6])
        aggr = sb("aggr", [P, GS, 2])
        fence = sb("fence", [P, 1])

        const_pool = sem("const_pool")
        with ExitStack() as c, nc.Block() as block:
            iota_i = sb("iota_i", [P, P], I32, c)

            @block.gpsimd
            def _(pool):
                order = Order(pool, const_pool)
                order.mark(pool.memset(ident[:], 0.0))
                order.mark(pool.memset(before[:], 1.0))
                order.mark(pool.memset(ones[:], 1.0))
                order.mark(pool.memset(zeros[:], 0.0))
                order.mark(pool.memset(mean_w[:], 1.0 / C))
                for e, t in eps.items():
                    order.mark(pool.memset(t[:], e))
                order.wait()
                order.mark(pool.affine_select(out=ident[:], in_=ident[:], compare_op=ALU.not_equal, fill=1.0,
                                              base=0, pattern=[[-1, P]], channel_multiplier=1))
                order.mark(pool.affine_select(out=before[:], in_=before[:], compare_op=ALU.is_gt, fill=0.0,
                                              base=0, pattern=[[1, P]], channel_multiplier=-1))
                for dst, n, step, mult in ((expert_no, E, 1, 0), (tile_no, LISTED, 1, 0), (lane_no, 1, 0, 1)):
                    order.mark(pool.iota(iota_i[:, 0:n], pattern=[[step, n]], base=0, channel_multiplier=mult))
                    order.wait()
                    order.mark(pool.tensor_copy(dst[:], iota_i[:, 0:n]))
                    order.wait()

        STATS_MARKS = 2 * GS + 1
        dve = sem("dve")
        stats_ready, std_ready = sem("stats_ready"), sem("std_ready")
        dve_marked = [0]
        deviations = [0, 0]

        def dve_order(v):
            order = Order(v, dve)
            order.base = dve_marked[0]
            return order

        def dve_leaves(order):
            dve_marked[0] = order.base + order.k

        def group_stats(v, order, i):
            v.nop(nofuse=True)
            for u in range(GS):
                order.mark(v.bn_stats(bn[:, u, :], one(res, i * GS + u)))
            order.wait()
            v.tensor_copy(fence[:], lane_no[:])
            for u in range(GS):
                order.mark(v.bn_aggr(aggr[:, u, :], bn[:, u, :]))
            order.wait()
            order.mark(v.tensor_copy(mu_var[:, bass.ds(i * GS, GS), :], aggr[:]))

        def deviations_act(act, e):
            deviations[0] += 1
            act.wait_ge(stats_ready, deviations[0])
            act.activation(rstd[:], mu_var[:, :, 1], ACT.Sqrt, bias=eps[e][:, 0:1]).then_inc(std_ready, 1)

        def deviations_dve(v, order):
            deviations[1] += 1
            order.wait()
            v.nop().then_inc(stats_ready, 1)
            v.wait_ge(std_ready, deviations[1])
            v.reciprocal(rstd[:], rstd[:])

        def moe(n, act_fn, w1, w2, b2, w_sem, w_full, ctx, load, next_eps):
            gate_w = moe_args[n][0]
            nm = lambda s: f"{s}{n}"
            gate = sb(nm("gate"), [CK, 2, E], ctx=ctx)
            logits = sb(nm("logits"), [P, NT, E], ctx=ctx)
            best = sb(nm("best"), [P, NT, 1], ctx=ctx)
            pick = sb(nm("pick"), [P, NT, 2, E], ctx=ctx)
            rank = sb(nm("rank"), [P, NT, 2], ctx=ctx)
            prob = sb(nm("prob"), [P, NT, 2], ctx=ctx)
            slot = sb(nm("slot"), [P, NT, 2], U32, ctx=ctx)
            listed = sb(nm("listed"), [P, 2, LISTED], U32, ctx=ctx)

            Q = 4
            RING = 4
            with ExitStack() as rc:
                xn = sb(nm("xn"), [P, RING, Q, C], ctx=rc)
                xnT = sb(nm("xnT"), [CK, 2, Q, P], ctx=rc)
                lg = sb(nm("lg"), [P, Q, E], ctx=rc)
                top8 = sb(nm("top8"), [P, Q, 8], ctx=rc)
                idx = sb(nm("idx"), [P, Q, 8], U32, ctx=rc)
                idf = sb(nm("idf"), [P, Q, 2], ctx=rc)
                taken = sb(nm("taken"), [P, Q, E], ctx=rc)
                carry = sb(nm("carry"), [P, Q + 1, E], ctx=rc)
                place = sb(nm("place"), [P, Q, E], ctx=rc)
                mine = sb(nm("mine"), [P, Q, 2, E], ctx=rc)
                rowf = sb(nm("rowf"), [P, Q, 2], ctx=rc)
                row = sb(nm("row"), [P, RING, Q, 2], U32, ctx=rc)
                total = sb(nm("total"), [P, E], ctx=rc)
                padf = sb(nm("padf"), [P, E], ctx=rc)
                pad = sb(nm("pad"), [P, E], U32, ctx=rc)
                tilesi = sb(nm("tilesi"), [P, E], I32, ctx=rc)
                tiles = sb(nm("tiles"), [P, E], ctx=rc)
                upto = sb(nm("upto"), [P, E], ctx=rc)
                base = sb(nm("base"), [P, E], ctx=rc)
                wide = sb(nm("wide"), [P, NT * 2, E], ctx=rc)
                past = sb(nm("past"), [P, LISTED, E], ctx=rc)
                skipped = sb(nm("skipped"), [P, LISTED, E], ctx=rc)
                lf = sb(nm("lf"), [P, 4, LISTED], ctx=rc)
                ex = sb(nm("ex"), [P, NT, E], ctx=rc)
                den = sb(nm("den"), [P, NT], ctx=rc)
                psT = ps(nm("psT"), [CK, 2, Q, P], ctx=rc)
                psL = ps(nm("psL"), [P, 2, 512], ctx=rc)
                psR = ps(nm("psR"), [P, 512], ctx=rc)
                (gate_in, xn_ready, xnT_psum, xnT_ready, logits_psum, taken_ready, rank_psum, row_ready,
                 carry_ready, total_psum, pad_ready, padded, exp_in, exp_done) = [sem(nm(s)) for s in (
                    "gate_in", "xn_ready", "xnT_psum", "xnT_ready", "logits_psum", "taken_ready", "rank_psum",
                    "row_ready", "carry_ready", "total_psum", "pad_ready", "padded", "exp_in", "exp_done")]
                scattered = [sem(nm(f"scattered{u}_")) for u in range(RING)]
                TRIPS = NT // (RING * Q)
                with nc.Block() as block:
                    @block.sync
                    def _(sp):
                        sp.dma_start(gate[:], gate_w.rearrange("(k c) e -> c k e", k=2)).then_inc(gate_in, 16)

                    @block.tensor
                    def _(pe):
                        pe.wait_ge(gate_in, 16)

                        def score(g, u):
                            pe.wait_ge(xn_ready, g * Q + Q)
                            for q in range(Q):
                                for k in range(2):
                                    last = pe.transpose(psT[:, k, q, :], xn[:, u, q, k * CK:(k + 1) * CK], ident[:])
                            last.then_inc(xnT_psum, 1)
                            pe.wait_ge(xnT_ready, g + 1)
                            for q in range(Q):
                                for k in range(2):
                                    last = pe.matmul(psL[:, u % 2, q * E:(q + 1) * E], xnT[:, k, q, :], gate[:, k, :],
                                                     start=k == 0, stop=k == 1)
                            last.then_inc(logits_psum, 1)

                        def body(i, first, last):
                            for u in range(RING):
                                g = i * RING + u
                                if not (last and u == RING - 1):
                                    score(i * RING + (u + 1), (u + 1) % RING)
                                pe.wait_ge(carry_ready, i * RING + (u + 1))
                                pe.matmul(psR[:, 0:Q * E], before[:], taken[:].rearrange("p q e -> p (q e)"),
                                          start=True, stop=False)
                                pe.matmul(psR[:, 0:Q * E], ones[:], carry[:, 0:Q, :].rearrange("p q e -> p (q e)"),
                                          start=False, stop=True).then_inc(rank_psum, 1)
                        score(0, 0)
                        repeat_to_last(pe, TRIPS, body)
                        pe.wait_ge(row_ready, RING * TRIPS)
                        pe.matmul(psR[:, 0:E], ones[:], carry[:, Q, :], start=True, stop=True).then_inc(total_psum, 1)

                    @block.scalar
                    def _(act):
                        if load:
                            load(act)

                        def body(i):
                            for u in range(RING):
                                act.wait_ge(xnT_psum, i * RING + (u + 1))
                                act.activation(xnT[:], psT[:], ACT.Copy).then_inc(xnT_ready, 1)
                        repeat(act, TRIPS, body)
                        act.wait_ge(exp_in, 1)
                        act.activation(ex[:], ex[:], ACT.Exp).then_inc(exp_done, 1)

                    @block.gpsimd
                    def _(pool):
                        def body(i):
                            for u in range(RING):
                                pool.wait_ge(row_ready, i * RING + (u + 1))
                                pool.nop(nofuse=True)
                                for q in range(Q):
                                    for k in range(2):
                                        pool.indirect_dma_start(
                                            expert_rows, bass.IndirectOffsetOnAxis(row[:, u, q, k:k + 1], 0),
                                            xn[:, u, q, :], None).then_inc(scattered[u], 16)
                        repeat(pool, TRIPS, body)
                        pool.wait_ge(pad_ready, 1)
                        for e in range(E):
                            pool.indirect_dma_start(expert_rows, bass.IndirectOffsetOnAxis(pad[:, e:e + 1], 0),
                                                    zeros[:], None).then_inc(padded, 16)
                        for u in range(RING):
                            pool.wait_ge(scattered[u], TRIPS * Q * 2 * 16)
                        pool.wait_ge(padded, E * 16)

                    @block.vector
                    def _(v):
                        order = dve_order(v)
                        order.mark(v.memset(carry[:], 0.0))
                        order.base += 1
                        order.leave(0)

                        def normalise(i, u, first):
                            at_ring, trip = u % RING, i + u // RING
                            if u == RING or not first:
                                v.wait_ge(scattered[at_ring], trip * (Q * 2 * 16))
                            for q in range(Q):
                                tile = i * (RING * Q) + (u * Q + q)
                                at = bass.ds(tile, 1)
                                v.tensor_scalar(xn[:, at_ring, q, :], one(res, tile), mu_var[:, at, 0], rstd[:, at],
                                                ALU.subtract, ALU.mult).then_inc(xn_ready, 1)

                        def body(i, first, last):
                            order.trip(i, RING * (3 * Q + 11))
                            for u in range(RING):
                                g = i * RING + u
                                if not (last and u == RING - 1):
                                    normalise(i, u + 1, first)
                                group = bass.ds(g * Q, Q)
                                v.wait_ge(logits_psum, g + 1)
                                order.mark(v.tensor_copy(lg[:], psL[:, u % 2, 0:Q * E].rearrange("p (q e) -> p q e", q=Q)))
                                order.wait()
                                order.mark(v.tensor_copy(logits[:, group, :], lg[:]))
                                for q in range(Q):
                                    order.mark(v.max(top8[:, q, :], lg[:, q, :]))
                                order.wait()
                                order.mark(v.tensor_copy(best[:, group, :], top8[:, :, 0:1]))
                                for q in range(Q):
                                    order.mark(v.max_index(idx[:, q, :], top8[:, q, :], lg[:, q, :]))
                                order.wait()
                                order.mark(v.tensor_copy(idf[:], idx[:, :, 0:2]))
                                order.wait()
                                chosen = pick[:, group, :, :]
                                order.mark(v.tensor_tensor(
                                    chosen.rearrange("p q k e -> p (q k) e"), spread(expert_no[:], 1, 2 * Q),
                                    spread(idf[:].rearrange("p q k -> p (q k)"), 2, E), ALU.is_equal))
                                order.wait()
                                if not first or u:
                                    v.wait_ge(rank_psum, g)
                                order.mark(v.tensor_tensor(taken[:], pick[:, group, 0, :], pick[:, group, 1, :], ALU.add))
                                order.mark(v.tensor_copy(carry[:, 0, :], carry[:, Q, :]))
                                order.wait()
                                for q in range(Q):
                                    order.mark(v.tensor_tensor(carry[:, q + 1, :], carry[:, q, :], taken[:, q, :], ALU.add))
                                    order.wait()
                                v.nop().then_inc(carry_ready, 1)
                                v.wait_ge(rank_psum, g + 1)
                                order.mark(v.tensor_copy(place[:], psR[:, 0:Q * E].rearrange("p (q e) -> p q e", q=Q)))
                                order.wait()
                                order.mark(v.tensor_tensor(mine[:], spread(place[:], 2, 2), chosen, ALU.mult))
                                order.wait()
                                order.mark(v.tensor_reduce(rank[:, group, :], mine[:], AX_X, ALU.add))
                                order.wait()
                                order.mark(v.scalar_tensor_tensor(rowf[:], idf[:], float(REGION), rank[:, group, :],
                                                                  ALU.mult, ALU.add))
                                order.wait()
                                v.tensor_copy(row[:, u, :, :], rowf[:]).then_inc(row_ready, 1)
                            order.end_trip()
                        normalise(0, 0, True)
                        repeat_to_last(v, TRIPS, body)
                        order.leave(TRIPS)

                        def step(ins):
                            order.mark(ins)
                            order.wait()
                        v.tensor_tensor(ex[:], logits[:], best[:].broadcast_to([P, NT, E]),
                                        ALU.subtract).then_inc(exp_in, 1)
                        v.wait_ge(total_psum, 1)
                        step(v.tensor_copy(total[:], psR[:, 0:E]))
                        step(v.scalar_tensor_tensor(padf[:], expert_no[:], float(REGION), total[:], ALU.mult, ALU.add))
                        step(v.tensor_scalar(padf[:], padf[:], lane_no[:, 0:1], None, ALU.add))
                        v.tensor_copy(pad[:], padf[:]).then_inc(pad_ready, 1)
                        step(v.tensor_scalar(tiles[:], total[:], float(P - 1), None, ALU.add))
                        step(v.tensor_copy(tilesi[:], tiles[:]))
                        step(v.tensor_scalar(tilesi[:], tilesi[:], P.bit_length() - 1, None, ALU.arith_shift_right))
                        step(v.tensor_copy(tiles[:], tilesi[:]))
                        step(v.tensor_tensor_scan(upto[:], ones[:, 0:E], tiles[:], 0.0, ALU.mult, ALU.add))
                        step(v.tensor_tensor(base[:], upto[:], tiles[:], ALU.subtract))
                        step(v.tensor_scalar(base[:], base[:], float(P), None, ALU.mult))
                        step(v.tensor_tensor(wide[:], pick[:].rearrange("p t k e -> p (t k) e"), spread(base[:], 1, 2 * NT), ALU.mult))
                        step(v.tensor_reduce(prob[:].rearrange("p t k -> p (t k)"), wide[:], AX_X, ALU.add))
                        step(v.tensor_tensor(rank[:], rank[:], prob[:], ALU.add))
                        step(v.tensor_copy(slot[:], rank[:]))
                        step(v.tensor_tensor(past[:], spread(tile_no[:], 2, E), spread(upto[:], 1, LISTED), ALU.is_ge))
                        step(v.tensor_reduce(lf[:, 0, :], past[:], AX_X, ALU.add))
                        step(v.tensor_tensor(skipped[:], past[:], spread(tiles[:], 1, LISTED), ALU.mult))
                        step(v.tensor_reduce(lf[:, 1, :], skipped[:], AX_X, ALU.add))
                        step(v.tensor_tensor(lf[:, 1, :], tile_no[:], lf[:, 1, :], ALU.subtract))
                        step(v.tensor_scalar(lf[:, 2, :], lf[:, 0, :], float(REGION // P), None, ALU.mult))
                        step(v.tensor_tensor(lf[:, 1, :], lf[:, 1, :], lf[:, 2, :], ALU.add))
                        step(v.tensor_scalar(lf[:, 3, :], lf[:, 0, :], float(E), None, ALU.is_lt))
                        step(v.tensor_tensor(lf[:, 0, :], lf[:, 0, :], lf[:, 3, :], ALU.mult))
                        step(v.tensor_tensor(lf[:, 1, :], lf[:, 1, :], lf[:, 3, :], ALU.mult))
                        step(v.tensor_copy(listed[:], lf[:, 0:2, :]))
                        v.wait_ge(exp_done, 1)
                        step(v.tensor_reduce(den[:], ex[:], AX_X, ALU.add))
                        step(v.reciprocal(den[:], den[:]))
                        step(v.tensor_tensor(wide[:].rearrange("p (t k) e -> p t k e", k=2), pick[:], spread(ex[:], 2, 2), ALU.mult))
                        step(v.tensor_reduce(prob[:].rearrange("p t k -> p (t k)"), wide[:], AX_X, ALU.add))
                        step(v.tensor_tensor(prob[:], prob[:], spread(den[:], 2, 2), ALU.mult))
                        dve_leaves(order)

            with ExitStack() as tc:
                xt = sb(nm("xt"), [P, 2, C], ctx=tc)
                xT_hi = sb(nm("xT_hi"), [CK + 1, 2, 2, P], F32R, ctx=tc)
                xT_lo = sb(nm("xT_lo"), [CK, 2, 2, P], F32R, ctx=tc)
                w1_hi = sb(nm("w1_hi"), [CK + 1, 2, E, FF], F32R, ctx=tc)
                h = sb(nm("h"), [P, 2, FF], ctx=tc)
                hT = sb(nm("hT"), [P, 2, FK, P], ctx=tc)
                y = sb(nm("y"), [P, 2, C], ctx=tc)
                psX = ps(nm("psX"), [CK, 2, P], ctx=tc)
                psU = ps(nm("psU"), [P, 2, 512], ctx=tc)
                psH = ps(nm("psH"), [P, 2, 512], ctx=tc)
                psY = ps(nm("psY"), [P, 512], ctx=tc)
                (x_lo_ready, split, xT_psum, xT_ready, up_psum, h_ready, hT_psum, hT_ready, y_psum, y_ready, ones_set) = [
                    sem(nm(s)) for s in ("x_lo_ready", "split", "xT_psum", "xT_ready", "up_psum", "h_ready", "hT_psum", "hT_ready", "y_psum",
                                         "y_ready", "ones_set")]
                x_in = [sem(nm(f"x_in{u}_")) for u in range(2)]
                y_out = [sem(nm(f"y_out{u}_")) for u in range(2)]
                TRIPS = SLOT_TILES // 2
                rows_of_tiles = expert_rows.rearrange("(t p) c -> t p c", p=P)
                out_tiles = slot_out.rearrange("(t p) c -> t p c", p=P)

                def split_weights(eng, e):
                    for k in range(2):
                        n_k = CK + 1 - k
                        eng.tensor_copy(w1_hi[0:n_k, k, e, :], w1[0:n_k, k, e, :]).then_inc(split, 1)
                        eng.wait_ge(split, 4 * e + 2 * k + 1)
                        eng.tensor_tensor(w1[0:n_k, k, e, :].bitcast(F32R), w1[0:n_k, k, e, :],
                                          w1_hi[0:n_k, k, e, :].bitcast(F32), ALU.subtract).then_inc(split, 1)

                with nc.Block() as block:
                    @block.sync
                    def _(sp):
                        def load(tile, u):
                            r = sp.value_load(listed[0:1, 1, bass.ds(tile, 1)], min_val=0, max_val=E * REGION // P - 1)
                            sp.dma_start(xt[:, u, :], rows_of_tiles[bass.ds(r, 1), :, :].rearrange("t p c -> (t p) c")).then_inc(x_in[u], 16)
                        for u in range(2):
                            load(u, u)

                        def store(tile, u):
                            sp.wait_ge(y_ready, tile + 1)
                            sp.nop(nofuse=True)
                            sp.dma_start(out_tiles[bass.ds(tile, 1), :, :].rearrange("t p c -> (t p) c"), y[:, u, :]).then_inc(y_out[u], 16)

                        def body(i):
                            for u in range(2):
                                sp.wait_ge(xT_psum, i * 2 + (u + 1))
                                load(i * 2 + (u + 2), u)
                                if later(i) or u:
                                    store(i * 2 + (u - 1), 1 - u)
                        repeat(sp, TRIPS, body)
                        store(SLOT_TILES - 1, 1)
                        for u in range(2):
                            sp.wait_ge(x_in[u], 16 * (TRIPS + 1))
                            sp.wait_ge(y_out[u], 16 * TRIPS)

                    @block.tensor
                    def _(pe):
                        pe.wait_ge(w_sem, w_full)
                        pe.wait_ge(ones_set, 1)

                        def turn_x(tile, u, trip):
                            pe.wait_ge(x_in[u], trip * 16 + 16)
                            for k in range(2):
                                last = pe.transpose(psX[:, k, :], xt[:, u, k * CK:(k + 1) * CK], ident[:])
                            last.then_inc(xT_psum, 1)

                        def expert(tile):
                            return pe.value_load(listed[0:1, 0, bass.ds(tile, 1)], min_val=0, max_val=E - 1)

                        def up(tile, u, e, first=False):
                            pe.wait_ge(x_lo_ready, tile + 1)
                            pe.wait_ge(split, e * 4 + 4)
                            if not first:
                                pe.wait_ge(h_ready, tile)
                            for f in range(2):
                                cols = slice(f * FH, (f + 1) * FH)
                                for k in range(2):
                                    n_k = CK + 1 - k
                                    pe.matmul(psU[:, f, 0:FH], xT_hi[0:n_k, u, k, :], w1_hi[0:n_k, k, bass.ds(e, 1), cols],
                                              start=k == 0, stop=False)
                                    pe.matmul(psU[:, f, 0:FH], xT_hi[0:n_k, u, k, :], w1[0:n_k, k, bass.ds(e, 1), cols].bitcast(F32R),
                                              start=False, stop=False)
                                    last = pe.matmul(psU[:, f, 0:FH], xT_lo[0:CK, u, k, :], w1_hi[0:CK, k, bass.ds(e, 1), cols],
                                                     start=False, stop=k == 1)
                            last.then_inc(up_psum, 1)

                        turn_x(0, 0, 0)
                        pe.wait_ge(x_lo_ready, 1)
                        turn_x(1, 1, 0)
                        up(0, 0, expert(0), first=True)

                        def body(i):
                            for u in range(2):
                                tile = i * 2 + u
                                e_next, e = expert(tile + 1), expert(tile)
                                pe.wait_ge(h_ready, tile + 1)
                                if later(i) or u:
                                    pe.wait_ge(hT_ready, tile)
                                for k in range(FK):
                                    last = pe.transpose(psH[:, k // 3, (k % 3) * P:(k % 3 + 1) * P],
                                                        h[:, u, k * P:(k + 1) * P], ident[:])
                                last.then_inc(hT_psum, 1)
                                pe.wait_ge(x_lo_ready, tile + 2)
                                turn_x(tile + 2, u, i + 1)
                                up(tile + 1, 1 - u, e_next)
                                pe.wait_ge(hT_ready, tile + 1)
                                if later(i) or u:
                                    pe.wait_ge(y_ready, tile)
                                for k in range(FK):
                                    last = pe.matmul(psY[:, 0:C], hT[:, u, k, :], w2[:, k, bass.ds(e, 1), :],
                                                     start=k == 0, stop=k == FK - 1)
                                last.then_inc(y_psum, 1)
                        repeat(pe, TRIPS, body)

                    @block.scalar
                    def _(act):
                        def turn(tile, u):
                            act.wait_ge(xT_psum, tile + 1)
                            act.activation(xT_hi[0:CK, u, :, :], psX[:], ACT.Copy).then_inc(xT_ready, 1)

                        def hidden(tile, u):
                            act.wait_ge(up_psum, tile + 1)
                            act.activation(h[:, u, :].rearrange("p (f m) -> p f m", f=2), psU[:, :, 0:FH], act_fn).then_inc(h_ready, 1)
                        turn(0, 0)
                        turn(1, 1)
                        hidden(0, 0)

                        def body(i):
                            for u in range(2):
                                act.wait_ge(up_psum, i * 2 + (u + 1))
                                turn(i * 2 + (u + 2), u)
                                hidden(i * 2 + (u + 1), 1 - u)
                        repeat(act, TRIPS, body)

                    @block.vector
                    def _(v):
                        v.tensor_copy(xT_hi[CK:CK + 1, :, 0, :], spread(ones[CK:CK + 1, :], 1, 2)).then_inc(ones_set, 1)

                        def x_rest(tile, u):
                            v.wait_ge(xT_ready, tile + 1)
                            v.tensor_tensor(xT_lo[:, u, :, :], psX[:], xT_hi[0:CK, u, :, :].bitcast(F32), ALU.subtract).then_inc(x_lo_ready, 1)
                        v.wait_ge(w_sem, w_full)
                        split_weights(v, 0)
                        x_rest(0, 0)
                        x_rest(1, 1)

                        def body(i):
                            for u in range(2):
                                tile = i * 2 + u
                                v.wait_ge(hT_psum, tile + 1)
                                v.tensor_copy(hT[:, u, :, :].rearrange("p (a b) t -> p a (b t)", a=2),
                                              psH[:, :, 0:FH]).then_inc(hT_ready, 1)
                                x_rest(tile + 2, u)
                                e = v.value_load(listed[0:1, 0, bass.ds(tile, 1)], min_val=0, max_val=E - 1)
                                v.wait_ge(y_psum, tile + 1)
                                if later(i):
                                    v.wait_ge(y_out[u], i * 16)
                                v.tensor_tensor(y[:, u, :], psY[:, 0:C], b2[:, bass.ds(e, 1), :].rearrange("p o c -> p (o c)"), ALU.add).then_inc(y_ready, 1)
                        repeat(v, TRIPS, body)

                    @block.gpsimd
                    def _(pool):
                        pool.wait_ge(split, 4)
                        for e in range(1, E):
                            split_weights(pool, e)

            with ExitStack() as gc:
                got = sb(nm("got"), [P, 4, 2, C], ctx=gc)
                at_idx = sb(nm("at_idx"), [P, 4, 2], U32, ctx=gc)
                gathered = [sem(nm(f"gathered{u}_")) for u in range(4)]
                added, idx_set = sem(nm("added")), sem(nm("idx_set"))
                oc = sb(nm("oc"), [CK, 2, 2, L], ctx=gc)
                ps_o = ps(nm("ps_o"), [CK, 2, 2, L], ctx=gc)
                if not next_eps:
                    o_turned, o_copied = sem("o_turned"), sem("o_copied")
                    o_out = [sem(f"o_out{u}") for u in range(2)]
                TRIPS = NT // 4
                with nc.Block() as block:
                    @block.gpsimd
                    def _(pool):
                        def body(i):
                            for u in range(4):
                                pool.wait_ge(idx_set, i * 4 + (u + 1))
                                pool.nop(nofuse=True)
                                for k in range(2):
                                    pool.indirect_dma_start(got[:, u, k, :], None, slot_out,
                                                            bass.IndirectOffsetOnAxis(at_idx[:, u, k:k + 1], 0)).then_inc(gathered[u], 16)
                        repeat(pool, TRIPS, body)

                    @block.vector
                    def _(v):
                        order = dve_order(v)
                        for u in range(4):
                            v.tensor_copy(at_idx[:, u, :], slot[:, u, :]).then_inc(idx_set, 1)

                        def body(i, first, last):
                            order.trip(i, GS + (STATS_MARKS if next_eps else 0))
                            for u in range(4):
                                at = bass.ds(i * 4 + u, 1)
                                v.wait_ge(gathered[u], i * 32 + 32)
                                order.mark(v.scalar_tensor_tensor(one(res, i * 4 + u), got[:, u, 0, :], prob[:, at, 0], one(res, i * 4 + u),
                                                                  ALU.mult, ALU.add))
                                order.wait()
                                v.scalar_tensor_tensor(one(res, i * 4 + u), got[:, u, 1, :], prob[:, at, 1], one(res, i * 4 + u),
                                                       ALU.mult, ALU.add).then_inc(added, 1)
                                if not last:
                                    v.wait_ge(added, i * 4 + (u + 1))
                                    v.tensor_copy(at_idx[:, u, :], one(slot, i * 4 + (u + 4))).then_inc(idx_set, 1)
                            if next_eps:
                                if not first:
                                    order.wait()
                                if last:
                                    v.wait_ge(added, i * 4 + 4)
                                group_stats(v, order, i)
                        repeat_to_last(v, TRIPS, body)
                        order.leave(TRIPS)
                        if next_eps:
                            deviations_dve(v, order)
                            dve_leaves(order)

                    if next_eps:
                        @block.scalar
                        def _(act):
                            deviations_act(act, next_eps)
                    else:
                        @block.tensor
                        def _(pe):
                            for b in range(B):
                                pe.wait_ge(added, 2 * b + 2)
                                if b >= 2:
                                    pe.wait_ge(o_copied, b - 1)
                                for k in range(2):
                                    for s in range(2):
                                        last = pe.transpose(ps_o[:, b % 2, k, s * P:(s + 1) * P],
                                                            res[:, 2 * b + s, k * CK:(k + 1) * CK], ident[:])
                                last.then_inc(o_turned, 1)

                        @block.scalar
                        def _(act):
                            def body(i):
                                for b in range(2):
                                    act.wait_ge(o_turned, i * 2 + (b + 1))
                                    if later(i):
                                        act.wait_ge(o_out[b], i * 32)
                                    act.activation(oc[:, b, :, :], ps_o[:, b, :, :], ACT.Copy).then_inc(o_copied, 1)
                            repeat(act, TRIPS, body)

                        @block.sync
                        def _(sp):
                            def body(i):
                                for b in range(2):
                                    sp.wait_ge(o_copied, i * 2 + (b + 1))
                                    sp.nop(nofuse=True)
                                    for k in range(2):
                                        sp.dma_start(out[bass.ds(i * 2 + b, 1), k * CK:(k + 1) * CK, :, :].rearrange("b c h w -> (b c) (h w)"),
                                                     oc[:, b, k, :]).then_inc(o_out[b], 16)
                            repeat(sp, TRIPS, body)
                            for b in range(2):
                                sp.wait_ge(o_out[b], 32 * TRIPS)

        def delta(ctx):
            wq, wk, wv, wb, wo = delta_args
            NH = wb.shape[1]
            D = C // NH
            K = 16
            HB = P // (L // K)
            HALVES = B // HB
            HT = NT // HALVES
            HC = NH // 2
            X = K + K
            NCH = L // K
            w_all = sb("w_all", [CK, 2, 3 * C + NH], ctx=ctx)
            w_o = sb("w_o", [CK, 2, C], ctx=ctx)
            blocks = sb("blocks", [CK, HC, D], ctx=ctx)
            area1 = sb("area1", [P, 2 * K * P * 2 // 2], ctx=ctx)
            tT = area1[0:CK, :].rearrange("c (k t) -> c k t", k=2)
            oT = tT
            y_rows = area1[:, 0:K * C].rearrange("p (t c) -> p t c", t=K)
            area2 = sb("area2", [P, K * 3 * C], ctx=ctx)
            qkv = area2[:].rearrange("p (t c) -> p t c", t=K)
            o_sys = area2[:, 0:K * C].rearrange("p (t c) -> p t c", t=K)
            uo_sys = area2[:, K * C:3 * K * C].rearrange("p (f x c) -> p f x c", f=2, x=X)
            z = sb("z", [P, K, 2 * C], ctx=ctx)
            zv = z[:].rearrange("p t (h d x) -> p t h d x", d=D, x=2)
            wqT = sb("wqT", [CK, 2, P, X], ctx=ctx)
            AREA3 = max(4 * 8 * CK + 4 * C, 2 * HB * X + 4 * C + 2 * C + 16 * CK)
            area3 = sb("area3", [P, AREA3], ctx=ctx)
            k_blk = area3[0:CK, 0:4 * 8 * CK].rearrange("c (u p m) -> c u p m", u=4, p=8)
            kq_out = area3[:, 4 * 8 * CK:4 * 8 * CK + 4 * C].rearrange("p (u g c) -> p u g c", u=2, g=4)
            at = 0

            def cut(n):
                nonlocal at
                at += n
                return area3[:, at - n:at]
            wq_n = cut(2 * HB * X)[0:CK, :].rearrange("c (u b x) -> c u b x", u=2, b=HB)
            yk = cut(2 * 2 * C).rearrange("p (u b m) -> p u b m", u=2, b=2)
            uo = cut(2 * C).rearrange("p (u b m) -> p u b m", u=2, b=2)
            s_blk = cut(4 * 4 * CK)[0:CK, :].rearrange("c (j g m) -> c j g m", j=4, g=4)
            assert at <= AREA3
            kp = sb("kp", [P, 2, X, HC, K], ctx=ctx)
            tmp = sb("tmp", [P, HC * X * K], ctx=ctx)
            tn = tmp[:, 0:2 * 4 * C].rearrange("p (u q c) -> p u q c", u=2, q=4)
            red = sb("red", [P, C], ctx=ctx)
            ss = sb("ss", [P, K, 2 * NH], ctx=ctx)
            beta = sb("beta", [P, K, NH], ctx=ctx)
            bank = ps("bank", [P, 8, 512], ctx=ctx)
            kq_rows = dram("kq_rows", [HALVES * 2, P // 4, P, CK])
            yk_rows = dram("yk_rows", [HALVES * 2, NCH, P, 2 * 2 * CK])
            uo_rows = dram("uo_rows", [HALVES * 2, NCH, P, 2 * CK])

            names = ("d_weights", "d_blocks", "d_pool", "half_open", "t_ready", "t_turned", "t_copied", "proj_psum",
                     "proj_act", "beta_copied", "squares", "norms", "gates", "kq_turned", "kq_copied", "kblk_dve",
                     "kblk_pool", "kk_psum", "kk_copied", "k_out", "z_ready", "w_turned", "w_copied",
                     "y_copied", "masked", "pool_products", "y_out", "s_zero", "s_ready", "wq_ready", "ws_psum", "uo_ready", "s_psum", "uo_in",
                     "o_ready", "o_turned_d", "o_copied_d", "y_psum_d", "y_added", "z_rows", "t_added", "wq_free")
            S = {s: sem(s) for s in names}
            kp_in = [sem(f"kp_in{x}") for x in range(2)]
            yk_in = [sem(f"yk_in{u}") for u in range(2)]
            uo_out = [sem(f"uo_out{u}") for u in range(2)]
            kk_out = [sem(f"kk_out{u}_") for u in range(2)]
            heads_of = lambda ap: ap.rearrange("p (h d) -> p h d", d=D)
            heads = lambda ap: ap.rearrange("p t (h d) -> p t h d", d=D)

            NC = P // 8

            def by_pool(k, c):
                return k == 1 or c % 3 == 2

            def expanded_by(pools, k, c):
                return sum(by_pool(k_, c_) == pools for k_ in range(2) for c_ in range(NC) if (k_, c_) <= (k, c))

            def expand_keys(eng, hb, k, c, ready):
                n = k * NC + c
                if n >= 4:
                    eng.wait_ge(S["kk_psum"], hb * (2 * NC) + (n - 3))
                eng.tensor_tensor(k_blk[:, n % 4, :, :].rearrange("c p (h t) -> c p h t", h=HC),
                                  spread(wqT[:, k, 8 * c:8 * c + 8, 0:K], 2, HC), spread(blocks[:], 1, 8),
                                  ALU.mult).then_inc(ready, 1)

            HD = 4
            POOL_PRODUCTS = K - 1 + K

            def solve_product(eng, f, i, lo, hi):
                return eng.tensor_tensor(tmp[:, lo * X * i:hi * X * i].rearrange("p (h x j) -> p h x j", h=hi - lo, x=X),
                                         spread(kp[:, f, i, lo:hi, 0:i], 2, X),
                                         z[:, 0:i, f * C + lo * X:f * C + hi * X].rearrange("p j (h x) -> p h x j", x=X), ALU.mult)

            def out_product(eng, f, m, i, lo, hi):
                n_j = 2 * m + 2
                at = i * CK * n_j
                return eng.tensor_tensor(tmp[:, at + lo * D * n_j:at + hi * D * n_j].rearrange("p (h e j) -> p h e j", h=hi - lo, e=D),
                                         spread(kp[:, f, K + 2 * m + i, lo:hi, 0:n_j], 2, D),
                                         uo_sys[:, f, 0:n_j, lo * D:hi * D].rearrange("p j (h e) -> p h e j", h=hi - lo), ALU.mult)

            with nc.Block() as block:
                @block.gpsimd
                def _(pool):
                    order = Order(pool, S["d_pool"])
                    order.mark(pool.memset(blocks[:], 1.0))
                    order.wait()
                    order.mark(pool.affine_select(out=blocks[:], in_=blocks[:], compare_op=ALU.is_ge, fill=0.0, base=0,
                                                  pattern=[[-D, HC], [0, D]], channel_multiplier=1))
                    order.wait()
                    pool.affine_select(out=blocks[:], in_=blocks[:], compare_op=ALU.is_ge, fill=0.0, base=D - 1,
                                       pattern=[[D, HC], [0, D]], channel_multiplier=-1).then_inc(S["d_blocks"], 1)
                    pool.wait_ge(S["d_blocks"], 1)
                    with pool.Fori(0, HALVES) as hb:
                        pool.wait_ge(S["kq_copied"], hb * K + K)
                        for k in range(2):
                            for c in range(NC):
                                if by_pool(k, c):
                                    expand_keys(pool, hb, k, c, S["kblk_pool"])
                        pool.wait_ge(S["kk_psum"], hb * (2 * NC) + 2 * NC)
                        for u in range(2):
                            pool.wait_ge(kk_out[u], hb * (16 * NC // 2) + 16 * NC // 2)
                        pool.nop(nofuse=True)
                        pool.memset(s_blk[:], 0.0).then_inc(S["s_zero"], 1)
                        pool.wait_ge(kp_in[0], hb * 32 + 32)
                        pool.wait_ge(S["gates"], hb + 1)
                        pool.tensor_tensor(kp[:, 1, 0:K, :, :], kp[:, 1, 0:K, :, :], spread(beta[:, :, HC:NH], 3, K), ALU.mult).then_inc(S["masked"], 1)
                        pool.wait_ge(kp_in[1], hb * 32 + 32)
                        pool.nop(nofuse=True)
                        for f in range(2):
                            pool.affine_select(out=kp[:, f, K:X, :, :], in_=kp[:, f, K:X, :, :], compare_op=ALU.is_ge, fill=0.0, base=0,
                                               pattern=[[1, K], [0, HC], [-1, K]], channel_multiplier=0).then_inc(S["masked"], 1)
                        for i in range(1, K):
                            pool.wait_ge(S["z_ready"], (hb * 2 + 1) * K + i)
                            solve_product(pool, 1, i, HD, HC).then_inc(S["pool_products"], 1)
                        pool.wait_ge(S["masked"], hb * 3 + 3)
                        pool.wait_ge(S["z_ready"], (hb * 2 + 2) * K)
                        for f in range(2):
                            pool.wait_ge(S["uo_in"], (hb * 2 + (f + 1)) * 128)
                            for m in range(K // 2):
                                if f or m:
                                    pool.wait_ge(S["o_ready"], hb * K + (f * (K // 2) + m))
                                for i in range(2):
                                    last = out_product(pool, f, m, i, HD, HC)
                                last.then_inc(S["pool_products"], 1)

                @block.sync
                def _(sp):
                    for n, w in enumerate((wq, wk, wv, wb)):
                        sp.dma_start(w_all[:, :, n * C:n * C + w.shape[1]], w.rearrange("(k c) o -> c k o", k=2)).then_inc(S["d_weights"], 16)
                    sp.dma_start(w_o[:], wo.rearrange("(k c) o -> c k o", k=2)).then_inc(S["d_weights"], 16)
                    for hf in range(HALVES * 2):
                        for j in range(4):
                            for b in range(2):
                                sp.dma_start(yk_rows[hf, :, X * j + K:X * j + X, b * C:(b + 1) * C],
                                             spread(zeros[0:NCH, :], 1, K)).then_inc(S["z_rows"], 16)
                    sp.wait_ge(S["z_rows"], 16 * HALVES * 2 * 4 * 2)
                    with sp.Fori(0, HALVES) as hb:
                        def key_rows(f, b, j, part):
                            lo = (2 * b + part) * CK
                            return yk_rows[bass.ds(hb * 2 + f, 1), :, X * j:X * j + K, lo:lo + CK].rearrange("o n x c -> (o n) x c")
                        sp.wait_ge(S["norms"], hb * 5 + 5)
                        sp.nop(nofuse=True)
                        for f in range(2):
                            for b in range(2):
                                for j in range(4):
                                    p0 = (b * 4 + j) * NCH
                                    sp.dma_start(key_rows(f, b, j, 1), qkv[p0:p0 + NCH, :, C + f * CK:C + (f + 1) * CK]).then_inc(S["k_out"], 16)
                        for f in range(2):
                            sc = hb * 2 + f
                            for c in range(NC // 2):
                                u = c % 2
                                sp.wait_ge(S["kk_copied"], sc * NC + (2 * c + 2))
                                sp.nop(nofuse=True)
                                sp.dma_start(kq_rows[bass.ds(hb * 2 + f, 1), 4 * c:4 * c + 4, :, :].rearrange("o g p c -> (o p) g c"),
                                             kq_out[:, u, :, :]).then_inc(kk_out[u], 16)
                            for u in range(2):
                                sp.wait_ge(kk_out[u], sc * (4 * NC) + 4 * NC)
                            if f:
                                for x in range(2):
                                    sp.wait_ge(kp_in[x], hb * 32 + 16)
                            sp.nop(nofuse=True)
                            chunk_rows = kq_rows[bass.ds(hb * 2 + f, 1), :, :, :].rearrange("o g (j x) c -> (o g j) x c", j=4)
                            for x in range(2):
                                sp.dma_start(kp[:, f, x * K:(x + 1) * K, :, :].rearrange("p x h t -> p (x h t)"),
                                             chunk_rows[:, x * K:(x + 1) * K, :].rearrange("p x c -> p (x c)")).then_inc(kp_in[x], 16)
                        for f in range(2):
                            sc = hb * 2 + f
                            sp.wait_ge(S["y_copied"], sc + 1)
                            sp.nop(nofuse=True)
                            for b in range(2):
                                for j in range(4):
                                    p0 = (b * 4 + j) * NCH
                                    sp.dma_start(key_rows(f, b, j, 0), y_rows[p0:p0 + NCH, :, f * CK:(f + 1) * CK]).then_inc(S["y_out"], 16)
                            sp.wait_ge(S["y_out"], sc * 128 + 128)
                            sp.wait_ge(S["k_out"], hb * 256 + 256)
                            sp.nop(nofuse=True)

                            def load(n, u):
                                sp.dma_start(yk[:, u, :, :].rearrange("p b m -> p (b m)"),
                                             yk_rows[bass.ds(hb * 2 + f, 1), bass.ds(n, 1), :, :].rearrange("o n p m -> (o n p) m")).then_inc(yk_in[u], 16)
                            for u in range(2):
                                load(u, u)

                            def chunks(i, more):
                                for u in range(2):
                                    sp.wait_ge(S["uo_ready"], sc * (2 * NCH) + (i * 4 + (2 * u + 2)))
                                    sp.nop(nofuse=True)
                                    sp.dma_start(uo_rows[bass.ds(hb * 2 + f, 1), bass.ds(i * 2 + u, 1), :, :].rearrange("o n p m -> (o n p) m"),
                                                 uo[:, u, :, :].rearrange("p b m -> p (b m)")).then_inc(uo_out[u], 16)
                                    if more:
                                        sp.wait_ge(S["s_psum"], sc * (2 * NCH) + (i * 4 + (2 * u + 2)))
                                        sp.nop(nofuse=True)
                                        load(i * 2 + (u + 2), u)
                            with sp.Fori(0, NCH // 2 - 1) as i:
                                chunks(i, True)
                            chunks(NCH // 2 - 1, False)
                            for u in range(2):
                                sp.wait_ge(uo_out[u], sc * (8 * NCH) + 8 * NCH)
                                sp.wait_ge(yk_in[u], sc * (8 * NCH) + 8 * NCH)
                            sp.nop(nofuse=True)
                            for b in range(2):
                                for j in range(4):
                                    p0 = (b * 4 + j) * NCH
                                    sp.dma_start(uo_sys[p0:p0 + NCH, f, :, :],
                                                 uo_rows[bass.ds(hb * 2 + f, 1), :, X * j:X * j + X, b * CK:(b + 1) * CK].rearrange("o n x c -> (o n) x c")).then_inc(S["uo_in"], 16)

                @block.tensor
                def _(pe):
                    pe.wait_ge(S["d_weights"], 16 * 5)
                    with pe.Fori(0, HALVES) as hb:
                        for g in range(4):
                            u = g % 2
                            pe.wait_ge(S["t_ready"], hb * 16 + (4 * g + 4))
                            if g >= 2:
                                pe.wait_ge(S["t_copied"], hb * 4 + (g - 1))
                            for q in range(4):
                                for k in range(2):
                                    last = pe.transpose(bank[0:CK, 2 * u + k, q * P:(q + 1) * P], tn[:, u, q, k * CK:(k + 1) * CK], ident[:])
                            last.then_inc(S["t_turned"], 1)
                        pe.wait_ge(S["t_copied"], hb * 4 + 4)
                        for t in range(K):
                            b0 = 4 + 2 * (t % 2)
                            if t >= 2:
                                pe.wait_ge(S["proj_act"], hb * (2 * K) + 2 * (t - 1))
                                pe.wait_ge(S["beta_copied"], hb * K + (t - 1))
                            for c, (lo, hi) in enumerate(((0, 2 * C), (2 * C, 3 * C + NH))):
                                for k in range(2):
                                    last = pe.matmul(bank[:, b0 + c, 0:hi - lo], tT[:, k, t::K], w_all[:, k, lo:hi], start=k == 0, stop=k == 1)
                            last.then_inc(S["proj_psum"], 1)
                        for t in range(K):
                            pe.wait_ge(S["norms"], hb * 5 + (t // 4 + 2))
                            if t < 2:
                                pe.wait_ge(S["beta_copied"], hb * K + K)
                            else:
                                pe.wait_ge(S["kq_copied"], hb * K + (t - 1))
                            for x in range(2):
                                for k in range(2):
                                    lo = (1 - x) * C + k * CK
                                    last = pe.transpose(bank[0:CK, 6 + t % 2, (2 * x + k) * P:(2 * x + k + 1) * P], qkv[:, t, lo:lo + CK], ident[:])
                            last.then_inc(S["kq_turned"], 1)
                        for k in range(2):
                            for c in range(NC):
                                n = k * NC + c
                                for pools, ready in ((False, "kblk_dve"), (True, "kblk_pool")):
                                    if expanded_by(pools, k, c):
                                        pe.wait_ge(S[ready], hb * expanded_by(pools, 1, NC - 1) + expanded_by(pools, k, c))
                                banks, b0 = (4, 0) if k == 0 else (2, 4)
                                if c >= banks:
                                    pe.wait_ge(S["kk_copied"], hb * (2 * NC) + (n - banks + 1))
                                for g in range(2):
                                    for j in range(4):
                                        last = pe.matmul(bank[32 * j:32 * j + 32, b0 + c % banks, g * CK:(g + 1) * CK],
                                                         wqT[:, k, 8 * c + 4 * g + j, :], k_blk[:, n % 4, 4 * g + j, :], start=True, stop=True,
                                                         tile_position=(0, 32 * j))
                                last.then_inc(S["kk_psum"], 1)
                        for f in range(2):
                            sc = hb * 2 + f
                            for t in range(K):
                                pe.wait_ge(S["z_ready"], sc * K + (t + 1))
                                if t >= 2:
                                    pe.wait_ge(S["w_copied"], sc * K + (t - 1))
                                pe.transpose(bank[0:CK, 6 + t % 2, 0:P], zv[:, t, f * HC:(f + 1) * HC, :, 1].rearrange("p h d -> p (h d)"),
                                             ident[:]).then_inc(S["w_turned"], 1)
                            pe.wait_ge(S["w_copied"], sc * K + K)
                            pe.wait_ge(S["s_zero"], hb + 1)
                            pe.nop(nofuse=True)
                            with pe.Fori(0, NCH // 2) as i:
                                for u in range(2):
                                    pe.wait_ge(S["wq_ready"], sc * NCH + (i * 2 + (u + 1)))
                                    for s in range(2):
                                        pe.wait_ge(S["s_ready"], sc * (2 * NCH + 2) + (i * 4 + (2 * u + s + 1)))
                                        for j in (2 * s, 2 * s + 1):
                                            for b in range(2):
                                                last = pe.matmul(bank[32 * j:32 * j + 32, 4 + s, b * CK:(b + 1) * CK], wq_n[:, u, 4 * b + j, :],
                                                                 s_blk[:, j, 2 * b + f, :], start=True, stop=True, tile_position=(0, 32 * j))
                                        last.then_inc(S["ws_psum"], 1)
                                    pe.wait_ge(yk_in[u], sc * (8 * NCH) + (i * 16 + 16))
                                    for s in range(2):
                                        pe.wait_ge(S["uo_ready"], sc * (2 * NCH) + (i * 4 + (2 * u + s + 1)))
                                        for j in (2 * s, 2 * s + 1):
                                            for b in range(2):
                                                m = (2 * b + f) * CK
                                                last = pe.matmul(bank[0:CK, j, m:m + CK], yk[32 * j:32 * j + K, u, b, CK:2 * CK],
                                                                 uo[32 * j:32 * j + K, u, b, :], start=False, stop=True,
                                                                 skip_group_check=True)
                                        last.then_inc(S["s_psum"], 1)
                        for t in range(K):
                            pe.wait_ge(S["o_ready"], hb * K + (K // 2 + t // 2 + 1))
                            if t >= 2:
                                pe.wait_ge(S["o_copied_d"], hb * K + (t - 1))
                            for k in range(2):
                                last = pe.transpose(bank[0:CK, 6 + t % 2, k * P:(k + 1) * P], o_sys[:, t, k * CK:(k + 1) * CK], ident[:])
                            last.then_inc(S["o_turned_d"], 1)
                        pe.wait_ge(S["o_copied_d"], hb * K + K)
                        for j in range(HT):
                            if j >= 2:
                                pe.wait_ge(S["y_added"], hb * HT + (j - 1))
                            for k in range(2):
                                last = pe.matmul(bank[:, 4 + j % 2, 0:C], oT[:, k, j * P:(j + 1) * P], w_o[:, k, :], start=k == 0, stop=k == 1)
                            last.then_inc(S["y_psum_d"], 1)

                @block.scalar
                def _(act):
                    with act.Fori(0, HALVES) as hb:
                        for g in range(4):
                            act.wait_ge(S["t_turned"], hb * 4 + (g + 1))
                            act.activation(tT[:, :, g * 4 * P:(g + 1) * 4 * P], bank[0:CK, 2 * (g % 2):2 * (g % 2) + 2, :], ACT.Copy).then_inc(S["t_copied"], 1)
                        for t in range(K):
                            act.wait_ge(S["proj_psum"], hb * K + (t + 1))
                            b0 = 4 + 2 * (t % 2)
                            act.activation(qkv[:, t, 0:2 * C], bank[:, b0, 0:2 * C], ACT.Silu).then_inc(S["proj_act"], 1)
                            act.activation(qkv[:, t, 2 * C:3 * C], bank[:, b0 + 1, 0:C], ACT.Silu).then_inc(S["proj_act"], 1)
                            act.activation(beta[:, t, :], bank[:, b0 + 1, C:C + NH], ACT.Copy).then_inc(S["beta_copied"], 1)
                        act.wait_ge(S["beta_copied"], hb * K + K)
                        act.activation(beta[:], beta[:], ACT.Sigmoid).then_inc(S["gates"], 1)
                        act.wait_ge(S["squares"], hb + 1)
                        act.activation(ss[:], ss[:], ACT.Sqrt, bias=eps[1e-6][:, 0:1]).then_inc(S["norms"], 1)
                        for t in range(K):
                            act.wait_ge(S["kq_turned"], hb * K + (t + 1))
                            act.activation(wqT[:].rearrange("c k p (x t) -> c x k p t", x=2)[:, :, :, :, t],
                                           bank[0:CK, 6 + t % 2, :].rearrange("c (x k p) -> c x k p", x=2, k=2), ACT.Copy).then_inc(S["kq_copied"], 1)
                        for k in range(2):
                            for c in range(NC):
                                n = k * NC + c
                                u = (c // 2) % 2
                                act.wait_ge(S["kk_psum"], hb * (2 * NC) + (n + 1))
                                if n >= 4 and c % 2 == 0:
                                    act.wait_ge(kk_out[u], hb * (8 * NC) + 16 * (n // 4))
                                b0 = c % 4 if k == 0 else 4 + c % 2
                                act.activation(kq_out[:, u, 2 * (c % 2):2 * (c % 2) + 2, :],
                                               bank[:, b0, 0:C].rearrange("p (g c) -> p g c", g=2), ACT.Copy).then_inc(S["kk_copied"], 1)
                        for f in range(2):
                            sc = hb * 2 + f
                            for t in range(K):
                                if t == (0 if f else K - 1):
                                    act.wait_ge(S["z_ready"], sc * K + K)
                                    act.activation(y_rows[:, :, f * CK:(f + 1) * CK], zv[:, :, f * HC:(f + 1) * HC, :, 0].rearrange("p t h d -> p t (h d)"),
                                                   ACT.Copy).then_inc(S["y_copied"], 1)
                                act.wait_ge(S["w_turned"], sc * K + (t + 1))
                                act.activation(wqT[:, f, :, t], bank[0:CK, 6 + t % 2, 0:P], ACT.Copy).then_inc(S["w_copied"], 1)
                            act.wait_ge(S["w_copied"], sc * K + K)
                            with act.Fori(0, NCH // 2) as i:
                                for u in range(2):
                                    act.wait_ge(S["wq_free"], sc * (NCH + 2) + (i * 2 + (u + 1)))
                                    act.activation(wq_n[:, u, :, :], wqT[:, f, :, :].rearrange("c (b n) x -> c b n x", n=NCH)[:, :, bass.ds(i * 2 + u, 1), :].rearrange("c b o x -> c b (o x)"),
                                                   ACT.Copy).then_inc(S["wq_ready"], 1)
                        for t in range(K):
                            act.wait_ge(S["o_turned_d"], hb * K + (t + 1))
                            act.activation(oT[:, :, t::K], bank[0:CK, 6 + t % 2, 0:2 * P].rearrange("c (k p) -> c k p", k=2), ACT.Copy).then_inc(S["o_copied_d"], 1)
                    deviations_act(act, 1e-5)

                @block.vector
                def _(v):
                    order = dve_order(v)
                    v.nop().then_inc(S["half_open"], 1)
                    with v.Fori(0, HALVES) as hb:
                        order.trip(hb, 16 + 1 + 2 + 1 + 2 * 15 * 3 + 1 + 2 * 8 * 3 + (HT // GS) * STATS_MARKS)

                        def step(ins):
                            order.mark(ins)
                            order.wait()
                        v.wait_ge(S["half_open"], hb + 1)
                        for g in range(4):
                            u = g % 2
                            if g >= 2:
                                v.wait_ge(S["t_turned"], hb * 4 + (g - 1))
                                v.wait_ge(S["t_added"], hb * 4 + (g - 1))
                            for q in range(4):
                                tile = hb * HT + (4 * g + q)
                                v.tensor_scalar(tn[:, u, q, :], one(res, tile), mu_var[:, bass.ds(tile, 1), 0], rstd[:, bass.ds(tile, 1)],
                                                ALU.subtract, ALU.mult).then_inc(S["t_ready"], 1)
                            v.wait_ge(S["t_ready"], hb * 16 + (4 * g + 4))
                            four = res[:, bass.ds(hb * HT + 4 * g, 4), :]
                            v.tensor_tensor(four, four, tn[:, u, :, :], ALU.add).then_inc(S["t_added"], 1)
                        v.wait_ge(S["t_added"], hb * 4 + 4)
                        v.wait_ge(S["t_turned"], hb * 4 + 4)
                        for g in range(8):
                            sq = tmp[:, 0:4 * C].rearrange("p (t c) -> p t c", t=2)
                            v.wait_ge(S["proj_act"], hb * (2 * K) + 4 * (g + 1))
                            step(v.tensor_tensor(sq, qkv[:, 2 * g:2 * g + 2, 0:2 * C], qkv[:, 2 * g:2 * g + 2, 0:2 * C], ALU.mult))
                            step(v.tensor_reduce(ss[:, 2 * g:2 * g + 2, :], sq.rearrange("p t (h d) -> p t h d", d=D), AX_X, ALU.add))
                        v.nop().then_inc(S["squares"], 1)
                        v.wait_ge(S["norms"], hb * 5 + 1)
                        step(v.reciprocal(ss[:], ss[:]))
                        for g in range(4):
                            four = heads(qkv[:, 4 * g:4 * g + 4, 0:2 * C])
                            v.tensor_tensor(four, four, spread(ss[:, 4 * g:4 * g + 4, :], 3, D), ALU.mult).then_inc(S["norms"], 1)
                        v.wait_ge(S["gates"], hb + 1)
                        v.wait_ge(S["norms"], hb * 5 + 5)
                        order.mark(v.tensor_tensor(zv[:, :, :, :, 0], heads(qkv[:, :, 2 * C:3 * C]), spread(beta[:], 3, D), ALU.mult))
                        order.mark(v.tensor_tensor(zv[:, :, :, :, 1], heads(qkv[:, :, C:2 * C]), spread(beta[:], 3, D), ALU.mult))
                        v.wait_ge(S["kq_copied"], hb * K + K)
                        v.wait_ge(S["d_blocks"], 1)
                        for c in range(NC):
                            if not by_pool(0, c):
                                expand_keys(v, hb, 0, c, S["kblk_dve"])
                        v.wait_ge(S["kk_copied"], hb * (2 * NC) + NC)
                        order.mark(v.memset(bank[0:CK, 0:4, 0:4 * CK], 0.0))
                        v.wait_ge(kp_in[0], hb * 32 + 16)
                        step(v.tensor_tensor(kp[:, 0, 0:K, :, :], kp[:, 0, 0:K, :, :], spread(beta[:, :, 0:HC], 3, K), ALU.mult))

                        def solve_products(f, i):
                            order.wait()
                            v.nop().then_inc(S["z_ready"], 1)
                            order.mark(solve_product(v, f, i, 0, HD if f else HC))

                        def solve_sums(f, i):
                            order.wait()
                            if f:
                                v.wait_ge(S["pool_products"], hb * POOL_PRODUCTS + i)
                            order.mark(v.tensor_reduce(red[:].rearrange("p (h x) -> p h x", x=X),
                                                       tmp[:, 0:HC * X * i].rearrange("p (h x j) -> p h x j", h=HC, x=X), AX_X, ALU.add))
                            order.wait()
                            order.mark(v.tensor_tensor(z[:, i, f * C:(f + 1) * C], z[:, i, f * C:(f + 1) * C], red[:], ALU.subtract))

                        def out_products(f, m):
                            order.wait()
                            for i in range(2):
                                order.mark(out_product(v, f, m, i, 0, HD))

                        def out_sums(f, m):
                            pair = o_sys[:, 2 * m:2 * m + 2, f * CK:(f + 1) * CK]
                            order.wait()
                            v.wait_ge(S["pool_products"], hb * POOL_PRODUCTS + (K - 1 + f * (K // 2) + m + 1))
                            order.mark(v.tensor_reduce(pair, tmp[:, 0:2 * CK * (2 * m + 2)].rearrange("p (i m j) -> p i m j", i=2, m=CK), AX_X, ALU.add))
                            order.wait()
                            v.tensor_tensor(pair, pair, uo_sys[:, f, K + 2 * m:K + 2 * m + 2, :], ALU.subtract).then_inc(S["o_ready"], 1)

                        def solved(f):
                            order.wait()
                            v.nop().then_inc(S["z_ready"], 1)

                        def scan(f, beside_update, beside_state):
                            sc = hb * 2 + f
                            for s in range(2):
                                v.nop().then_inc(S["s_ready"], 1)
                                v.nop().then_inc(S["wq_free"], 1)
                            for n in range(NCH):
                                u = n % 2
                                if n >= 2:
                                    v.wait_ge(uo_out[u], sc * (8 * NCH) + 16 * (n // 2))
                                v.wait_ge(yk_in[u], sc * (8 * NCH) + (16 * (n // 2) + 16))
                                for s in range(2):
                                    at = slice(64 * s, 64 * s + 64)
                                    v.wait_ge(S["ws_psum"], sc * (2 * NCH) + (2 * n + s + 1))
                                    v.tensor_tensor(uo[at, u, :, :], yk[at, u, :, 0:CK],
                                                    bank[at, 4 + s, 0:C].rearrange("x (b c) -> x b c", b=2), ALU.subtract).then_inc(S["uo_ready"], 1)
                                v.nop().then_inc(S["wq_free"], 1)
                                beside_update(n)
                                for s in range(2):
                                    v.wait_ge(S["s_psum"], sc * (2 * NCH) + (2 * n + s + 1))
                                    v.tensor_tensor(s_blk[:, 2 * s:2 * s + 2, f::2, :],
                                                    bank[0:CK, 2 * s:2 * s + 2, 0:4 * CK].rearrange("c j (g m) -> c j g m", g=4)[:, :, f::2, :],
                                                    spread(spread(blocks[:].rearrange("c h d -> c (h d)"), 1, 2), 1, 2), ALU.mult).then_inc(S["s_ready"], 1)
                                beside_state(n)

                        for i in range(1, K):
                            solve_products(0, i)
                            solve_sums(0, i)
                        solved(0)
                        v.wait_ge(S["masked"], hb * 3 + 1)
                        scan(0, lambda n: solve_products(1, n) if n else None, lambda n: solve_sums(1, n) if n else None)
                        solved(1)
                        v.wait_ge(S["uo_in"], (hb * 2 + 1) * 128)
                        v.wait_ge(S["masked"], hb * 3 + 3)
                        scan(1, lambda n: None if n % 2 else out_products(0, n // 2), lambda n: out_sums(0, n // 2) if n % 2 else None)
                        v.wait_ge(S["uo_in"], (hb * 2 + 2) * 128)
                        for m in range(K // 2):
                            out_products(1, m)
                            out_sums(1, m)
                        for g in range(HT // GS):
                            for q in range(GS):
                                j = g * GS + q
                                v.wait_ge(S["y_psum_d"], hb * HT + (j + 1))
                                tile = hb * HT + j
                                v.tensor_tensor(one(res, tile), one(res, tile), bank[:, 4 + j % 2, 0:C], ALU.add).then_inc(S["y_added"], 1)
                            v.wait_ge(S["y_added"], hb * HT + (g + 1) * GS)
                            order.wait()
                            group_stats(v, order, hb * (HT // GS) + g)
                        order.wait()
                        v.nop().then_inc(S["half_open"], 1)
                        order.end_trip()
                    order.leave(HALVES)
                    deviations_dve(v, order)
                    dve_leaves(order)

        def load_experts(eng, n, w1, w2, b2, done):
            _, up, b_up, down, b_down = moe_args[n]
            for k in range(2):
                eng.dma_start(w1[0:CK, k, :, :], up[:, k * CK:(k + 1) * CK, :].rearrange("e c f -> c e f")).then_inc(done, 16)
            eng.dma_start(w1[CK:CK + 1, 0, :, :], b_up.rearrange("(o e) f -> o e f", o=1)).then_inc(done, 16)
            for k in range(FK):
                eng.dma_start(w2[:, k, :, :], down[:, k * P:(k + 1) * P, :].rearrange("e p d -> p e d")).then_inc(done, 16)
            eng.dma_start(b2[:].rearrange("p e c -> p (e c)"), b_down.rearrange("e d -> (e d)").partition_broadcast(P)).then_inc(done, 16)

        LOADS = 16 * (2 + 1 + FK + 1)

        with ExitStack() as m0:
            w1 = sb("w1_0", [CK + 1, 2, E, FF], ctx=m0)
            w2 = sb("w2_0", [P, FK, E, C], ctx=m0)
            b2 = sb("b2_0", [P, E, C], ctx=m0)
            w_in = sem("w_in0")
            with ExitStack() as a:
                xc = sb("xc", [CK, 2, T], ctx=a)
                xn = sb("xn", [CK, 2, T], ctx=a)
                BLK = 512
                NB = T // BLK
                GRP = 4
                sq = sb("sq", [CK, 2, 2, BLK], ctx=a)
                sd = sb("sd", [CK, 2, BLK], ctx=a)
                w_raw = sb("w_raw", [CK, 2, 2, C], ctx=a)
                w_T = sb("w_T", [CK, 2, 2, C], ctx=a)
                bias = sb("bias", [CK, 2, NG], ctx=a)
                (x_in, bias_in, mean_psum, centred, sq_ready, var_psum, sd_ready, rs_ready, normed, wT_psum, wT_ready,
                 conv_psum, conv_done) = [sem(s) for s in (
                    "x_in", "bias_in", "mean_psum", "centred", "sq_ready", "var_psum", "sd_ready", "rs_ready", "normed",
                    "wT_psum", "wT_ready", "conv_psum", "conv_done")]
                w_raw_in = [sem(f"w_raw_in{u}") for u in range(2)]
                with ExitStack() as s1:
                    ps_mean = ps("ps_mean", [CK, GRP, BLK], ctx=s1)
                    ps_var = ps("ps_var", [CK, GRP, BLK], ctx=s1)
                    with nc.Block() as block:
                        @block.sync
                        def _(sp):
                            for b in range(0, B, 4):
                                for k in range(2):
                                    sp.dma_start(xc[:, k, b * L:(b + 4) * L].rearrange("c (b l) -> c b l", b=4),
                                                 x[b:b + 4, k * CK:(k + 1) * CK, :, :].rearrange("b c h w -> c b (h w)")).then_inc(x_in, 16)
                            with nc.allow_non_contiguous_dma("a small bias"):
                                for k in range(2):
                                    sp.dma_start(bias[:, k, :], conv_b[:, k * CK:(k + 1) * CK].rearrange("g c -> c g")).then_inc(bias_in, 16)

                        @block.scalar
                        def _(act):
                            act.wait_ge(x_in, 16 * B // 2)
                            load_experts(act, 0, w1, w2, b2, w_in)

                            def body(i):
                                for q in range(GRP):
                                    act.wait_ge(centred, i * GRP + (q + 1))
                                    if later(i) or q >= 2:
                                        act.wait_ge(var_psum, i * GRP + (q - 1))
                                    act.activation(sq[:, q % 2, :, :], xn[:, :, bass.ds((i * GRP + q) * BLK, BLK)], ACT.Square).then_inc(sq_ready, 1)
                                    act.wait_ge(var_psum, i * GRP + (q + 1))
                                    if later(i) or q >= 2:
                                        act.wait_ge(normed, i * GRP + (q - 1))
                                    act.activation(sd[:, q % 2, :], ps_var[:, q, :], ACT.Sqrt, bias=eps[1e-6][0:CK, 0:1]).then_inc(sd_ready, 1)
                            repeat(act, NB // GRP, body)

                        @block.tensor
                        def _(pe):
                            pe.wait_ge(x_in, 16 * B // 2)

                            def body(i):
                                for q in range(GRP):
                                    if later(i):
                                        pe.wait_ge(centred, i * GRP + (q - 3))
                                    for k in range(2):
                                        last = pe.matmul(ps_mean[:, q, :], mean_w[:], xc[:, k, bass.ds((i * GRP + q) * BLK, BLK)],
                                                         start=k == 0, stop=k == 1)
                                    last.then_inc(mean_psum, 1)
                                for q in range(GRP):
                                    pe.wait_ge(sq_ready, i * GRP + (q + 1))
                                    for k in range(2):
                                        last = pe.matmul(ps_var[:, q, :], mean_w[:], sq[:, q % 2, k, :], start=k == 0, stop=k == 1)
                                    last.then_inc(var_psum, 1)
                            repeat(pe, NB // GRP, body)

                        @block.vector
                        def _(v):
                            def body(i):
                                for q in range(GRP):
                                    at = bass.ds((i * GRP + q) * BLK, BLK)
                                    v.wait_ge(mean_psum, i * GRP + (q + 1))
                                    v.tensor_tensor(xn[:, :, at], xc[:, :, at], spread(ps_mean[:, q, :], 1, 2), ALU.subtract).then_inc(centred, 1)
                                for q in range(GRP):
                                    at = bass.ds((i * GRP + q) * BLK, BLK)
                                    v.wait_ge(sd_ready, i * GRP + (q + 1))
                                    v.reciprocal(sd[:, q % 2, :], sd[:, q % 2, :]).then_inc(rs_ready, 1)
                                    v.wait_ge(rs_ready, i * GRP + (q + 1))
                                    v.tensor_tensor(xn[:, :, at], xn[:, :, at], spread(sd[:, q % 2, :], 1, 2), ALU.mult).then_inc(normed, 1)
                            v.wait_ge(x_in, 16 * B // 2)
                            repeat(v, NB // GRP, body)

                with ExitStack() as s2:
                    ps_w = ps("ps_w", [CK, 2, 512], ctx=s2)
                    ps_c = ps("ps_c", [CK, 2, 512], ctx=s2)
                    def places(t, k, gh, gw):
                        v = t[:, k, :].rearrange("c (r i w j) -> c r i w j", i=GS, w=W // GS, j=GS)
                        return v[:, :, bass.ds(gh, 1), :, gw].rearrange("c r o w -> c (r o) w")
                    with nc.Block() as block:
                        @block.sync
                        def _(sp):
                            def body(i):
                                for j in range(GS):
                                    u = j % 2
                                    if later(i) or j >= 2:
                                        sp.wait_ge(wT_psum, i * GS + (j - 1))
                                    sp.dma_start(w_raw[:, u, :, :], conv_w[bass.ds(i * GS + j, 1), :, :].rearrange("o (k p) c -> p (o k) c", k=2)).then_inc(w_raw_in[u], 16)
                            repeat(sp, GS, body)

                        @block.tensor
                        def _(pe):
                            def turn(i, j):
                                u = j % 2
                                pe.wait_ge(w_raw_in[u], i * 32 + (16 * (j // 2) + 16))
                                if later(i) or i or j >= 2:
                                    pe.wait_ge(wT_ready, i * GS + (j - 1))
                                for k in range(2):
                                    for o in range(2):
                                        last = pe.transpose(ps_w[:, u, k * C + o * CK:k * C + (o + 1) * CK],
                                                            w_raw[:, u, o, k * CK:(k + 1) * CK], ident[0:CK, 0:CK])
                                last.then_inc(wT_psum, 1)

                            def body(i, first, last_trip):
                                for j in range(GS):
                                    u = j % 2
                                    if j < GS - 1:
                                        turn(i, j + 1)
                                    elif not last_trip:
                                        turn(i + 1, 0)
                                    pe.wait_ge(wT_ready, i * GS + (j + 1))
                                    if not first or j >= 2:
                                        pe.wait_ge(conv_done, i * (2 * GS) + 2 * (j - 1))
                                    for o in range(2):
                                        for k in range(2):
                                            last = pe.matmul(ps_c[:, u, o * B * 16:(o + 1) * B * 16], w_T[:, u, k, o * CK:(o + 1) * CK],
                                                             places(xn, k, i, j), start=k == 0, stop=k == 1)
                                    last.then_inc(conv_psum, 1)
                            turn(0, 0)
                            repeat_to_last(pe, GS, body)

                        @block.scalar
                        def _(act):
                            def body(i):
                                for j in range(GS):
                                    act.wait_ge(wT_psum, i * GS + (j + 1))
                                    if later(i) or j >= 2:
                                        act.wait_ge(conv_psum, i * GS + (j - 1))
                                    act.activation(w_T[:, j % 2, :, :], ps_w[:, j % 2, 0:2 * C].rearrange("c (k o) -> c k o", k=2), ACT.Copy).then_inc(wT_ready, 1)
                            repeat(act, GS, body)

                        @block.vector
                        def _(v):
                            v.wait_ge(bias_in, 32)

                            def body(i):
                                for j in range(GS):
                                    v.wait_ge(conv_psum, i * GS + (j + 1))
                                    for o in range(2):
                                        v.scalar_tensor_tensor(
                                            places(xc, o, i, j), ps_c[:, j % 2, o * B * 16:(o + 1) * B * 16].rearrange("c (r w) -> c r w", w=W // GS),
                                            bias[:, o, bass.ds(i * GS + j, 1)], places(xc, o, i, j), ALU.add, ALU.add).then_inc(conv_done, 1)
                            repeat(v, GS, body)

                with ExitStack() as s3:
                    ps_t = ps("ps_t", [P, 4, 512], ctx=s3)
                    turned, copied = sem("turned"), sem("copied")
                    with nc.Block() as block:
                        @block.tensor
                        def _(pe):
                            for t in range(NT):
                                if t >= GS:
                                    pe.wait_ge(copied, t - 3)
                                for k in range(2):
                                    last = pe.transpose(ps_t[:, t % 4, k * CK:(k + 1) * CK], xc[:, k, t * P:(t + 1) * P], ident[0:CK, 0:CK])
                                last.then_inc(turned, 1)

                        @block.vector
                        def _(v):
                            order = dve_order(v)

                            def body(i):
                                order.trip(i, STATS_MARKS)
                                v.wait_ge(copied, i * GS + GS)
                                if later(i):
                                    order.wait()
                                group_stats(v, order, i)
                            repeat(v, NT // GS, body)
                            order.leave(NT // GS)
                            deviations_dve(v, order)
                            dve_leaves(order)

                        @block.scalar
                        def _(act):
                            def body(i):
                                for u in range(GS):
                                    act.wait_ge(turned, i * GS + (u + 1))
                                    act.activation(one(res, i * GS + u), ps_t[:, u, 0:C], ACT.Copy).then_inc(copied, 1)
                            repeat(act, NT // GS, body)
                            deviations_act(act, 1e-5)

            moe(0, ACT.Gelu, w1, w2, b2, w_in, LOADS, m0, None, 1e-6)

        with ExitStack() as d:
            delta(d)
        with ExitStack() as m1:
            w1 = sb("w1_1", [CK + 1, 2, E, FF], ctx=m1)
            w2 = sb("w2_1", [P, FK, E, C], ctx=m1)
            b2 = sb("b2_1", [P, E, C], ctx=m1)
            w_in = sem("w_in1")
            moe(1, ACT.Relu, w1, w2, b2, w_in, LOADS, m1, lambda eng: load_experts(eng, 1, w1, w2, b2, w_in), None)


_INS = ['x', 'L0_conv_Wg', 'L0_conv_bg', 'L0_ffn_gate_w', 'L0_ffn_w_up', 'L0_ffn_b_up', 'L0_ffn_w_down', 'L0_ffn_b_down',
        'L1_conv_Wq', 'L1_conv_Wk', 'L1_conv_Wv', 'L1_conv_Wb', 'L1_conv_Wo', 'L1_ffn_Wg', 'L1_ffn_W1', 'L1_ffn_b1',
        'L1_ffn_W2', 'L1_ffn_b2']
_OUTS = [((16, 192, 16, 16), 'float32')]


def kernel(**inputs):
    import numpy as _np
    import concourse.bacc as _bacc
    from concourse import mybir as _mybir
    from concourse.bass_utils import run_bass_kernel_spmd as _run

    nc = _bacc.Bacc("TRN2", target_bir_lowering=False, num_devices=1)
    arrays, aps = {}, {}
    for name in _INS:
        a = _np.ascontiguousarray(inputs[name])
        arrays[f"in_{name}_dram"] = a
        aps[name] = nc.dram_tensor(f"in_{name}_dram", a.shape, _mybir.dt.from_np(a.dtype), kind="ExternalInput").ap()
    (shape, dtype), = _OUTS
    out = nc.dram_tensor("out_0_dram", shape, _mybir.dt.from_np(_np.dtype(dtype)), kind="ExternalOutput").ap()
    metaformer(nc, aps['x'], aps['L0_conv_Wg'], aps['L0_conv_bg'],
               [[aps[n] for n in _INS[3:8]], [aps[n] for n in _INS[13:18]]],
               [aps[n] for n in _INS[8:13]], out)
    r = _run(nc, [arrays], core_ids=[0])
    return r.results[0]["out_0_dram"]
```

```python
from contextlib import ExitStack

import concourse.bass as bass
from concourse import mybir

F32 = mybir.dt.float32
F32R = mybir.dt.float32r
I32 = mybir.dt.int32
U32 = mybir.dt.uint32
ALU = mybir.AluOpType
ACT = mybir.ActivationFunctionType
AX_X = mybir.AxisListType.X

P = 128


def spread(ap, axis, n):
    wide = ap.unsqueeze(axis)
    shape = list(wide.shape)
    shape[axis] = n
    return wide.broadcast_to(shape)


def repeat(eng, trips, body):
    body(0)
    if trips > 1:
        with eng.Fori(1, trips) as i:
            body(i)


def repeat_to_last(eng, trips, body):
    body(0, True, trips == 1)
    if trips > 2:
        with eng.Fori(1, trips - 1) as i:
            body(i, False, False)
    if trips > 1:
        body(trips - 1, False, True)


def one(t, i):
    return t[:, bass.ds(i, 1), :].rearrange("p o c -> p (o c)")


def later(i):
    return not isinstance(i, int) or i > 0


class Order:

    def __init__(self, eng, sem):
        self.eng, self.sem, self.base, self.k, self.it, self.per = eng, sem, 0, 0, 0, 0

    def mark(self, ins):
        ins.then_inc(self.sem, 1)
        self.k += 1
        return ins

    def wait(self):
        self.eng.wait_ge(self.sem, self.it * self.per + (self.base + self.k))

    def trip(self, i, per):
        self.it, self.per, self.k = i, per, 0

    def end_trip(self):
        assert self.k == self.per, f"the body leaves {self.k} marks"

    def leave(self, trips):
        self.base, self.k, self.it, self.per = self.base + self.per * trips, 0, 0, 0


def metaformer(nc, x, conv_w, conv_b, moe_args, delta_args, out):
    B, C, H, W = x.shape
    L = H * W
    T = B * L
    NT = T // P
    CK = C // 2
    NG = conv_w.shape[0]
    GS = 4
    E = moe_args[0][0].shape[1]
    FF = moe_args[0][1].shape[2]
    FK = FF // P
    FH = FF // 2
    SLOT_TILES = 2 * NT + E - 1
    assert SLOT_TILES % 2 == 1
    REGION = T + P
    AHEAD = 2
    LISTED = SLOT_TILES + AHEAD

    with ExitStack() as top:
        def sb(name, shape, dt=F32, ctx=top):
            return ctx.enter_context(nc.sbuf_tensor(name, shape, dt))

        def ps(name, shape, dt=F32, ctx=top):
            return ctx.enter_context(nc.psum_tensor(name, shape, dt))

        def sem(name):
            return top.enter_context(nc.semaphore(name))

        def dram(name, shape, dt=F32):
            return nc.dram_tensor(name, shape, dt, kind="Internal").ap()

        expert_rows = dram("expert_rows", [E * REGION, C])
        slot_out = dram("slot_out", [SLOT_TILES * P, C])

        res = sb("res", [P, NT, C])
        ident = sb("ident", [P, P])
        ones = sb("ones", [P, P])
        before = sb("before", [P, P])
        mean_w = sb("mean_w", [CK, CK])
        zeros = sb("zeros", [P, C])
        expert_no = sb("expert_no", [P, E])
        tile_no = sb("tile_no", [P, LISTED])
        lane_no = sb("lane_no", [P, 1])
        eps = {e: sb(f"eps{n}", [P, 1]) for n, e in enumerate((1e-5, 1e-6))}
        mu_var = sb("mu_var", [P, NT, 2])
        rstd = sb("rstd", [P, NT])
        bn = sb("bn", [P, GS, 6])
        aggr = sb("aggr", [P, GS, 2])
        fence = sb("fence", [P, 1])
        prob = sb("prob", [P, NT, 2])
        slot = sb("slot", [P, NT, 2], U32)

        const_pool = sem("const_pool")
        with ExitStack() as c, nc.Block() as block:
            iota_i = sb("iota_i", [P, P], I32, c)

            @block.gpsimd
            def _(pool):
                order = Order(pool, const_pool)
                order.mark(pool.memset(ident[:], 0.0))
                order.mark(pool.memset(before[:], 1.0))
                order.mark(pool.memset(ones[:], 1.0))
                order.mark(pool.memset(zeros[:], 0.0))
                order.mark(pool.memset(mean_w[:], 1.0 / C))
                for e, t in eps.items():
                    order.mark(pool.memset(t[:], e))
                order.wait()
                order.mark(pool.affine_select(out=ident[:], in_=ident[:], compare_op=ALU.not_equal, fill=1.0,
                                              base=0, pattern=[[-1, P]], channel_multiplier=1))
                order.mark(pool.affine_select(out=before[:], in_=before[:], compare_op=ALU.is_gt, fill=0.0,
                                              base=0, pattern=[[1, P]], channel_multiplier=-1))
                for dst, n, step, mult in ((expert_no, E, 1, 0), (tile_no, LISTED, 1, 0), (lane_no, 1, 0, 1)):
                    order.mark(pool.iota(iota_i[:, 0:n], pattern=[[step, n]], base=0, channel_multiplier=mult))
                    order.wait()
                    order.mark(pool.tensor_copy(dst[:], iota_i[:, 0:n]))
                    order.wait()

        STATS_MARKS = 2 * GS + 1
        dve = sem("dve")
        stats_ready, std_ready = sem("stats_ready"), sem("std_ready")
        dve_marked = [0]
        deviations = [0, 0, 0]

        def dve_order(v):
            order = Order(v, dve)
            order.base = dve_marked[0]
            return order

        def dve_leaves(order):
            dve_marked[0] = order.base + order.k

        def group_stats(v, order, i):
            v.nop(nofuse=True)
            for u in range(GS):
                order.mark(v.bn_stats(bn[:, u, :], one(res, i * GS + u)))
            order.wait()
            v.tensor_copy(fence[:], lane_no[:])
            for u in range(GS):
                order.mark(v.bn_aggr(aggr[:, u, :], bn[:, u, :]))
            order.wait()
            order.mark(v.tensor_copy(mu_var[:, bass.ds(i * GS, GS), :], aggr[:]))

        def deviations_act(act, e, lo, hi, times=1):
            deviations[0] += 1
            act.wait_ge(stats_ready, deviations[0])
            act.activation(rstd[:, lo:hi], mu_var[:, lo:hi, 1], ACT.Sqrt, bias=eps[e][:, 0:1]).then_inc(std_ready, 1)
            deviations[1] += times

        def stats_done(v, order):
            order.wait()
            v.nop().then_inc(stats_ready, 1)

        def invert_deviations(v, lo, hi, times=1):
            v.wait_ge(std_ready, deviations[2] + 1)
            deviations[2] += times
            v.reciprocal(rstd[:, lo:hi], rstd[:, lo:hi])

        def deviations_dve(v, order, lo, hi):
            stats_done(v, order)
            invert_deviations(v, lo, hi)

        gate_in, total_psum, pad_ready, padded, exp_in, exp_done = [sem(s) for s in (
            "gate_in", "total_psum", "pad_ready", "padded", "exp_in", "exp_done")]

        class Gather:

            def __init__(self, n):
                self.gathered = [sem(f"gathered{u}_{n}") for u in range(4)]
                self.added, self.idx_set = sem(f"added{n}"), sem(f"idx_set{n}")

            def buffers(self, got, at_idx):
                self.got, self.at_idx = got, at_idx

            def fetch(self, pool, i):
                for u in range(4):
                    pool.wait_ge(self.idx_set, i * 4 + (u + 1))
                    pool.nop(nofuse=True)
                    for k in range(2):
                        pool.indirect_dma_start(self.got[:, u, k, :], None, slot_out,
                                                bass.IndirectOffsetOnAxis(self.at_idx[:, u, k:k + 1], 0)).then_inc(self.gathered[u], 16)

            def first_slots(self, v, i):
                for u in range(4):
                    v.tensor_copy(self.at_idx[:, u, :], slot[:, i * 4 + u, :]).then_inc(self.idx_set, 1)

            def add(self, v, order, i, last, stats, first=False):
                for u in range(4):
                    at = bass.ds(i * 4 + u, 1)
                    v.wait_ge(self.gathered[u], i * 32 + 32)
                    order.mark(v.scalar_tensor_tensor(one(res, i * 4 + u), self.got[:, u, 0, :], prob[:, at, 0], one(res, i * 4 + u),
                                                      ALU.mult, ALU.add))
                    order.wait()
                    v.scalar_tensor_tensor(one(res, i * 4 + u), self.got[:, u, 1, :], prob[:, at, 1], one(res, i * 4 + u),
                                           ALU.mult, ALU.add).then_inc(self.added, 1)
                    if not last:
                        v.wait_ge(self.added, i * 4 + (u + 1))
                        v.tensor_copy(self.at_idx[:, u, :], one(slot, i * 4 + (u + 4))).then_inc(self.idx_set, 1)
                if stats:
                    if not first:
                        order.wait()
                    if last:
                        v.wait_ge(self.added, i * 4 + 4)
                    group_stats(v, order, i)

        gathers = [Gather(n) for n in range(2)]

        def moe(n, act_fn, w1, w2, b2, w_sem, w_full, ctx, load, next_eps):
            gate_w = moe_args[n][0]
            nm = lambda s: f"{s}{n}"
            gate = sb(nm("gate"), [CK, 2, E], ctx=ctx)
            logits = sb(nm("logits"), [P, NT, E], ctx=ctx)
            best = sb(nm("best"), [P, NT, 1], ctx=ctx)
            pick = sb(nm("pick"), [P, NT, 2, E], ctx=ctx)
            rank = sb(nm("rank"), [P, NT, 2], ctx=ctx)
            listed = sb(nm("listed"), [P, 2, LISTED], U32, ctx=ctx)

            Q = 4
            RING = 4
            with ExitStack() as rc:
                xn = sb(nm("xn"), [P, RING, Q, C], ctx=rc)
                xnT = sb(nm("xnT"), [CK, 2, Q, P], ctx=rc)
                lg = sb(nm("lg"), [P, Q, E], ctx=rc)
                top8 = sb(nm("top8"), [P, Q, 8], ctx=rc)
                idx = sb(nm("idx"), [P, Q, 8], U32, ctx=rc)
                idf = sb(nm("idf"), [P, Q, 2], ctx=rc)
                taken = sb(nm("taken"), [P, Q, E], ctx=rc)
                carry = sb(nm("carry"), [P, Q + 1, E], ctx=rc)
                place = sb(nm("place"), [P, Q, E], ctx=rc)
                mine = sb(nm("mine"), [P, Q, 2, E], ctx=rc)
                rowf = sb(nm("rowf"), [P, Q, 2], ctx=rc)
                row = sb(nm("row"), [P, RING, Q, 2], U32, ctx=rc)
                total = sb(nm("total"), [P, E], ctx=rc)
                padf = sb(nm("padf"), [P, E], ctx=rc)
                pad = sb(nm("pad"), [P, E], U32, ctx=rc)
                tilesi = sb(nm("tilesi"), [P, E], I32, ctx=rc)
                tiles = sb(nm("tiles"), [P, E], ctx=rc)
                upto = sb(nm("upto"), [P, E], ctx=rc)
                base = sb(nm("base"), [P, E], ctx=rc)
                wide = sb(nm("wide"), [P, NT * 2, E], ctx=rc)
                past = sb(nm("past"), [P, LISTED, E], ctx=rc)
                skipped = sb(nm("skipped"), [P, LISTED, E], ctx=rc)
                lf = sb(nm("lf"), [P, 4, LISTED], ctx=rc)
                ex = sb(nm("ex"), [P, NT, E], ctx=rc)
                den = sb(nm("den"), [P, NT], ctx=rc)
                psT = ps(nm("psT"), [CK, 2, Q, P], ctx=rc)
                psL = ps(nm("psL"), [P, 2, 512], ctx=rc)
                psR = ps(nm("psR"), [P, 512], ctx=rc)
                (xn_ready, xnT_psum, xnT_ready, logits_psum, rank_psum, row_ready, carry_ready) = [sem(nm(s)) for s in (
                    "xn_ready", "xnT_psum", "xnT_ready", "logits_psum", "rank_psum", "row_ready", "carry_ready")]
                scattered = [sem(nm(f"scattered{u}_")) for u in range(RING)]
                TRIPS = NT // (RING * Q)
                with nc.Block() as block:
                    @block.sync
                    def _(sp):
                        sp.dma_start(gate[:], gate_w.rearrange("(k c) e -> c k e", k=2)).then_inc(gate_in, 16)

                    @block.tensor
                    def _(pe):
                        pe.wait_ge(gate_in, 16 * (n + 1))

                        def score(g, u):
                            pe.wait_ge(xn_ready, g * Q + Q)
                            for q in range(Q):
                                for k in range(2):
                                    last = pe.transpose(psT[:, k, q, :], xn[:, u, q, k * CK:(k + 1) * CK], ident[:])
                            last.then_inc(xnT_psum, 1)
                            pe.wait_ge(xnT_ready, g + 1)
                            for q in range(Q):
                                for k in range(2):
                                    last = pe.matmul(psL[:, u % 2, q * E:(q + 1) * E], xnT[:, k, q, :], gate[:, k, :],
                                                     start=k == 0, stop=k == 1)
                            last.then_inc(logits_psum, 1)

                        def body(i, first, last):
                            for u in range(RING):
                                pe.wait_ge(carry_ready, i * RING + (u + 1))
                                pe.matmul(psR[:, 0:Q * E], before[:], taken[:].rearrange("p q e -> p (q e)"),
                                          start=True, stop=False)
                                pe.matmul(psR[:, 0:Q * E], ones[:], carry[:, 0:Q, :].rearrange("p q e -> p (q e)"),
                                          start=False, stop=True).then_inc(rank_psum, 1)
                                if first and u == 0:
                                    score(1, 1)
                                if not (last and u >= RING - 2):
                                    score(i * RING + (u + 2), (u + 2) % RING)
                        score(0, 0)
                        repeat_to_last(pe, TRIPS, body)
                        pe.wait_ge(row_ready, RING * TRIPS)
                        pe.matmul(psR[:, 0:E], ones[:], carry[:, Q, :], start=True, stop=True).then_inc(total_psum, 1)

                    @block.scalar
                    def _(act):
                        if load:
                            load(act)

                        def body(i):
                            for u in range(RING):
                                act.wait_ge(xnT_psum, i * RING + (u + 1))
                                act.activation(xnT[:], psT[:], ACT.Copy).then_inc(xnT_ready, 1)
                        repeat(act, TRIPS, body)
                        act.wait_ge(exp_in, n + 1)
                        act.activation(ex[:], ex[:], ACT.Exp).then_inc(exp_done, 1)

                    @block.gpsimd
                    def _(pool):
                        def body(i):
                            for u in range(RING):
                                pool.wait_ge(row_ready, i * RING + (u + 1))
                                pool.nop(nofuse=True)
                                for q in range(Q):
                                    for k in range(2):
                                        pool.indirect_dma_start(
                                            expert_rows, bass.IndirectOffsetOnAxis(row[:, u, q, k:k + 1], 0),
                                            xn[:, u, q, :], None).then_inc(scattered[u], 16)
                        repeat(pool, TRIPS, body)
                        pool.wait_ge(pad_ready, n + 1)
                        for e in range(E):
                            pool.indirect_dma_start(expert_rows, bass.IndirectOffsetOnAxis(pad[:, e:e + 1], 0),
                                                    zeros[:], None).then_inc(padded, 16)
                        for u in range(RING):
                            pool.wait_ge(scattered[u], TRIPS * Q * 2 * 16)
                        pool.wait_ge(padded, E * 16 * (n + 1))

                    @block.vector
                    def _(v):
                        order = dve_order(v)
                        order.mark(v.memset(carry[:], 0.0))
                        order.base += 1
                        order.leave(0)

                        def normalise(i, u, first):
                            at_ring, trip = u % RING, i + u // RING
                            if u >= RING or not first:
                                v.wait_ge(scattered[at_ring], trip * (Q * 2 * 16))
                            for q in range(Q):
                                tile = i * (RING * Q) + (u * Q + q)
                                at = bass.ds(tile, 1)
                                v.tensor_scalar(xn[:, at_ring, q, :], one(res, tile), mu_var[:, at, 0], rstd[:, at],
                                                ALU.subtract, ALU.mult).then_inc(xn_ready, 1)

                        def body(i, first, last):
                            order.trip(i, RING * (3 * Q + 11))
                            for u in range(RING):
                                g = i * RING + u
                                if not (last and u >= RING - 2):
                                    normalise(i, u + 2, first)
                                group = bass.ds(g * Q, Q)
                                v.wait_ge(logits_psum, g + 1)
                                order.mark(v.tensor_copy(lg[:], psL[:, u % 2, 0:Q * E].rearrange("p (q e) -> p q e", q=Q)))
                                order.wait()
                                order.mark(v.tensor_copy(logits[:, group, :], lg[:]))
                                for q in range(Q):
                                    order.mark(v.max(top8[:, q, :], lg[:, q, :]))
                                order.wait()
                                order.mark(v.tensor_copy(best[:, group, :], top8[:, :, 0:1]))
                                for q in range(Q):
                                    order.mark(v.max_index(idx[:, q, :], top8[:, q, :], lg[:, q, :]))
                                order.wait()
                                order.mark(v.tensor_copy(idf[:], idx[:, :, 0:2]))
                                order.wait()
                                chosen = pick[:, group, :, :]
                                order.mark(v.tensor_tensor(
                                    chosen.rearrange("p q k e -> p (q k) e"), spread(expert_no[:], 1, 2 * Q),
                                    spread(idf[:].rearrange("p q k -> p (q k)"), 2, E), ALU.is_equal))
                                order.wait()
                                if not first or u:
                                    v.wait_ge(rank_psum, g)
                                order.mark(v.tensor_tensor(taken[:], pick[:, group, 0, :], pick[:, group, 1, :], ALU.add))
                                order.mark(v.tensor_copy(carry[:, 0, :], carry[:, Q, :]))
                                order.wait()
                                for q in range(Q):
                                    order.mark(v.tensor_tensor(carry[:, q + 1, :], carry[:, q, :], taken[:, q, :], ALU.add))
                                    order.wait()
                                v.nop().then_inc(carry_ready, 1)
                                v.wait_ge(rank_psum, g + 1)
                                order.mark(v.tensor_copy(place[:], psR[:, 0:Q * E].rearrange("p (q e) -> p q e", q=Q)))
                                order.wait()
                                order.mark(v.tensor_tensor(mine[:], spread(place[:], 2, 2), chosen, ALU.mult))
                                order.wait()
                                order.mark(v.tensor_reduce(rank[:, group, :], mine[:], AX_X, ALU.add))
                                order.wait()
                                order.mark(v.scalar_tensor_tensor(rowf[:], idf[:], float(REGION), rank[:, group, :],
                                                                  ALU.mult, ALU.add))
                                order.wait()
                                v.tensor_copy(row[:, u, :, :], rowf[:]).then_inc(row_ready, 1)
                            order.end_trip()
                        normalise(0, 0, True)
                        normalise(0, 1, True)
                        repeat_to_last(v, TRIPS, body)
                        order.leave(TRIPS)

                        def step(ins):
                            order.mark(ins)
                            order.wait()
                        v.tensor_tensor(ex[:], logits[:], best[:].broadcast_to([P, NT, E]),
                                        ALU.subtract).then_inc(exp_in, 1)
                        v.wait_ge(total_psum, n + 1)
                        step(v.tensor_copy(total[:], psR[:, 0:E]))
                        step(v.scalar_tensor_tensor(padf[:], expert_no[:], float(REGION), total[:], ALU.mult, ALU.add))
                        step(v.tensor_scalar(padf[:], padf[:], lane_no[:, 0:1], None, ALU.add))
                        v.tensor_copy(pad[:], padf[:]).then_inc(pad_ready, 1)
                        step(v.tensor_scalar(tiles[:], total[:], float(P - 1), None, ALU.add))
                        step(v.tensor_copy(tilesi[:], tiles[:]))
                        step(v.tensor_scalar(tilesi[:], tilesi[:], P.bit_length() - 1, None, ALU.arith_shift_right))
                        step(v.tensor_copy(tiles[:], tilesi[:]))
                        step(v.tensor_tensor_scan(upto[:], ones[:, 0:E], tiles[:], 0.0, ALU.mult, ALU.add))
                        step(v.tensor_tensor(base[:], upto[:], tiles[:], ALU.subtract))
                        step(v.tensor_scalar(base[:], base[:], float(P), None, ALU.mult))
                        step(v.tensor_tensor(wide[:], pick[:].rearrange("p t k e -> p (t k) e"), spread(base[:], 1, 2 * NT), ALU.mult))
                        step(v.tensor_reduce(prob[:].rearrange("p t k -> p (t k)"), wide[:], AX_X, ALU.add))
                        step(v.tensor_tensor(rank[:], rank[:], prob[:], ALU.add))
                        step(v.tensor_copy(slot[:], rank[:]))
                        step(v.tensor_tensor(past[:], spread(tile_no[:], 2, E), spread(upto[:], 1, LISTED), ALU.is_ge))
                        step(v.tensor_reduce(lf[:, 0, :], past[:], AX_X, ALU.add))
                        step(v.tensor_tensor(skipped[:], past[:], spread(tiles[:], 1, LISTED), ALU.mult))
                        step(v.tensor_reduce(lf[:, 1, :], skipped[:], AX_X, ALU.add))
                        step(v.tensor_tensor(lf[:, 1, :], tile_no[:], lf[:, 1, :], ALU.subtract))
                        step(v.tensor_scalar(lf[:, 2, :], lf[:, 0, :], float(REGION // P), None, ALU.mult))
                        step(v.tensor_tensor(lf[:, 1, :], lf[:, 1, :], lf[:, 2, :], ALU.add))
                        step(v.tensor_scalar(lf[:, 3, :], lf[:, 0, :], float(E), None, ALU.is_lt))
                        step(v.tensor_tensor(lf[:, 0, :], lf[:, 0, :], lf[:, 3, :], ALU.mult))
                        step(v.tensor_tensor(lf[:, 1, :], lf[:, 1, :], lf[:, 3, :], ALU.mult))
                        step(v.tensor_copy(listed[:], lf[:, 0:2, :]))
                        v.wait_ge(exp_done, n + 1)
                        step(v.tensor_reduce(den[:], ex[:], AX_X, ALU.add))
                        step(v.reciprocal(den[:], den[:]))
                        step(v.tensor_tensor(wide[:].rearrange("p (t k) e -> p t k e", k=2), pick[:], spread(ex[:], 2, 2), ALU.mult))
                        step(v.tensor_reduce(prob[:].rearrange("p t k -> p (t k)"), wide[:], AX_X, ALU.add))
                        step(v.tensor_tensor(prob[:], prob[:], spread(den[:], 2, 2), ALU.mult))
                        dve_leaves(order)

            with ExitStack() as tc:
                xt = sb(nm("xt"), [P, 2, C], ctx=tc)
                xT_hi = sb(nm("xT_hi"), [CK + 1, 2, 2, P], F32R, ctx=tc)
                xT_lo = sb(nm("xT_lo"), [CK, 2, 2, P], F32R, ctx=tc)
                w1_hi = sb(nm("w1_hi"), [CK + 1, 2, E, FF], F32R, ctx=tc)
                h = sb(nm("h"), [P, 2, FF], ctx=tc)
                hT = sb(nm("hT"), [P, 2, FK, P], ctx=tc)
                y = sb(nm("y"), [P, 2, C], ctx=tc)
                psX = ps(nm("psX"), [CK, 2, P], ctx=tc)
                psU = ps(nm("psU"), [P, 2, 512], ctx=tc)
                psH = ps(nm("psH"), [P, 2, 512], ctx=tc)
                psY = ps(nm("psY"), [P, 512], ctx=tc)
                (x_lo_ready, split, xT_psum, xT_ready, up_psum, h_ready, hT_psum, hT_ready, y_psum, y_ready, ones_set) = [
                    sem(nm(s)) for s in ("x_lo_ready", "split", "xT_psum", "xT_ready", "up_psum", "h_ready", "hT_psum", "hT_ready", "y_psum",
                                         "y_ready", "ones_set")]
                x_in = [sem(nm(f"x_in{u}_")) for u in range(2)]
                y_out = [sem(nm(f"y_out{u}_")) for u in range(2)]
                TRIPS = SLOT_TILES // 2
                LAST = SLOT_TILES - 1
                rows_of_tiles = expert_rows.rearrange("(t p) c -> t p c", p=P)
                out_tiles = slot_out.rearrange("(t p) c -> t p c", p=P)

                def split_weights(eng, e):
                    for k in range(2):
                        n_k = CK + 1 - k
                        eng.tensor_copy(w1_hi[0:n_k, k, e, :], w1[0:n_k, k, e, :]).then_inc(split, 1)
                        eng.wait_ge(split, 4 * e + 2 * k + 1)
                        eng.tensor_tensor(w1[0:n_k, k, e, :].bitcast(F32R), w1[0:n_k, k, e, :],
                                          w1_hi[0:n_k, k, e, :].bitcast(F32), ALU.subtract).then_inc(split, 1)

                with nc.Block() as block:
                    @block.sync
                    def _(sp):
                        def load(tile, u):
                            r = sp.value_load(listed[0:1, 1, bass.ds(tile, 1)], min_val=0, max_val=E * REGION // P - 1)
                            sp.dma_start(xt[:, u, :], rows_of_tiles[bass.ds(r, 1), :, :].rearrange("t p c -> (t p) c")).then_inc(x_in[u], 16)
                        for u in range(2):
                            load(u, u)

                        def store(tile, u):
                            sp.wait_ge(y_ready, tile + 1)
                            sp.nop(nofuse=True)
                            sp.dma_start(out_tiles[bass.ds(tile, 1), :, :].rearrange("t p c -> (t p) c"), y[:, u, :]).then_inc(y_out[u], 16)

                        def body(i):
                            for u in range(2):
                                sp.wait_ge(xT_psum, i * 2 + (u + 1))
                                load(i * 2 + (u + 2), u)
                                if later(i) or u:
                                    store(i * 2 + (u - 1), 1 - u)
                        repeat(sp, TRIPS, body)
                        store(LAST - 1, 1)
                        store(LAST, 0)
                        for u in range(2):
                            sp.wait_ge(x_in[u], 16 * (TRIPS + 1))
                            sp.wait_ge(y_out[u], 16 * (TRIPS + 1 - u))

                    @block.tensor
                    def _(pe):
                        pe.wait_ge(w_sem, w_full)
                        pe.wait_ge(ones_set, 1)

                        def turn_x(tile, u, trip):
                            pe.wait_ge(x_in[u], trip * 16 + 16)
                            for k in range(2):
                                last = pe.transpose(psX[:, k, :], xt[:, u, k * CK:(k + 1) * CK], ident[:])
                            last.then_inc(xT_psum, 1)

                        def expert(tile):
                            return pe.value_load(listed[0:1, 0, bass.ds(tile, 1)], min_val=0, max_val=E - 1)

                        def up(tile, u, e, first=False):
                            pe.wait_ge(x_lo_ready, tile + 1)
                            pe.wait_ge(split, e * 4 + 4)
                            if not first:
                                pe.wait_ge(h_ready, tile)
                            for f in range(2):
                                cols = slice(f * FH, (f + 1) * FH)
                                for k in range(2):
                                    n_k = CK + 1 - k
                                    pe.matmul(psU[:, f, 0:FH], xT_hi[0:n_k, u, k, :], w1_hi[0:n_k, k, bass.ds(e, 1), cols],
                                              start=k == 0, stop=False)
                                    pe.matmul(psU[:, f, 0:FH], xT_hi[0:n_k, u, k, :], w1[0:n_k, k, bass.ds(e, 1), cols].bitcast(F32R),
                                              start=False, stop=False)
                                    last = pe.matmul(psU[:, f, 0:FH], xT_lo[0:CK, u, k, :], w1_hi[0:CK, k, bass.ds(e, 1), cols],
                                                     start=False, stop=k == 1)
                            last.then_inc(up_psum, 1)

                        turn_x(0, 0, 0)
                        pe.wait_ge(x_lo_ready, 1)
                        turn_x(1, 1, 0)
                        up(0, 0, expert(0), first=True)

                        def turn_hidden(tile, u, first=False):
                            pe.wait_ge(h_ready, tile + 1)
                            if not first:
                                pe.wait_ge(hT_ready, tile)
                            for k in range(FK):
                                last = pe.transpose(psH[:, k // 3, (k % 3) * P:(k % 3 + 1) * P],
                                                    h[:, u, k * P:(k + 1) * P], ident[:])
                            last.then_inc(hT_psum, 1)

                        def down(tile, u, e, first=False):
                            pe.wait_ge(hT_ready, tile + 1)
                            if not first:
                                pe.wait_ge(y_ready, tile)
                            for k in range(FK):
                                last = pe.matmul(psY[:, 0:C], hT[:, u, k, :], w2[:, k, bass.ds(e, 1), :],
                                                 start=k == 0, stop=k == FK - 1)
                            last.then_inc(y_psum, 1)

                        def body(i):
                            for u in range(2):
                                tile = i * 2 + u
                                e_next, e = expert(tile + 1), expert(tile)
                                turn_hidden(tile, u, first=not later(i) and not u)
                                pe.wait_ge(x_lo_ready, tile + 2)
                                turn_x(tile + 2, u, i + 1)
                                up(tile + 1, 1 - u, e_next)
                                down(tile, u, e, first=not later(i) and not u)
                        repeat(pe, TRIPS, body)
                        e = expert(LAST)
                        turn_hidden(LAST, 0)
                        down(LAST, 0, e)

                    @block.scalar
                    def _(act):
                        def turn(tile, u):
                            act.wait_ge(xT_psum, tile + 1)
                            act.activation(xT_hi[0:CK, u, :, :], psX[:], ACT.Copy).then_inc(xT_ready, 1)

                        def hidden(tile, u):
                            act.wait_ge(up_psum, tile + 1)
                            act.activation(h[:, u, :].rearrange("p (f m) -> p f m", f=2), psU[:, :, 0:FH], act_fn).then_inc(h_ready, 1)
                        turn(0, 0)
                        turn(1, 1)
                        hidden(0, 0)

                        def body(i):
                            for u in range(2):
                                act.wait_ge(up_psum, i * 2 + (u + 1))
                                turn(i * 2 + (u + 2), u)
                                hidden(i * 2 + (u + 1), 1 - u)
                        repeat(act, TRIPS, body)

                    @block.vector
                    def _(v):
                        v.tensor_copy(xT_hi[CK:CK + 1, :, 0, :], spread(ones[CK:CK + 1, :], 1, 2)).then_inc(ones_set, 1)

                        def x_rest(tile, u):
                            v.wait_ge(xT_ready, tile + 1)
                            v.tensor_tensor(xT_lo[:, u, :, :], psX[:], xT_hi[0:CK, u, :, :].bitcast(F32), ALU.subtract).then_inc(x_lo_ready, 1)
                        v.wait_ge(w_sem, w_full)
                        split_weights(v, 0)
                        x_rest(0, 0)
                        x_rest(1, 1)

                        def copy_hidden(tile, u):
                            v.wait_ge(hT_psum, tile + 1)
                            v.tensor_copy(hT[:, u, :, :].rearrange("p (a b) t -> p a (b t)", a=2),
                                          psH[:, :, 0:FH]).then_inc(hT_ready, 1)

                        def add_bias(tile, u, stored):
                            e = v.value_load(listed[0:1, 0, bass.ds(tile, 1)], min_val=0, max_val=E - 1)
                            v.wait_ge(y_psum, tile + 1)
                            if stored is not None:
                                v.wait_ge(y_out[u], stored * 16)
                            v.tensor_tensor(y[:, u, :], psY[:, 0:C], b2[:, bass.ds(e, 1), :].rearrange("p o c -> p (o c)"), ALU.add).then_inc(y_ready, 1)

                        def body(i):
                            for u in range(2):
                                tile = i * 2 + u
                                copy_hidden(tile, u)
                                x_rest(tile + 2, u)
                                add_bias(tile, u, i if later(i) else None)
                        repeat(v, TRIPS, body)
                        copy_hidden(LAST, 0)
                        add_bias(LAST, 0, TRIPS)

                    @block.gpsimd
                    def _(pool):
                        pool.wait_ge(split, 4)
                        for e in range(1, E):
                            split_weights(pool, e)

            with ExitStack() as gc:
                gather = gathers[n]
                gather.buffers(sb(nm("got"), [P, 4, 2, C], ctx=gc), sb(nm("at_idx"), [P, 4, 2], U32, ctx=gc))
                added = gather.added
                tiles_here = NT // 2 if next_eps else NT
                oc = sb(nm("oc"), [CK, 2, 2, L], ctx=gc)
                ps_o = ps(nm("ps_o"), [CK, 2, 2, L], ctx=gc)
                if not next_eps:
                    o_turned, o_copied = sem("o_turned"), sem("o_copied")
                    o_out = [sem(f"o_out{u}") for u in range(2)]
                TRIPS = tiles_here // 4
                with nc.Block() as block:
                    @block.gpsimd
                    def _(pool):
                        repeat(pool, TRIPS, lambda i: gather.fetch(pool, i))

                    @block.vector
                    def _(v):
                        order = dve_order(v)
                        gather.first_slots(v, 0)

                        def body(i, first, last):
                            order.trip(i, GS + (STATS_MARKS if next_eps else 0))
                            gather.add(v, order, i, last, bool(next_eps), first)
                        repeat_to_last(v, TRIPS, body)
                        order.leave(TRIPS)
                        if next_eps:
                            deviations_dve(v, order, 0, tiles_here)
                        dve_leaves(order)

                    if next_eps:
                        @block.scalar
                        def _(act):
                            deviations_act(act, next_eps, 0, tiles_here)
                    else:
                        @block.tensor
                        def _(pe):
                            for b in range(B):
                                pe.wait_ge(added, 2 * b + 2)
                                if b >= 2:
                                    pe.wait_ge(o_copied, b - 1)
                                for k in range(2):
                                    for s in range(2):
                                        last = pe.transpose(ps_o[:, b % 2, k, s * P:(s + 1) * P],
                                                            res[:, 2 * b + s, k * CK:(k + 1) * CK], ident[:])
                                last.then_inc(o_turned, 1)

                        @block.scalar
                        def _(act):
                            def body(i):
                                for b in range(2):
                                    act.wait_ge(o_turned, i * 2 + (b + 1))
                                    if later(i):
                                        act.wait_ge(o_out[b], i * 32)
                                    act.activation(oc[:, b, :, :], ps_o[:, b, :, :], ACT.Copy).then_inc(o_copied, 1)
                            repeat(act, TRIPS, body)

                        @block.sync
                        def _(sp):
                            def body(i):
                                for b in range(2):
                                    sp.wait_ge(o_copied, i * 2 + (b + 1))
                                    sp.nop(nofuse=True)
                                    for k in range(2):
                                        sp.dma_start(out[bass.ds(i * 2 + b, 1), k * CK:(k + 1) * CK, :, :].rearrange("b c h w -> (b c) (h w)"),
                                                     oc[:, b, k, :]).then_inc(o_out[b], 16)
                            repeat(sp, TRIPS, body)
                            for b in range(2):
                                sp.wait_ge(o_out[b], 32 * TRIPS)

        def delta(ctx):
            wq, wk, wv, wb, wo = delta_args
            NH = wb.shape[1]
            D = C // NH
            K = 16
            HB = P // (L // K)
            HALVES = B // HB
            HT = NT // HALVES
            HC = NH // 2
            X = K + K
            NCH = L // K
            w_all = sb("w_all", [CK, 2, 3 * C + NH], ctx=ctx)
            w_o = sb("w_o", [CK, 2, C], ctx=ctx)
            blocks = sb("blocks", [CK, HC, D], ctx=ctx)
            area1 = sb("area1", [P, 2 * K * P], ctx=ctx)
            tT = area1[0:CK, :].rearrange("c (k t) -> c k t", k=2)
            oT = tT
            y_rows = area1[:, 0:K * C].rearrange("p (t c) -> p t c", t=K)
            area2 = sb("area2", [P, K * 3 * C], ctx=ctx)
            qkv = area2[:].rearrange("p (t c) -> p t c", t=K)
            o_sys = area2[:, 0:K * C].rearrange("p (t c) -> p t c", t=K)
            uo_sys = area2[:, K * C:3 * K * C].rearrange("p (f x c) -> p f x c", f=2, x=X)
            z = sb("z", [P, K, 2 * C], ctx=ctx)
            zv = z[:].rearrange("p t (h d x) -> p t h d x", d=D, x=2)
            wqT = sb("wqT", [CK, 2, P, X], ctx=ctx)
            AREA3 = max(4 * 8 * CK + 4 * C, 2 * HB * X + 4 * C + 2 * C + 16 * CK)
            area3 = sb("area3", [P, AREA3], ctx=ctx)
            k_blk = area3[0:CK, 0:4 * 8 * CK].rearrange("c (u p m) -> c u p m", u=4, p=8)
            kq_out = area3[:, 4 * 8 * CK:4 * 8 * CK + 4 * C].rearrange("p (u g c) -> p u g c", u=2, g=4)
            at = 0

            def cut(n):
                nonlocal at
                at += n
                return area3[:, at - n:at]
            wq_n = cut(2 * HB * X)[0:CK, :].rearrange("c (u b x) -> c u b x", u=2, b=HB)
            yk = cut(2 * 2 * C).rearrange("p (u b m) -> p u b m", u=2, b=2)
            uo = cut(2 * C).rearrange("p (u b m) -> p u b m", u=2, b=2)
            s_blk = cut(4 * 4 * CK)[0:CK, :].rearrange("c (j g m) -> c j g m", j=4, g=4)
            assert at <= AREA3
            kp = sb("kp", [P, 2, X, HC, K], ctx=ctx)
            tmp = sb("tmp", [P, HC * X * K], ctx=ctx)
            at_idx = sb("at_idx_d", [P, 4, 2], U32, ctx=ctx)
            gathers[0].buffers(tmp[:, 2 * 4 * C:4 * 4 * C].rearrange("p (u k c) -> p u k c", u=4, k=2), at_idx)
            tn = tmp[:, 0:2 * 4 * C].rearrange("p (u q c) -> p u q c", u=2, q=4)
            red = sb("red", [P, C], ctx=ctx)
            ss = sb("ss", [P, K, 2 * NH], ctx=ctx)
            beta = sb("beta", [P, K, NH], ctx=ctx)
            bank = ps("bank", [P, 8, 512], ctx=ctx)
            kq_rows = dram("kq_rows", [HALVES * 2, P // 4, P, CK])
            yk_rows = dram("yk_rows", [HALVES * 2, NCH, P, 2 * 2 * CK])
            uo_rows = dram("uo_rows", [HALVES * 2, NCH, 2, P, CK])

            names = ("d_weights", "d_blocks", "d_pool", "half_open", "t_ready", "t_turned", "t_copied", "proj_psum",
                     "proj_act", "beta_copied", "squares", "norms", "gates", "kq_turned", "kq_copied", "kblk_dve",
                     "kblk_pool", "kk_psum", "kk_copied", "k_out", "z_ready", "w_turned", "w_copied", "w_copied_dve",
                     "y_copied", "masked", "pool_products", "y_out", "s_zero", "s_ready", "wq_ready", "ws_psum", "uo_ready", "s_psum", "uo_in",
                     "o_ready", "o_turned_d", "o_copied_d", "y_psum_d", "y_added", "z_rows", "t_added", "wq_free")
            S = {s: sem(s) for s in names}
            kp_in = [sem(f"kp_in{x}") for x in range(2)]
            yk_in = [sem(f"yk_in{u}") for u in range(2)]
            uo_out = [sem(f"uo_out{u}") for u in range(2)]
            kk_out = [sem(f"kk_out{u}_") for u in range(2)]
            heads_of = lambda ap: ap.rearrange("p (h d) -> p h d", d=D)
            heads = lambda ap: ap.rearrange("p t (h d) -> p t h d", d=D)

            NC = P // 8

            def by_pool(k, c):
                return k == 1 or c % 3 == 2

            def expanded_by(pools, k, c):
                return sum(by_pool(k_, c_) == pools for k_ in range(2) for c_ in range(NC) if (k_, c_) <= (k, c))

            def expand_keys(eng, hb, k, c, ready):
                n = k * NC + c
                if n >= 4:
                    eng.wait_ge(S["kk_psum"], hb * (2 * NC) + (n - 3))
                eng.tensor_tensor(k_blk[:, n % 4, :, :].rearrange("c p (h t) -> c p h t", h=HC),
                                  spread(wqT[:, k, 8 * c:8 * c + 8, 0:K], 2, HC), spread(blocks[:], 1, 8),
                                  ALU.mult).then_inc(ready, 1)

            SOLVE_HEADS, OUT_HEADS = 3, 4
            SHARED = 11
            POOL_PRODUCTS = K - SHARED + K - 1 + K

            def solve_product(eng, f, i, lo, hi):
                return eng.tensor_tensor(tmp[:, lo * X * i:hi * X * i].rearrange("p (h x j) -> p h x j", h=hi - lo, x=X),
                                         spread(kp[:, f, i, lo:hi, 0:i], 2, X),
                                         z[:, 0:i, f * C + lo * X:f * C + hi * X].rearrange("p j (h x) -> p h x j", x=X), ALU.mult)

            def out_product(eng, f, m, i, lo, hi):
                n_j = 2 * m + 2
                at = i * CK * n_j
                return eng.tensor_tensor(tmp[:, at + lo * D * n_j:at + hi * D * n_j].rearrange("p (h e j) -> p h e j", h=hi - lo, e=D),
                                         spread(kp[:, f, K + 2 * m + i, lo:hi, 0:n_j], 2, D),
                                         uo_sys[:, f, 0:n_j, lo * D:hi * D].rearrange("p j (h e) -> p h e j", h=hi - lo), ALU.mult)

            with nc.Block() as block:
                @block.gpsimd
                def _(pool):
                    order = Order(pool, S["d_pool"])
                    order.mark(pool.memset(blocks[:], 1.0))
                    order.wait()
                    order.mark(pool.affine_select(out=blocks[:], in_=blocks[:], compare_op=ALU.is_ge, fill=0.0, base=0,
                                                  pattern=[[-D, HC], [0, D]], channel_multiplier=1))
                    order.wait()
                    pool.affine_select(out=blocks[:], in_=blocks[:], compare_op=ALU.is_ge, fill=0.0, base=D - 1,
                                       pattern=[[D, HC], [0, D]], channel_multiplier=-1).then_inc(S["d_blocks"], 1)
                    pool.wait_ge(S["d_blocks"], 1)
                    with pool.Fori(HT // 4, NT // 4) as i:
                        gathers[0].fetch(pool, i)
                    with pool.Fori(0, HALVES) as hb:
                        pool.wait_ge(S["kq_copied"], hb * K + K)
                        for k in range(2):
                            for c in range(NC):
                                if by_pool(k, c):
                                    expand_keys(pool, hb, k, c, S["kblk_pool"])
                        pool.wait_ge(S["kk_psum"], hb * (2 * NC) + 2 * NC)
                        for u in range(2):
                            pool.wait_ge(kk_out[u], hb * (16 * NC // 2) + 16 * NC // 2)
                        pool.nop(nofuse=True)
                        pool.memset(s_blk[:], 0.0).then_inc(S["s_zero"], 1)
                        pool.wait_ge(kp_in[0], hb * 32 + 32)
                        pool.wait_ge(S["gates"], hb + 1)
                        pool.tensor_tensor(kp[:, 1, 0:K, :, :], kp[:, 1, 0:K, :, :], spread(beta[:, :, HC:NH], 3, K), ALU.mult).then_inc(S["masked"], 1)
                        pool.wait_ge(kp_in[1], hb * 32 + 32)
                        pool.nop(nofuse=True)
                        for f in range(2):
                            pool.affine_select(out=kp[:, f, K:X, :, :], in_=kp[:, f, K:X, :, :], compare_op=ALU.is_ge, fill=0.0, base=0,
                                               pattern=[[1, K], [0, HC], [-1, K]], channel_multiplier=0).then_inc(S["masked"], 1)
                        for f, i in [(0, i) for i in range(SHARED, K)] + [(1, i) for i in range(1, K)]:
                            pool.wait_ge(S["z_ready"], (hb * 2 + f) * K + i)
                            solve_product(pool, f, i, SOLVE_HEADS, HC).then_inc(S["pool_products"], 1)
                        pool.wait_ge(S["masked"], hb * 3 + 3)
                        pool.wait_ge(S["z_ready"], (hb * 2 + 2) * K)
                        for f in range(2):
                            pool.wait_ge(S["uo_in"], (hb * 2 + (f + 1)) * 128)
                            for m in range(K // 2):
                                if f or m:
                                    pool.wait_ge(S["o_ready"], hb * K + (f * (K // 2) + m))
                                for i in range(2):
                                    last = out_product(pool, f, m, i, OUT_HEADS, HC)
                                last.then_inc(S["pool_products"], 1)

                @block.sync
                def _(sp):
                    for n, w in enumerate((wq, wk, wv, wb)):
                        sp.dma_start(w_all[:, :, n * C:n * C + w.shape[1]], w.rearrange("(k c) o -> c k o", k=2)).then_inc(S["d_weights"], 16)
                    sp.dma_start(w_o[:], wo.rearrange("(k c) o -> c k o", k=2)).then_inc(S["d_weights"], 16)
                    for hf in range(HALVES * 2):
                        for j in range(4):
                            for b in range(2):
                                sp.dma_start(yk_rows[hf, :, X * j + K:X * j + X, b * C:(b + 1) * C],
                                             spread(zeros[0:NCH, :], 1, K)).then_inc(S["z_rows"], 16)
                    sp.wait_ge(S["z_rows"], 16 * HALVES * 2 * 4 * 2)
                    with sp.Fori(0, HALVES) as hb:
                        def key_rows(f, b, j, part):
                            lo = (2 * b + part) * CK
                            return yk_rows[bass.ds(hb * 2 + f, 1), :, X * j:X * j + K, lo:lo + CK].rearrange("o n x c -> (o n) x c")
                        sp.wait_ge(S["norms"], hb * 5 + 5)
                        sp.nop(nofuse=True)
                        for f in range(2):
                            for b in range(2):
                                for j in range(4):
                                    p0 = (b * 4 + j) * NCH
                                    sp.dma_start(key_rows(f, b, j, 1), qkv[p0:p0 + NCH, :, C + f * CK:C + (f + 1) * CK]).then_inc(S["k_out"], 16)
                        for f in range(2):
                            sc = hb * 2 + f
                            for c in range(NC // 2):
                                u = c % 2
                                sp.wait_ge(S["kk_copied"], sc * NC + (2 * c + 2))
                                sp.nop(nofuse=True)
                                sp.dma_start(kq_rows[bass.ds(hb * 2 + f, 1), 4 * c:4 * c + 4, :, :].rearrange("o g p c -> (o p) g c"),
                                             kq_out[:, u, :, :]).then_inc(kk_out[u], 16)
                            for u in range(2):
                                sp.wait_ge(kk_out[u], sc * (4 * NC) + 4 * NC)
                            if f:
                                for x in range(2):
                                    sp.wait_ge(kp_in[x], hb * 32 + 16)
                            sp.nop(nofuse=True)
                            chunk_rows = kq_rows[bass.ds(hb * 2 + f, 1), :, :, :].rearrange("o g (j x) c -> (o g j) x c", j=4)
                            for x in range(2):
                                sp.dma_start(kp[:, f, x * K:(x + 1) * K, :, :].rearrange("p x h t -> p (x h t)"),
                                             chunk_rows[:, x * K:(x + 1) * K, :].rearrange("p x c -> p (x c)")).then_inc(kp_in[x], 16)
                        for f in range(2):
                            sc = hb * 2 + f
                            sp.wait_ge(S["y_copied"], sc + 1)
                            sp.nop(nofuse=True)
                            for b in range(2):
                                for j in range(4):
                                    p0 = (b * 4 + j) * NCH
                                    sp.dma_start(key_rows(f, b, j, 0), y_rows[p0:p0 + NCH, :, f * CK:(f + 1) * CK]).then_inc(S["y_out"], 16)
                            sp.wait_ge(S["y_out"], sc * 128 + 128)
                            sp.wait_ge(S["k_out"], hb * 256 + 256)
                            sp.nop(nofuse=True)

                            def load(n, u):
                                sp.dma_start(yk[:, u, :, :].rearrange("p b m -> p (b m)"),
                                             yk_rows[bass.ds(hb * 2 + f, 1), bass.ds(n, 1), :, :].rearrange("o n p m -> (o n p) m")).then_inc(yk_in[u], 16)
                            for u in range(2):
                                load(u, u)

                            def chunks(i, more):
                                for u in range(2):
                                    sp.wait_ge(S["uo_ready"], sc * (2 * NCH) + (i * 4 + (2 * u + 2)))
                                    sp.nop(nofuse=True)
                                    sp.dma_start(uo_rows[bass.ds(hb * 2 + f, 1), bass.ds(i * 2 + u, 1), :, :, :].rearrange("o n b p m -> (o n p) b m"),
                                                 uo[:, u, :, :]).then_inc(uo_out[u], 16)
                                    if more:
                                        sp.wait_ge(S["s_psum"], sc * (2 * NCH) + (i * 4 + (2 * u + 2)))
                                        sp.nop(nofuse=True)
                                        load(i * 2 + (u + 2), u)
                            with sp.Fori(0, NCH // 2 - 1) as i:
                                chunks(i, True)
                            chunks(NCH // 2 - 1, False)
                            for u in range(2):
                                sp.wait_ge(uo_out[u], sc * (8 * NCH) + 8 * NCH)
                                sp.wait_ge(yk_in[u], sc * (8 * NCH) + 8 * NCH)
                            sp.nop(nofuse=True)
                            for b in range(2):
                                for j in range(4):
                                    p0 = (b * 4 + j) * NCH
                                    sp.dma_start(uo_sys[p0:p0 + NCH, f, :, :].rearrange("p x c -> p (x c)"),
                                                 uo_rows[bass.ds(hb * 2 + f, 1), :, b, X * j:X * j + X, :].rearrange("o n x c -> (o n) (x c)")).then_inc(S["uo_in"], 16)

                @block.tensor
                def _(pe):
                    pe.wait_ge(S["d_weights"], 16 * 5)
                    with pe.Fori(0, HALVES) as hb:
                        for g in range(4):
                            u = g % 2
                            pe.wait_ge(S["t_ready"], hb * 16 + (4 * g + 4))
                            if g >= 2:
                                pe.wait_ge(S["t_copied"], hb * 4 + (g - 1))
                            for q in range(4):
                                for k in range(2):
                                    last = pe.transpose(bank[0:CK, 2 * u + k, q * P:(q + 1) * P], tn[:, u, q, k * CK:(k + 1) * CK], ident[:])
                            last.then_inc(S["t_turned"], 1)
                        pe.wait_ge(S["t_copied"], hb * 4 + 4)
                        for t in range(K):
                            b0 = 4 + 2 * (t % 2)
                            if t >= 2:
                                pe.wait_ge(S["proj_act"], hb * (2 * K) + 2 * (t - 1))
                                pe.wait_ge(S["beta_copied"], hb * K + (t - 1))
                            for c, (lo, hi) in enumerate(((0, 2 * C), (2 * C, 3 * C + NH))):
                                for k in range(2):
                                    last = pe.matmul(bank[:, b0 + c, 0:hi - lo], tT[:, k, t::K], w_all[:, k, lo:hi], start=k == 0, stop=k == 1)
                            last.then_inc(S["proj_psum"], 1)
                        for t in range(K):
                            pe.wait_ge(S["norms"], hb * 5 + (t // 4 + 2))
                            if t < 2:
                                pe.wait_ge(S["beta_copied"], hb * K + K)
                            else:
                                pe.wait_ge(S["kq_copied"], hb * K + (t - 1))
                            for x in range(2):
                                for k in range(2):
                                    lo = (1 - x) * C + k * CK
                                    last = pe.transpose(bank[0:CK, 6 + t % 2, (2 * x + k) * P:(2 * x + k + 1) * P], qkv[:, t, lo:lo + CK], ident[:])
                            last.then_inc(S["kq_turned"], 1)
                        for k in range(2):
                            for c in range(NC):
                                n = k * NC + c
                                for pools, ready in ((False, "kblk_dve"), (True, "kblk_pool")):
                                    if expanded_by(pools, k, c):
                                        pe.wait_ge(S[ready], hb * expanded_by(pools, 1, NC - 1) + expanded_by(pools, k, c))
                                banks, b0 = (4, 0) if k == 0 else (2, 4)
                                if c >= banks:
                                    pe.wait_ge(S["kk_copied"], hb * (2 * NC) + (n - banks + 1))
                                for g in range(2):
                                    for j in range(4):
                                        last = pe.matmul(bank[32 * j:32 * j + 32, b0 + c % banks, g * CK:(g + 1) * CK],
                                                         wqT[:, k, 8 * c + 4 * g + j, :], k_blk[:, n % 4, 4 * g + j, :], start=True, stop=True,
                                                         tile_position=(0, 32 * j))
                                last.then_inc(S["kk_psum"], 1)
                        for f in range(2):
                            sc = hb * 2 + f
                            for t in range(K):
                                pe.wait_ge(S["z_ready"], sc * K + (t + 1))
                                if t >= 2 and f == 0:
                                    pe.wait_ge(S["w_copied"], hb * (K + K // 2) + (t - 1))
                                elif t >= 2 and t % 2 == 0:
                                    pe.wait_ge(S["w_copied"], hb * (K + K // 2) + (K + t // 2))
                                elif t >= 2:
                                    pe.wait_ge(S["w_copied_dve"], hb * (K // 2) + t // 2)
                                pe.transpose(bank[0:CK, 6 + t % 2, 0:P], zv[:, t, f * HC:(f + 1) * HC, :, 1].rearrange("p h d -> p (h d)"),
                                             ident[:]).then_inc(S["w_turned"], 1)
                            pe.wait_ge(S["w_copied"], hb * (K + K // 2) + (K + f * (K // 2)))
                            pe.wait_ge(S["s_zero"], hb + 1)
                            pe.nop(nofuse=True)
                            with pe.Fori(0, NCH // 2) as i:
                                for u in range(2):
                                    pe.wait_ge(S["wq_ready"], sc * NCH + (i * 2 + (u + 1)))
                                    for s in range(2):
                                        pe.wait_ge(S["s_ready"], sc * (2 * NCH + 2) + (i * 4 + (2 * u + s + 1)))
                                        for j in (2 * s, 2 * s + 1):
                                            for b in range(2):
                                                last = pe.matmul(bank[32 * j:32 * j + 32, 4 + s, b * CK:(b + 1) * CK], wq_n[:, u, 4 * b + j, :],
                                                                 s_blk[:, j, 2 * b + f, :], start=True, stop=True, tile_position=(0, 32 * j))
                                        last.then_inc(S["ws_psum"], 1)
                                    pe.wait_ge(yk_in[u], sc * (8 * NCH) + (i * 16 + 16))
                                    for s in range(2):
                                        pe.wait_ge(S["uo_ready"], sc * (2 * NCH) + (i * 4 + (2 * u + s + 1)))
                                        for j in (2 * s, 2 * s + 1):
                                            for b in range(2):
                                                m = (2 * b + f) * CK
                                                last = pe.matmul(bank[0:CK, j, m:m + CK], yk[32 * j:32 * j + K, u, b, CK:2 * CK],
                                                                 uo[32 * j:32 * j + K, u, b, :], start=False, stop=True,
                                                                 skip_group_check=True)
                                        last.then_inc(S["s_psum"], 1)
                        for t in range(K):
                            pe.wait_ge(S["o_ready"], hb * K + (K // 2 + t // 2 + 1))
                            if t >= 2:
                                pe.wait_ge(S["o_copied_d"], hb * K + (t - 1))
                            for k in range(2):
                                last = pe.transpose(bank[0:CK, 6 + t % 2, k * P:(k + 1) * P], o_sys[:, t, k * CK:(k + 1) * CK], ident[:])
                            last.then_inc(S["o_turned_d"], 1)
                        pe.wait_ge(S["o_copied_d"], hb * K + K)
                        for j in range(HT):
                            if j >= 2:
                                pe.wait_ge(S["y_added"], hb * HT + (j - 1))
                            for k in range(2):
                                last = pe.matmul(bank[:, 4 + j % 2, 0:C], oT[:, k, j * P:(j + 1) * P], w_o[:, k, :], start=k == 0, stop=k == 1)
                            last.then_inc(S["y_psum_d"], 1)

                @block.scalar
                def _(act):
                    with act.Fori(0, HALVES) as hb:
                        for g in range(4):
                            act.wait_ge(S["t_turned"], hb * 4 + (g + 1))
                            act.activation(tT[:, :, g * 4 * P:(g + 1) * 4 * P], bank[0:CK, 2 * (g % 2):2 * (g % 2) + 2, :], ACT.Copy).then_inc(S["t_copied"], 1)
                        for t in range(K):
                            act.wait_ge(S["proj_psum"], hb * K + (t + 1))
                            b0 = 4 + 2 * (t % 2)
                            act.activation(qkv[:, t, 0:2 * C], bank[:, b0, 0:2 * C], ACT.Silu).then_inc(S["proj_act"], 1)
                            act.activation(qkv[:, t, 2 * C:3 * C], bank[:, b0 + 1, 0:C], ACT.Silu).then_inc(S["proj_act"], 1)
                            act.activation(beta[:, t, :], bank[:, b0 + 1, C:C + NH], ACT.Copy).then_inc(S["beta_copied"], 1)
                        act.wait_ge(S["beta_copied"], hb * K + K)
                        act.activation(beta[:], beta[:], ACT.Sigmoid).then_inc(S["gates"], 1)
                        act.wait_ge(S["squares"], hb + 1)
                        deviations_act(act, 1e-6, HT, NT, times=HALVES)
                        act.activation(ss[:], ss[:], ACT.Sqrt, bias=eps[1e-6][:, 0:1]).then_inc(S["norms"], 1)
                        for t in range(K):
                            act.wait_ge(S["kq_turned"], hb * K + (t + 1))
                            act.activation(wqT[:].rearrange("c k p (x t) -> c x k p t", x=2)[:, :, :, :, t],
                                           bank[0:CK, 6 + t % 2, :].rearrange("c (x k p) -> c x k p", x=2, k=2), ACT.Copy).then_inc(S["kq_copied"], 1)
                        for k in range(2):
                            for c in range(NC):
                                n = k * NC + c
                                u = (c // 2) % 2
                                act.wait_ge(S["kk_psum"], hb * (2 * NC) + (n + 1))
                                if n >= 4 and c % 2 == 0:
                                    act.wait_ge(kk_out[u], hb * (8 * NC) + 16 * (n // 4))
                                b0 = c % 4 if k == 0 else 4 + c % 2
                                act.activation(kq_out[:, u, 2 * (c % 2):2 * (c % 2) + 2, :],
                                               bank[:, b0, 0:C].rearrange("p (g c) -> p g c", g=2), ACT.Copy).then_inc(S["kk_copied"], 1)
                        for f in range(2):
                            sc = hb * 2 + f
                            for t in range(K):
                                if t == (0 if f else K - 1):
                                    act.wait_ge(S["z_ready"], sc * K + K)
                                    act.activation(y_rows[:, :, f * CK:(f + 1) * CK], zv[:, :, f * HC:(f + 1) * HC, :, 0].rearrange("p t h d -> p t (h d)"),
                                                   ACT.Copy).then_inc(S["y_copied"], 1)
                                if f and t % 2:
                                    continue
                                act.wait_ge(S["w_turned"], sc * K + (t + 1))
                                act.activation(wqT[:, f, :, t], bank[0:CK, 6 + t % 2, 0:P], ACT.Copy).then_inc(S["w_copied"], 1)
                            act.wait_ge(S["w_copied"], hb * (K + K // 2) + (K + f * (K // 2)))
                            if f:
                                act.wait_ge(S["w_copied_dve"], hb * (K // 2) + K // 2)
                            with act.Fori(0, NCH // 2) as i:
                                for u in range(2):
                                    act.wait_ge(S["wq_free"], sc * (NCH + 2) + (i * 2 + (u + 1)))
                                    act.activation(wq_n[:, u, :, :], wqT[:, f, :, :].rearrange("c (b n) x -> c b n x", n=NCH)[:, :, bass.ds(i * 2 + u, 1), :].rearrange("c b o x -> c b (o x)"),
                                                   ACT.Copy).then_inc(S["wq_ready"], 1)
                        for t in range(K):
                            act.wait_ge(S["o_turned_d"], hb * K + (t + 1))
                            act.activation(oT[:, :, t::K], bank[0:CK, 6 + t % 2, 0:2 * P].rearrange("c (k p) -> c k p", k=2), ACT.Copy).then_inc(S["o_copied_d"], 1)
                    deviations_act(act, 1e-5, 0, NT)

                @block.vector
                def _(v):
                    order = dve_order(v)
                    v.nop().then_inc(S["half_open"], 1)
                    gathers[0].first_slots(v, HT // 4)
                    for hb in range(HALVES):
                        def step(ins):
                            order.mark(ins)
                            order.wait()
                        v.wait_ge(S["half_open"], hb + 1)
                        for g in range(4):
                            u = g % 2
                            if g >= 2:
                                v.wait_ge(S["t_turned"], hb * 4 + (g - 1))
                                v.wait_ge(S["t_added"], hb * 4 + (g - 1))
                            for q in range(4):
                                tile = hb * HT + (4 * g + q)
                                v.tensor_scalar(tn[:, u, q, :], one(res, tile), mu_var[:, bass.ds(tile, 1), 0], rstd[:, bass.ds(tile, 1)],
                                                ALU.subtract, ALU.mult).then_inc(S["t_ready"], 1)
                            v.wait_ge(S["t_ready"], hb * 16 + (4 * g + 4))
                            four = res[:, bass.ds(hb * HT + 4 * g, 4), :]
                            v.tensor_tensor(four, four, tn[:, u, :, :], ALU.add).then_inc(S["t_added"], 1)
                        v.wait_ge(S["t_added"], hb * 4 + 4)
                        v.wait_ge(S["t_turned"], hb * 4 + 4)
                        def square(g):
                            sq = tmp[:, 0:4 * C].rearrange("p (t c) -> p t c", t=2)
                            v.wait_ge(S["proj_act"], hb * (2 * K) + 4 * (g + 1))
                            step(v.tensor_tensor(sq, qkv[:, 2 * g:2 * g + 2, 0:2 * C], qkv[:, 2 * g:2 * g + 2, 0:2 * C], ALU.mult))
                            step(v.tensor_reduce(ss[:, 2 * g:2 * g + 2, :], sq.rearrange("p t (h d) -> p t h d", d=D), AX_X, ALU.add))

                        for g in range(8):
                            if hb == 0 and g % 2 == 0:
                                i = HT // 4 + g // 2
                                order.wait()
                                gathers[0].add(v, order, i, i == NT // 4 - 1, True)
                            square(g)
                        if hb == 0:
                            stats_done(v, order)
                        v.nop().then_inc(S["squares"], 1)
                        if hb == 0:
                            invert_deviations(v, HT, NT, times=HALVES)
                        v.wait_ge(S["norms"], hb * 5 + 1)
                        step(v.reciprocal(ss[:], ss[:]))
                        for g in range(4):
                            four = heads(qkv[:, 4 * g:4 * g + 4, 0:2 * C])
                            v.tensor_tensor(four, four, spread(ss[:, 4 * g:4 * g + 4, :], 3, D), ALU.mult).then_inc(S["norms"], 1)
                        v.wait_ge(S["gates"], hb + 1)
                        v.wait_ge(S["norms"], hb * 5 + 5)
                        order.mark(v.tensor_tensor(zv[:, :, :, :, 0], heads(qkv[:, :, 2 * C:3 * C]), spread(beta[:], 3, D), ALU.mult))
                        order.mark(v.tensor_tensor(zv[:, :, :, :, 1], heads(qkv[:, :, C:2 * C]), spread(beta[:], 3, D), ALU.mult))
                        v.wait_ge(S["kq_copied"], hb * K + K)
                        v.wait_ge(S["d_blocks"], 1)
                        for c in range(NC):
                            if not by_pool(0, c):
                                expand_keys(v, hb, 0, c, S["kblk_dve"])
                        v.wait_ge(S["kk_copied"], hb * (2 * NC) + NC)
                        order.mark(v.memset(bank[0:CK, 0:4, 0:4 * CK], 0.0))
                        v.wait_ge(kp_in[0], hb * 32 + 16)
                        step(v.tensor_tensor(kp[:, 0, 0:K, :, :], kp[:, 0, 0:K, :, :], spread(beta[:, :, 0:HC], 3, K), ALU.mult))

                        def solve_products(f, i):
                            order.wait()
                            v.nop().then_inc(S["z_ready"], 1)
                            order.mark(solve_product(v, f, i, 0, SOLVE_HEADS if f or i >= SHARED else HC))

                        def solve_reduce(i, lo, hi):
                            order.mark(v.tensor_reduce(red[:, lo * X:hi * X].rearrange("p (h x) -> p h x", x=X),
                                                       tmp[:, lo * X * i:hi * X * i].rearrange("p (h x j) -> p h x j", h=hi - lo, x=X), AX_X, ALU.add))

                        def solve_subtract(f, i):
                            order.wait()
                            order.mark(v.tensor_tensor(z[:, i, f * C:(f + 1) * C], z[:, i, f * C:(f + 1) * C], red[:], ALU.subtract))

                        def solve_sums(f, i):
                            order.wait()
                            solve_reduce(i, 0, HC)
                            solve_subtract(f, i)

                        def solve_own_sums(i):
                            order.wait()
                            solve_reduce(i, 0, SOLVE_HEADS)

                        def solve_pools_sums(f, i):
                            v.wait_ge(S["pool_products"], hb * POOL_PRODUCTS + (K - SHARED + i if f else i - SHARED + 1))
                            solve_reduce(i, SOLVE_HEADS, HC)
                            solve_subtract(f, i)

                        def out_products(f, m):
                            order.wait()
                            for i in range(2):
                                order.mark(out_product(v, f, m, i, 0, OUT_HEADS))

                        def out_sums(f, m):
                            pair = o_sys[:, 2 * m:2 * m + 2, f * CK:(f + 1) * CK]
                            order.wait()
                            v.wait_ge(S["pool_products"], hb * POOL_PRODUCTS + (K - SHARED + K - 1 + f * (K // 2) + m + 1))
                            order.mark(v.tensor_reduce(pair, tmp[:, 0:2 * CK * (2 * m + 2)].rearrange("p (i m j) -> p i m j", i=2, m=CK), AX_X, ALU.add))

                        def out_subtract(f, m):
                            pair = o_sys[:, 2 * m:2 * m + 2, f * CK:(f + 1) * CK]
                            order.wait()
                            v.tensor_tensor(pair, pair, uo_sys[:, f, K + 2 * m:K + 2 * m + 2, :], ALU.subtract).then_inc(S["o_ready"], 1)

                        def solved(f):
                            order.wait()
                            v.nop().then_inc(S["z_ready"], 1)

                        def scan(f, beside_update, between_states, beside_products):
                            sc = hb * 2 + f
                            for s in range(2):
                                v.nop().then_inc(S["s_ready"], 1)
                                v.nop().then_inc(S["wq_free"], 1)
                            for n in range(NCH):
                                u = n % 2
                                if n >= 2:
                                    v.wait_ge(uo_out[u], sc * (8 * NCH) + 16 * (n // 2))
                                v.wait_ge(yk_in[u], sc * (8 * NCH) + (16 * (n // 2) + 16))
                                for s in range(2):
                                    at = slice(64 * s, 64 * s + 64)
                                    v.wait_ge(S["ws_psum"], sc * (2 * NCH) + (2 * n + s + 1))
                                    v.tensor_tensor(uo[at, u, :, :], yk[at, u, :, 0:CK],
                                                    bank[at, 4 + s, 0:C].rearrange("x (b c) -> x b c", b=2), ALU.subtract).then_inc(S["uo_ready"], 1)
                                v.nop().then_inc(S["wq_free"], 1)
                                beside_update(n)
                                for s in range(2):
                                    v.wait_ge(S["s_psum"], sc * (2 * NCH) + (2 * n + s + 1))
                                    v.tensor_tensor(s_blk[:, 2 * s:2 * s + 2, f::2, :],
                                                    bank[0:CK, 2 * s:2 * s + 2, 0:4 * CK].rearrange("c j (g m) -> c j g m", g=4)[:, :, f::2, :],
                                                    spread(spread(blocks[:].rearrange("c h d -> c (h d)"), 1, 2), 1, 2), ALU.mult).then_inc(S["s_ready"], 1)
                                    if s == 0:
                                        between_states(n)
                                beside_products(n)

                        for i in range(1, K):
                            solve_products(0, i)
                            if i < SHARED:
                                solve_sums(0, i)
                            else:
                                solve_own_sums(i)
                                solve_pools_sums(0, i)
                        solved(0)
                        v.wait_ge(S["masked"], hb * 3 + 1)
                        scan(0, lambda n: solve_products(1, n) if n else None,
                             lambda n: solve_own_sums(n) if n else None,
                             lambda n: solve_pools_sums(1, n) if n else None)
                        solved(1)
                        for t in range(1, K, 2):
                            v.wait_ge(S["w_turned"], (hb * 2 + 1) * K + (t + 1))
                            v.tensor_copy(wqT[:, 1, :, t], bank[0:CK, 7, 0:P]).then_inc(S["w_copied_dve"], 1)
                        v.wait_ge(S["uo_in"], (hb * 2 + 1) * 128)
                        v.wait_ge(S["masked"], hb * 3 + 3)
                        LATE = 2 * 6
                        scan(1, lambda n: out_products(0, n // 2) if n % 2 == 0 and n < LATE else None,
                             lambda n: out_sums(0, n // 2) if n % 2 and n < LATE else None,
                             lambda n: out_subtract(0, n // 2) if n % 2 and n < LATE else None)
                        for m in range(LATE // 2, K // 2):
                            out_products(0, m)
                            out_sums(0, m)
                            out_subtract(0, m)
                        v.wait_ge(S["uo_in"], (hb * 2 + 2) * 128)
                        for m in range(K // 2):
                            out_products(1, m)
                            out_sums(1, m)
                            out_subtract(1, m)
                        for g in range(HT // GS):
                            for q in range(GS):
                                j = g * GS + q
                                v.wait_ge(S["y_psum_d"], hb * HT + (j + 1))
                                tile = hb * HT + j
                                v.tensor_tensor(one(res, tile), one(res, tile), bank[:, 4 + j % 2, 0:C], ALU.add).then_inc(S["y_added"], 1)
                            v.wait_ge(S["y_added"], hb * HT + (g + 1) * GS)
                            order.wait()
                            group_stats(v, order, hb * (HT // GS) + g)
                        order.wait()
                        v.nop().then_inc(S["half_open"], 1)
                    deviations_dve(v, order, 0, NT)
                    dve_leaves(order)

        def load_experts(eng, n, w1, w2, b2, done):
            _, up, b_up, down, b_down = moe_args[n]
            for k in range(2):
                eng.dma_start(w1[0:CK, k, :, :], up[:, k * CK:(k + 1) * CK, :].rearrange("e c f -> c e f")).then_inc(done, 16)
            eng.dma_start(w1[CK:CK + 1, 0, :, :], b_up.rearrange("(o e) f -> o e f", o=1)).then_inc(done, 16)
            for k in range(FK):
                eng.dma_start(w2[:, k, :, :], down[:, k * P:(k + 1) * P, :].rearrange("e p d -> p e d")).then_inc(done, 16)
            eng.dma_start(b2[:].rearrange("p e c -> p (e c)"), b_down.rearrange("e d -> (e d)").partition_broadcast(P)).then_inc(done, 16)

        LOADS = 16 * (2 + 1 + FK + 1)

        with ExitStack() as m0:
            w1 = sb("w1_0", [CK + 1, 2, E, FF], ctx=m0)
            w2 = sb("w2_0", [P, FK, E, C], ctx=m0)
            b2 = sb("b2_0", [P, E, C], ctx=m0)
            w_in = sem("w_in0")
            with ExitStack() as a:
                xc = sb("xc", [CK, 2, T], ctx=a)
                xn = sb("xn", [CK, 2, T], ctx=a)
                BLK = 512
                NB = T // BLK
                GRP = 4
                sq = sb("sq", [CK, 2, 2, BLK], ctx=a)
                sd = sb("sd", [CK, 2, BLK], ctx=a)
                w_raw = sb("w_raw", [CK, 2, 2, C], ctx=a)
                w_T = sb("w_T", [CK, 2, 2, C], ctx=a)
                bias = sb("bias", [CK, 2, NG], ctx=a)
                (bias_in, mean_psum, centred, sq_ready, var_psum, sd_ready, rs_ready, normed, wT_psum, wT_ready,
                 conv_psum, conv_done) = [sem(s) for s in (
                    "bias_in", "mean_psum", "centred", "sq_ready", "var_psum", "sd_ready", "rs_ready", "normed",
                    "wT_psum", "wT_ready", "conv_psum", "conv_done")]
                x_in = [sem(f"images_in{g}") for g in range(NB // 2)]

                def images_there(eng, i, q):
                    if not later(i):
                        if q % 2 == 0:
                            eng.wait_ge(x_in[q // 2], 32)
                    elif q == 0:
                        for g in range(GRP // 2, NB // 2):
                            eng.wait_ge(x_in[g], 32)
                w_raw_in = [sem(f"w_raw_in{u}") for u in range(2)]
                with ExitStack() as s1:
                    ps_mean = ps("ps_mean", [CK, GRP, BLK], ctx=s1)
                    ps_var = ps("ps_var", [CK, GRP, BLK], ctx=s1)
                    with nc.Block() as block:
                        @block.sync
                        def _(sp):
                            n_img = 2 * BLK // L
                            for g in range(NB // 2):
                                b = g * n_img
                                for k in range(2):
                                    sp.dma_start(xc[:, k, b * L:(b + n_img) * L].rearrange("c (b l) -> c b l", b=n_img),
                                                 x[b:b + n_img, k * CK:(k + 1) * CK, :, :].rearrange("b c h w -> c b (h w)")).then_inc(x_in[g], 16)
                            with nc.allow_non_contiguous_dma("a small bias"):
                                for k in range(2):
                                    sp.dma_start(bias[:, k, :], conv_b[:, k * CK:(k + 1) * CK].rearrange("g c -> c g")).then_inc(bias_in, 16)
                            for g in range(NB // 2):
                                sp.wait_ge(x_in[g], 32)
                            load_experts(sp, 0, w1, w2, b2, w_in)

                        @block.scalar
                        def _(act):
                            def body(i):
                                for q in range(GRP):
                                    act.wait_ge(centred, i * GRP + (q + 1))
                                    if later(i) or q >= 2:
                                        act.wait_ge(var_psum, i * GRP + (q - 1))
                                    act.activation(sq[:, q % 2, :, :], xn[:, :, bass.ds((i * GRP + q) * BLK, BLK)], ACT.Square).then_inc(sq_ready, 1)
                                    act.wait_ge(var_psum, i * GRP + (q + 1))
                                    if later(i) or q >= 2:
                                        act.wait_ge(normed, i * GRP + (q - 1))
                                    act.activation(sd[:, q % 2, :], ps_var[:, q, :], ACT.Sqrt, bias=eps[1e-6][0:CK, 0:1]).then_inc(sd_ready, 1)
                            repeat(act, NB // GRP, body)

                        @block.gpsimd
                        def _(pool):
                            def body(i):
                                for q in range(GRP):
                                    at = bass.ds((i * GRP + q) * BLK, BLK)
                                    pool.wait_ge(rs_ready, i * GRP + (q + 1))
                                    pool.tensor_tensor(xn[:, :, at], xn[:, :, at], spread(sd[:, q % 2, :], 1, 2), ALU.mult).then_inc(normed, 1)
                            repeat(pool, NB // GRP, body)

                        @block.tensor
                        def _(pe):
                            def body(i):
                                for q in range(GRP):
                                    images_there(pe, i, q)
                                    if later(i):
                                        pe.wait_ge(centred, i * GRP + (q - 3))
                                    for k in range(2):
                                        last = pe.matmul(ps_mean[:, q, :], mean_w[:], xc[:, k, bass.ds((i * GRP + q) * BLK, BLK)],
                                                         start=k == 0, stop=k == 1)
                                    last.then_inc(mean_psum, 1)
                                for q in range(GRP):
                                    pe.wait_ge(sq_ready, i * GRP + (q + 1))
                                    for k in range(2):
                                        last = pe.matmul(ps_var[:, q, :], mean_w[:], sq[:, q % 2, k, :], start=k == 0, stop=k == 1)
                                    last.then_inc(var_psum, 1)
                            repeat(pe, NB // GRP, body)

                        @block.vector
                        def _(v):
                            def body(i):
                                for q in range(GRP):
                                    at = bass.ds((i * GRP + q) * BLK, BLK)
                                    images_there(v, i, q)
                                    v.wait_ge(mean_psum, i * GRP + (q + 1))
                                    v.tensor_tensor(xn[:, :, at], xc[:, :, at], spread(ps_mean[:, q, :], 1, 2), ALU.subtract).then_inc(centred, 1)
                                for q in range(GRP):
                                    at = bass.ds((i * GRP + q) * BLK, BLK)
                                    v.wait_ge(sd_ready, i * GRP + (q + 1))
                                    v.reciprocal(sd[:, q % 2, :], sd[:, q % 2, :]).then_inc(rs_ready, 1)
                            repeat(v, NB // GRP, body)

                with ExitStack() as s2:
                    ps_w = ps("ps_w", [CK, 2, 512], ctx=s2)
                    ps_c = ps("ps_c", [CK, 2, 512], ctx=s2)
                    def places(t, k, gh, gw):
                        v = t[:, k, :].rearrange("c (r i w j) -> c r i w j", i=GS, w=W // GS, j=GS)
                        return v[:, :, bass.ds(gh, 1), :, gw].rearrange("c r o w -> c (r o) w")
                    with nc.Block() as block:
                        @block.sync
                        def _(sp):
                            def body(i):
                                for j in range(GS):
                                    u = j % 2
                                    if later(i) or j >= 2:
                                        sp.wait_ge(wT_psum, i * GS + (j - 1))
                                    sp.dma_start(w_raw[:, u, :, :], conv_w[bass.ds(i * GS + j, 1), :, :].rearrange("o (k p) c -> p (o k) c", k=2)).then_inc(w_raw_in[u], 16)
                            repeat(sp, GS, body)

                        @block.tensor
                        def _(pe):
                            def turn(i, j):
                                u = j % 2
                                pe.wait_ge(w_raw_in[u], i * 32 + (16 * (j // 2) + 16))
                                if later(i) or i or j >= 2:
                                    pe.wait_ge(wT_ready, i * GS + (j - 1))
                                for k in range(2):
                                    for o in range(2):
                                        last = pe.transpose(ps_w[:, u, k * C + o * CK:k * C + (o + 1) * CK],
                                                            w_raw[:, u, o, k * CK:(k + 1) * CK], ident[0:CK, 0:CK])
                                last.then_inc(wT_psum, 1)

                            def body(i, first, last_trip):
                                for j in range(GS):
                                    u = j % 2
                                    if j < GS - 1:
                                        turn(i, j + 1)
                                    elif not last_trip:
                                        turn(i + 1, 0)
                                    pe.wait_ge(wT_ready, i * GS + (j + 1))
                                    if not first or j >= 2:
                                        pe.wait_ge(conv_done, i * (2 * GS) + 2 * (j - 1))
                                    for o in range(2):
                                        for k in range(2):
                                            last = pe.matmul(ps_c[:, u, o * B * 16:(o + 1) * B * 16], w_T[:, u, k, o * CK:(o + 1) * CK],
                                                             places(xn, k, i, j), start=k == 0, stop=k == 1)
                                    last.then_inc(conv_psum, 1)
                            turn(0, 0)
                            repeat_to_last(pe, GS, body)

                        @block.scalar
                        def _(act):
                            def body(i):
                                for j in range(GS):
                                    act.wait_ge(wT_psum, i * GS + (j + 1))
                                    if later(i) or j >= 2:
                                        act.wait_ge(conv_psum, i * GS + (j - 1))
                                    act.activation(w_T[:, j % 2, :, :], ps_w[:, j % 2, 0:2 * C].rearrange("c (k o) -> c k o", k=2), ACT.Copy).then_inc(wT_ready, 1)
                            repeat(act, GS, body)

                        @block.vector
                        def _(v):
                            v.wait_ge(bias_in, 32)

                            def body(i):
                                for j in range(GS):
                                    v.wait_ge(conv_psum, i * GS + (j + 1))
                                    for o in range(2):
                                        v.scalar_tensor_tensor(
                                            places(xc, o, i, j), ps_c[:, j % 2, o * B * 16:(o + 1) * B * 16].rearrange("c (r w) -> c r w", w=W // GS),
                                            bias[:, o, bass.ds(i * GS + j, 1)], places(xc, o, i, j), ALU.add, ALU.add).then_inc(conv_done, 1)
                            repeat(v, GS, body)

                with ExitStack() as s3:
                    ps_t = ps("ps_t", [P, 4, 512], ctx=s3)
                    turned, copied = sem("turned"), sem("copied")
                    with nc.Block() as block:
                        @block.tensor
                        def _(pe):
                            for t in range(NT):
                                if t >= GS:
                                    pe.wait_ge(copied, t - 3)
                                for k in range(2):
                                    last = pe.transpose(ps_t[:, t % 4, k * CK:(k + 1) * CK], xc[:, k, t * P:(t + 1) * P], ident[0:CK, 0:CK])
                                last.then_inc(turned, 1)

                        @block.vector
                        def _(v):
                            order = dve_order(v)

                            def body(i):
                                order.trip(i, STATS_MARKS)
                                v.wait_ge(copied, i * GS + GS)
                                if later(i):
                                    order.wait()
                                group_stats(v, order, i)
                            repeat(v, NT // GS, body)
                            order.leave(NT // GS)
                            deviations_dve(v, order, 0, NT)
                            dve_leaves(order)

                        @block.scalar
                        def _(act):
                            def body(i):
                                for u in range(GS):
                                    act.wait_ge(turned, i * GS + (u + 1))
                                    act.activation(one(res, i * GS + u), ps_t[:, u, 0:C], ACT.Copy).then_inc(copied, 1)
                            repeat(act, NT // GS, body)
                            deviations_act(act, 1e-5, 0, NT)

            moe(0, ACT.Gelu, w1, w2, b2, w_in, LOADS, m0, None, 1e-6)

        with ExitStack() as d:
            delta(d)
        with ExitStack() as m1:
            w1 = sb("w1_1", [CK + 1, 2, E, FF], ctx=m1)
            w2 = sb("w2_1", [P, FK, E, C], ctx=m1)
            b2 = sb("b2_1", [P, E, C], ctx=m1)
            w_in = sem("w_in1")
            moe(1, ACT.Relu, w1, w2, b2, w_in, LOADS, m1, lambda eng: load_experts(eng, 1, w1, w2, b2, w_in), None)


_INS = ['x', 'L0_conv_Wg', 'L0_conv_bg', 'L0_ffn_gate_w', 'L0_ffn_w_up', 'L0_ffn_b_up', 'L0_ffn_w_down', 'L0_ffn_b_down',
        'L1_conv_Wq', 'L1_conv_Wk', 'L1_conv_Wv', 'L1_conv_Wb', 'L1_conv_Wo', 'L1_ffn_Wg', 'L1_ffn_W1', 'L1_ffn_b1',
        'L1_ffn_W2', 'L1_ffn_b2']
_OUTS = [((16, 192, 16, 16), 'float32')]


def kernel(**inputs):
    import numpy as _np
    import concourse.bacc as _bacc
    from concourse import mybir as _mybir
    from concourse.bass_utils import run_bass_kernel_spmd as _run

    nc = _bacc.Bacc("TRN2", target_bir_lowering=False, num_devices=1)
    arrays, aps = {}, {}
    for name in _INS:
        a = _np.ascontiguousarray(inputs[name])
        arrays[f"in_{name}_dram"] = a
        aps[name] = nc.dram_tensor(f"in_{name}_dram", a.shape, _mybir.dt.from_np(a.dtype), kind="ExternalInput").ap()
    (shape, dtype), = _OUTS
    out = nc.dram_tensor("out_0_dram", shape, _mybir.dt.from_np(_np.dtype(dtype)), kind="ExternalOutput").ap()
    metaformer(nc, aps['x'], aps['L0_conv_Wg'], aps['L0_conv_bg'],
               [[aps[n] for n in _INS[3:8]], [aps[n] for n in _INS[13:18]]],
               [aps[n] for n in _INS[8:13]], out)
    r = _run(nc, [arrays], core_ids=[0])
    return r.results[0]["out_0_dram"]
```
